# Optimizing a Trainium2 kernel written in Bass

```python
import numpy as np
import jax
import jax.numpy as jnp

def _softmax(x, axis=-1):
    return jax.nn.softmax(x, axis=axis)

def _gelu(x):
    return jax.nn.gelu(x, approximate=True)

def _silu(x):
    return jax.nn.silu(x)

def _sigmoid(x):
    return jax.nn.sigmoid(x)

def _layernorm(x, axis=-1, eps=1e-05):
    m = jnp.mean(x, axis=axis, keepdims=True)
    v = jnp.var(x, axis=axis, keepdims=True)
    return (x - m) / jnp.sqrt(v + eps)

def _scatter_add(tgt, idx, src, axis=0):
    return tgt.at[idx].add(src)

def _segment_sum(src, seg, n):
    return jax.ops.segment_sum(src, seg, n)
kernel_name = 'mk_adaln_d1_jaxref_r4_683526'

def setup_inputs(seed: int=0):
    np.random.seed(seed)
    _w = jnp.asarray

    def _L0_attn_setup():
        import jax, jax.numpy as jnp
        import numpy as np
        import math
        B, T, E = (1, 512, 256)
        H = 16
        D = E // H
        L = 64
        key = jax.random.key(seed)
        ks = jax.random.split(key, 7)
        s = lambda fan: 1.0 / math.sqrt(fan)
        return {'hidden_states': jax.random.normal(ks[0], (B, T, E), dtype=jnp.float32), 'Wq': jax.random.normal(ks[1], (E, E), dtype=jnp.float32) * s(E), 'Wk_down': jax.random.normal(ks[2], (L, E), dtype=jnp.float32) * s(E), 'Wv_down': jax.random.normal(ks[3], (L, E), dtype=jnp.float32) * s(E), 'q_to_latent': jax.random.normal(ks[4], (H, D, L), dtype=jnp.float32) * s(D), 'v_up': jax.random.normal(ks[5], (H, L, D), dtype=jnp.float32) * s(L), 'Wout': jax.random.normal(ks[6], (E, E), dtype=jnp.float32) * s(E)}
    _L0_attn_in = _L0_attn_setup()

    def _L0_ffn_setup():
        import jax, jax.numpy as jnp
        import numpy as np
        import math
        E = 16
        TOP_K = 2
        D = 256
        F = 1024
        SH = 512
        key = jax.random.key(seed)
        ks = jax.random.split(key, 10)
        s = lambda k, shape, fan: jax.random.normal(k, shape, jnp.float32) / np.sqrt(fan)
        return {'x': jax.random.normal(ks[0], (32, 64, D), jnp.float32), 'gate_w': s(ks[1], (E, D), D), 'up_w': s(ks[2], (E, F, D), D), 'up_b': s(ks[3], (E, F), D), 'gw': s(ks[4], (E, F, D), D), 'gb': s(ks[5], (E, F), D), 'down_w': s(ks[6], (E, D, F), F), 'down_b': s(ks[7], (E, D), F), 'sh_gate_w': s(ks[8], (SH, D), D), 'sh_up_w': s(ks[9], (SH, D), D), 'sh_down_w': s(jax.random.fold_in(key, 11), (D, SH), SH)}
    _L0_ffn_in = _L0_ffn_setup()
    _L0_c = _w((lambda *s: np.random.randn(*s).astype(np.float32) * 0.05)(8, 256))
    _L0_wmod = _w((lambda *s: np.random.randn(*s).astype(np.float32) * 0.05)(256, 6 * 256) * 256 ** (-0.5))
    _d = {'L0_attn_hidden_states': _L0_attn_in['hidden_states'], 'L0_attn_Wq': _L0_attn_in['Wq'], 'L0_attn_Wk_down': _L0_attn_in['Wk_down'], 'L0_attn_Wv_down': _L0_attn_in['Wv_down'], 'L0_attn_q_to_latent': _L0_attn_in['q_to_latent'], 'L0_attn_v_up': _L0_attn_in['v_up'], 'L0_attn_Wout': _L0_attn_in['Wout'], 'L0_ffn_gate_w': _L0_ffn_in['gate_w'], 'L0_ffn_up_w': _L0_ffn_in['up_w'], 'L0_ffn_up_b': _L0_ffn_in['up_b'], 'L0_ffn_gw': _L0_ffn_in['gw'], 'L0_ffn_gb': _L0_ffn_in['gb'], 'L0_ffn_down_w': _L0_ffn_in['down_w'], 'L0_ffn_down_b': _L0_ffn_in['down_b'], 'L0_ffn_sh_gate_w': _L0_ffn_in['sh_gate_w'], 'L0_ffn_sh_up_w': _L0_ffn_in['sh_up_w'], 'L0_ffn_sh_down_w': _L0_ffn_in['sh_down_w'], 'L0_c': _L0_c, 'L0_wmod': _L0_wmod}
    _x0 = _d['L0_attn_hidden_states']
    _d['L0_attn_hidden_states'] = jax.random.normal(jax.random.fold_in(jax.random.key(seed), 1), (8, 512, 256), dtype=_x0.dtype)
    del _x0
    return _d

def reference(L0_attn_hidden_states, L0_attn_Wq, L0_attn_Wk_down, L0_attn_Wv_down, L0_attn_q_to_latent, L0_attn_v_up, L0_attn_Wout, L0_ffn_gate_w, L0_ffn_up_w, L0_ffn_up_b, L0_ffn_gw, L0_ffn_gb, L0_ffn_down_w, L0_ffn_down_b, L0_ffn_sh_gate_w, L0_ffn_sh_up_w, L0_ffn_sh_down_w, L0_c, L0_wmod):

    def _L0_attn_ref(hidden_states, Wq, Wk_down, Wv_down, q_to_latent, v_up, Wout):
        import jax, jax.numpy as jnp
        import numpy as np
        import math
        B, T, E = (1, 512, 256)
        H = 16
        D = E // H
        L = 64
        'RA_MLA_Attention forward (default config: coupling_scale=0 so the RA\n            reciprocal-band branch is inactive; no cache, no RoPE, dropout=0).'
        b, t, e = hidden_states.shape
        h, d, l = q_to_latent.shape
        Q = (hidden_states @ Wq.T).reshape(b, t, h, d)
        latent_k = hidden_states @ Wk_down.T
        latent_v = hidden_states @ Wv_down.T
        q_lat = jnp.einsum('bthd,hdl->bthl', Q, q_to_latent)
        logits = jnp.einsum('bthl,bsl->bhts', q_lat, latent_k) / math.sqrt(l)
        causal = jnp.tril(jnp.ones((t, t), dtype=bool))
        logits = jnp.where(causal[None, None], logits, jnp.float32(-1e+30))
        attn = jax.nn.softmax(logits, axis=-1)
        ctx_lat = jnp.einsum('bhts,bsl->bhtl', attn, latent_v)
        heads = jnp.einsum('bhtl,hld->bthd', ctx_lat, v_up)
        out = heads.reshape(b, t, h * d) @ Wout.T
        return out

    def _L0_ffn_ref(x, gate_w, up_w, up_b, gw, gb, down_w, down_b, sh_gate_w, sh_up_w, sh_down_w):
        import jax, jax.numpy as jnp
        import numpy as np
        import math
        E = 16
        TOP_K = 2
        D = 256
        F = 1024
        SH = 512
        B, S, Dm = x.shape
        h = x.reshape(-1, Dm)
        T = h.shape[0]
        scores = jax.nn.sigmoid(h @ gate_w.T)
        cap = math.ceil(T / E * TOP_K)
        topk_score, topk_ids = jax.lax.top_k(scores.T, cap)
        xin = h[topk_ids]
        up = jnp.einsum('ecd,efd->ecf', xin, up_w) + up_b[:, None, :]
        g = jnp.einsum('ecd,efd->ecf', xin, gw) + gb[:, None, :]
        eo = jax.nn.silu(g) * up
        eo = jnp.einsum('ecf,edf->ecd', eo, down_w) + down_b[:, None, :]
        flat = (eo * topk_score[..., None]).reshape(-1, Dm)
        out = jnp.zeros_like(h).at[topk_ids.reshape(-1)].add(flat)
        out = out.reshape(B, S, Dm)
        shared = jax.nn.silu(jnp.einsum('bsd,fd->bsf', x, sh_gate_w)) * jnp.einsum('bsd,fd->bsf', x, sh_up_w)
        shared = jnp.einsum('bsf,df->bsd', shared, sh_down_w)
        return out + shared
    x = L0_attn_hidden_states
    mod = (_silu(L0_c) @ L0_wmod).reshape(L0_c.shape[0], 6, 1, -1)
    sa, ca, ga, sb, cb, gb = (mod[:, 0], mod[:, 1], mod[:, 2], mod[:, 3], mod[:, 4], mod[:, 5])
    ga = (2 * (ga >= 0) - 1) * jnp.maximum(jnp.abs(ga), 0.25)
    gb = (2 * (gb >= 0) - 1) * jnp.maximum(jnp.abs(gb), 0.25)
    h = _layernorm(x, axis=-1) * (1 + ca) + sa
    x = x + ga * _L0_attn_ref(h, L0_attn_Wq, L0_attn_Wk_down, L0_attn_Wv_down, L0_attn_q_to_latent, L0_attn_v_up, L0_attn_Wout)
    h = _layernorm(x, axis=-1) * (1 + cb) + sb
    x = x + gb * _L0_ffn_ref(h, L0_ffn_gate_w, L0_ffn_up_w, L0_ffn_up_b, L0_ffn_gw, L0_ffn_gb, L0_ffn_down_w, L0_ffn_down_b, L0_ffn_sh_gate_w, L0_ffn_sh_up_w, L0_ffn_sh_down_w)
    return x

_drawn_inputs = setup_inputs


def setup_inputs(seed=0):
    import zlib

    import numpy as np

    out = dict(_drawn_inputs(seed))
    spreads = {}
    factors = {'L0_ffn_up_b': 5.241, 'L0_ffn_gb': 5.091, 'L0_ffn_down_b': 6.25}
    for name, (base, spread) in spreads.items():
        noise = np.random.default_rng([zlib.crc32(name.encode()), seed]).standard_normal(out[name].shape)
        drawn = base * np.exp(spread * noise) if base else spread * noise
        out[name] = jnp.asarray(drawn.astype(out[name].dtype))
    for name, factor in factors.items():
        out[name] = (out[name] * factor).astype(out[name].dtype)
    return out
```

```python
from contextlib import ExitStack

import concourse.bass as bass
from concourse import mybir

ALU = mybir.AluOpType
ACT = mybir.ActivationFunctionType
F32 = mybir.dt.float32
F32R = mybir.dt.float32r
BF16 = mybir.dt.bfloat16
I32 = mybir.dt.int32
U32 = mybir.dt.uint32

NB = 8
T = 512
D = 256
NH = 16
DH = 16
NU = 16
NE = 16
F = 1024
SH = 512
CAP = 512
EPS = 1e-5
NEG = -1e30
ROW = D + NE + D

SPAN = {0: (0, 512), 1: (512, 384), 3: (896, 128), 2: (1024, 256)}
MSPAN = {3: (0, 512), 2: (512, 384), 0: (896, 128), 1: (1024, 256)}


class Lane:

    def __init__(self, sem):
        self.sem, self.n, self.ops, self.seen = sem, 0, [], {}

    def wait(self, *marks):
        for m in marks:
            if m is None:
                continue
            sem, v = m
            if self.seen.get(sem.name, 0) < v:
                self.seen[sem.name] = v
                self.ops.append((None, sem, v))

    def do(self, f):
        self.n += 1
        self.ops.append((f, self.sem, 1))
        return (self.sem, self.n)

    def quiet(self, f):
        self.ops.append((f, None, 0))

    def dma(self, c, f):
        c.n += 16
        self.ops.append((f, c.sem, 16))
        return (c.sem, c.n)

    def last(self):
        return (self.sem, self.n)

    def emit(self, eng):
        for f, sem, v in self.ops:
            if f is None:
                eng.wait_ge(sem, v)
            elif sem is None:
                f(eng)
            else:
                f(eng).then_inc(sem, v)


class Count:

    def __init__(self, sem):
        self.sem, self.n = sem, 0


def block_program(nc, x, wq, wkd, wvd, q2l, vup, wo, gate, uw, ub, gw, gb, dw, db, sg, su, sd, ct, wmod,
                  cst, cpos, out):
    ctx = ExitStack()
    with ctx:
        def sem(name):
            return ctx.enter_context(nc.semaphore(name))

        def sb_in(stack, name, shape, dt=F32):
            return stack.enter_context(nc.sbuf_tensor(name, shape, dt))

        def dram(name, shape, dt=F32):
            return nc.dram_tensor(name, shape, dt).ap()

        PE, DVE, AC, PL, SP = (Lane(sem(n)) for n in ("s_pe", "s_dve", "s_act", "s_pool", "s_sp"))

        def count(name):
            return Count(sem(name))

        LB = ctx.enter_context(nc.psum_tensor("LB", [128, 1536], F32))
        MB = ctx.enter_context(nc.psum_tensor("MB", [128, 1536], F32))
        UB = ctx.enter_context(nc.psum_tensor("UB", [128, 512], F32))
        XB = ctx.enter_context(nc.psum_tensor("XB", [128, 512], F32))

        modD = dram("modD", [NB, 6, D])
        sdD = dram("sdD", [NU, 2, 128, 2, 512])
        udD = dram("udD", [NU, 2, 128, 512])
        hD = dram("hD", [NB, 128, 2, 2, 512])
        xD = dram("xD", [NB, 128, 4, D])
        tab = dram("tab", [NB * T, ROW])
        tabv = tab.rearrange("(b k p) r -> b p k r", k=4, p=128)
        outv = out.rearrange("b (k p) d -> b p k d", p=128)
        out2 = out.rearrange("b t d -> (b t) d")
        xv = x.rearrange("b (k p) d -> b p k d", p=128)

        C = sb_in(ctx, "C", [128, 512])
        ident, Gm, Lm, iotaf = C[:, 0:128], C[:, 128:256], C[:, 256:384], C[:, 384:512]
        LG = sb_in(ctx, "LG", [128, 512])
        ubT = sb_in(ctx, "ubT", [128, NE, 8])
        gbT = sb_in(ctx, "gbT", [128, NE, 8])

        A = ExitStack()

        def sa(name, shape, dt=F32):
            return sb_in(A, name, shape, dt)

        MK = sa("MK", [128, 512])
        W = {n: (sa(n + "h", [128, 2, 256], F32R), sa(n + "l", [128, 2, 256], F32R)) for n in ("wq", "wk", "wv", "wo")}
        GPh, GPl = sa("GPh", [128, 2, 240], F32R), sa("GPl", [128, 2, 240], F32R)
        modT = sa("modT", [128, 2, 2, NB])
        QS = sa("QS", [128, 8, 512], F32R)
        KS = sa("KS", [128, 8, 512], F32R)
        X = sa("X", [128, 4, 4, D])
        xh = sa("xh", [128, 4, D])
        st = sa("st", [128, 4, 6])
        mv = sa("mv", [128, 4, 2])
        rs = sa("rs", [128, 4])
        epsc = sa("epsc", [128, 4])
        halfc = sa("halfc", [128, 4])
        hf = sa("hf", [128, 2, 512])
        hh = sa("hh", [128, 2, 512], F32R)
        hl = sa("hl", [128, 2, 512], F32R)
        ST = [sa(f"ST{i}", [128, 2, 512], F32R) for i in range(4)]
        V = [sa(f"V{i}", [128, 4, NH, 32]) for i in range(2)]
        pro = ExitStack()
        wqr, wor = sb_in(pro, "wqr", [128, 512]), sb_in(pro, "wor", [128, 512])
        kdr = sb_in(pro, "kdr", [64, 4, 256])
        grr = sb_in(pro, "grr", [128, 96])
        modS = sb_in(pro, "modS", [NB, 6 * D])
        modA = sb_in(pro, "modA", [NB, 2, D])
        modB = sb_in(pro, "modB", [NB, 2, D])
        WM = sb_in(pro, "WM", [128, 2, 3 * 512])
        pro.close()
        NP = 6
        P = [sa(f"P{i}", [128, 1280]) for i in range(NP)]
        NM = sa("NM", [128, 2, 16])
        NMh = [sa(f"NMh{i}", [16, 128], F32R) for i in range(2)]
        NMl = [sa(f"NMl{i}", [16, 128], F32R) for i in range(2)]
        junk = sa("junk", [128, 1280], BF16)
        Us = [sa(f"Us{i}", [128, 512]) for i in range(2)]
        HT = [sa(f"HT{i}", [128, 512]) for i in range(2)]
        DN = [sa(f"DN{i}", [128, 512]) for i in range(2)]
        nf = sa("nf", [128, 512])
        HNh = sa("HNh", [128, 2, 512], F32R)
        HNl = sa("HNl", [128, 2, 512], F32R)
        BT = [sa(f"BT{i}", [128, 3, D]) for i in range(2)]
        tf = sa("tf", [128, 2, D])
        th = sa("th", [128, D])
        st2 = sa("st2", [128, 4, 6])
        mv2 = sa("mv2", [128, 4, 2])
        rs2 = sa("rs2", [128, 4])
        H2 = sa("H2", [128, 4, D])
        h2 = sa("h2", [128, 2, 2, 512], F32R)

        c_in, c_mod, c_mr = count("c_in"), count("c_mod"), count("c_mr")
        c_x = [count(f"c_x{i}") for i in range(4)]
        c_w = [count(f"c_w{i}") for i in range(4)]
        c_q = [count(f"c_q{i}") for i in range(4)]
        c_nm = [count(f"c_nm{i}") for i in range(2)]
        c_u = [count(f"c_u{i}") for i in range(2)]
        c_ur = [count(f"c_ur{i}") for i in range(2)]
        c_bt = [count(f"c_bt{i}") for i in range(2)]
        c_gt = count("c_gt")
        c_h2, c_hd, c_xd = count("c_h2"), count("c_hd"), count("c_xd")

        raw = {"wq": wqr[:], "wo": wor[:]}
        kd, vd, q2, vu = (kdr[:, i, :] for i in range(4))
        gr = grr[:, 0:32]
        cT = grr[:, 32:48]
        sT = grr[:, 64:80]

        m_c = SP.dma(c_mod, lambda e: e.dma_start(cT.rearrange("p (k b) -> p k b", k=2), ct.rearrange("(k p) b -> p k b", p=128)))
        m_wm = SP.dma(c_mod, lambda e: e.dma_start(WM[:], wmod.rearrange("(k p) n -> p k n", p=128)))
        SP.dma(c_in, lambda e: e.dma_start(C[:], cst))
        m_xl = {}

        def load_x(b, free=None):
            SP.wait(free)
            m_xl[b] = SP.dma(c_x[b % 4], lambda e: e.dma_start(X[:, b % 4, :, :], xv[b]))

        load_x(0)
        for n, src in (("wq", wq), ("wo", wo)):
            SP.dma(c_in, lambda e, n=n, src=src: e.dma_start(raw[n].rearrange("p (k n) -> p k n", k=2), src.rearrange("(k p) n -> p k n", p=128)))
        for dst, src in ((kd, wkd), (vd, wvd), (q2, q2l), (vu, vup)):
            SP.dma(c_in, lambda e, dst=dst, src=src: e.dma_start(dst, src))
        SP.dma(c_in, lambda e: e.dma_start(gr.rearrange("p (k n) -> p k n", k=2), gate.rearrange("(k p) n -> p k n", p=128)))
        SP.dma(c_in, lambda e: e.dma_start(MK[:], cpos[:, 0:512]))
        SP.dma(c_in, lambda e: e.dma_start(ubT[:].rearrange("p e m -> p (e m)"), ub))
        m_in = SP.dma(c_in, lambda e: e.dma_start(gbT[:].rearrange("p e m -> p (e m)"), gb))
        for b in range(1, 4):
            load_x(b)

        DVE.do(lambda e: e.memset(GPh[:].bitcast(F32), 0.0))
        DVE.do(lambda e: e.memset(GPl[:].bitcast(F32), 0.0))
        DVE.do(lambda e: e.memset(epsc[:], EPS))
        DVE.do(lambda e: e.memset(halfc[:], -0.5))
        DVE.do(lambda e: e.memset(LG[:], 0.0))
        for i in range(2):
            DVE.do(lambda e, i=i: e.memset(V[i][:], 1.0))
        DVE.do(lambda e: e.memset(KS[32:64, :, :].bitcast(F32), 1.0))
        m_ms = DVE.do(lambda e: e.memset(KS[96:128, :, :].bitcast(F32), 1.0))

        AC.wait(m_wm)
        m = AC.do(lambda e: e.activation(sT, cT, ACT.Exp, scale=-1.0))
        DVE.wait(m)
        m = DVE.do(lambda e: e.tensor_scalar(sT, sT, 1.0, None, ALU.add))
        DVE.wait(m)
        m = DVE.do(lambda e: e.reciprocal(sT, sT))
        DVE.wait(m)
        m_sT = DVE.do(lambda e: e.tensor_tensor(sT, sT, cT, ALU.mult))
        PE.wait(m_sT, m_wm)
        for g in range(3):
            for k in range(2):
                m = PE.do(lambda e, g=g, k=k: e.matmul(LB[0:NB, g * 512:(g + 1) * 512], sT[:, 8 * k:8 * k + 8],
                                                      WM[:, k, g * 512:(g + 1) * 512], start=(k == 0), stop=(k == 1)))
        m_modp = m
        for c4 in range(4):
            for k in range(2):
                m = PE.do(lambda e, c4=c4, k=k: e.matmul(UB[:, c4 * 8:c4 * 8 + 8], WM[:, k, c4 * 128:(c4 + 1) * 128],
                                                        sT[:, 8 * k:8 * k + 8], start=(k == 0), stop=(k == 1)))
        DVE.wait(m, m_modp)
        m = DVE.do(lambda e: e.tensor_copy(modT[:].rearrange("p a c b -> p (a c b)"), UB[:, 0:32]))
        m_modT0 = m
        DVE.wait(m)
        m_modT = DVE.do(lambda e: e.tensor_scalar(modT[:, 1, :, :], modT[:, 1, :, :], 1.0, None, ALU.add))
        m = DVE.do(lambda e: e.tensor_copy(modS[:], LB[0:NB, :]))
        DVE.wait(m)
        gates = modS[:].rearrange("p (a r d) -> p a r d", a=2, r=3)[:, :, 2, :]
        m1 = DVE.do(lambda e: e.scalar_tensor_tensor(out=modA[:], in0=gates, scalar=-1.0, in1=gates, op0=ALU.mult, op1=ALU.max))
        DVE.wait(m1)
        DVE.do(lambda e: e.tensor_scalar(modA[:], modA[:], 0.25, None, ALU.max))
        m2 = DVE.do(lambda e: e.tensor_scalar(modB[:], gates, 0.0, 2.0, ALU.is_ge, ALU.mult))
        DVE.wait(m2)
        m2 = DVE.do(lambda e: e.tensor_scalar(modB[:], modB[:], -1.0, None, ALU.add))
        DVE.wait(m2)
        DVE.do(lambda e: e.tensor_tensor(gates, modA[:], modB[:], ALU.mult))
        m = DVE.do(lambda e: e.tensor_scalar(modS[:, 4 * D:5 * D], modS[:, 4 * D:5 * D], 1.0, None, ALU.add))
        SP.wait(m)
        m_modD = SP.dma(c_mr, lambda e: e.dma_start(modD.rearrange("b r d -> b (r d)"), modS[:]))

        m_bt = {}

        def load_bt(b, free=None):
            SP.wait(free, m_modD)
            for i, r in enumerate((2, 4, 3)):
                m_bt[b] = SP.dma(c_bt[b % 2], lambda e, i=i, r=r: e.dma_start(
                    BT[b % 2][:, i, :], modD[b, r:r + 1, :].broadcast_to([128, D])))
            SP.dma(c_gt, lambda e: e.dma_start(tab[b * T:(b + 1) * T, D + NE:ROW], modD[b, 5:6, :].broadcast_to([T, D])))

        load_bt(0)
        load_bt(1)

        PE.wait(m_in)
        PE.wait(m)
        for dst, (a, r) in ((0, (kd, q2)), (1, (vd, vu))):
            for c in range(2):
                m = PE.do(lambda e, dst=dst, a=a, r=r, c=c: e.matmul(MB[:, dst * 512 + c * 256:dst * 512 + c * 256 + 256],
                                                                    a[:, c * 128:(c + 1) * 128], r, start=True, stop=True))
        DVE.wait(m, m_in, m_ms)
        srcs = {"wk": MB[:, 0:512], "wv": MB[:, 512:1024], "wq": raw["wq"], "wo": raw["wo"]}
        for n in ("wq", "wk", "wv", "wo"):
            h_, l_ = (W[n][i][:].rearrange("p k n -> p (k n)") for i in range(2))
            s_ = srcs[n]
            m = DVE.do(lambda e, h_=h_, s_=s_: e.tensor_copy(h_, s_))
            DVE.wait(m)
            m_w = DVE.do(lambda e, h_=h_, s_=s_, l_=l_: e.tensor_tensor(l_, s_, h_.bitcast(F32), ALU.subtract))
        grv = gr.rearrange("p (k n) -> p k n", k=2)
        m = DVE.do(lambda e: e.tensor_copy(GPh[:, :, 112:128], grv))
        DVE.wait(m)
        m_w = DVE.do(lambda e: e.tensor_tensor(GPl[:, :, 112:128], grv, GPh[:, :, 112:128].bitcast(F32), ALU.subtract))

        xfree = [m_w]
        ufree = [m_modT0]
        lfree = [m, m, m]
        mfree = [m_w, m_w, m_w]
        s = {}

        def terms3(ps, lh, ll, rh, rl):
            seq = [(c, a, b) for c in range(2) for a, b in ((lh, rh), (lh, rl), (ll, rh))]
            for i, (c, a, b) in enumerate(seq):
                f = (lambda e, i=i, c=c, a=a, b=b: e.matmul(ps, a(c), b(c), start=(i == 0), stop=(i == 5)))
                if i < 5:
                    PE.quiet(f)
                else:
                    m = PE.do(f)
            return m

        def norm1(b):
            xb = X[:, b % 4, :, :]
            DVE.wait(m_xl[b])
            for k in range(4):
                m = DVE.do(lambda e, k=k: e.bn_stats(st[:, k, :], xb[:, k, :]))
            DVE.wait(m, s.get("rs1"))
            for k in range(4):
                m = DVE.do(lambda e, k=k: e.bn_aggr(mv[:, k, :], st[:, k, :]))
            DVE.wait(m)
            m = DVE.do(lambda e: e.tensor_scalar(rs[:], mv[:, :, 1], EPS, None, ALU.add))
            PL.wait(m)
            m = s["rs1"] = PL.do(lambda e: e.tensor_tensor(rs[:], rs[:], halfc[:], ALU.pow))
            DVE.wait(m, s.get(("hTp", b - 1)))
            for k in range(4):
                m = DVE.do(lambda e, k=k: e.tensor_scalar(xh[:, k, :], xb[:, k, :], mv[:, k, 0:1], rs[:, k:k + 1],
                                                         ALU.subtract, ALU.mult))
            s["xh", b] = m

        def hT(b, c):
            PE.wait(s["xh", b], xfree[0])
            for k in range(4):
                m = PE.do(lambda e, k=k: e.transpose(XB[:, k * 128:(k + 1) * 128], xh[:, k, c * 128:(c + 1) * 128], ident))
            s["hTp", b] = m
            AC.wait(m, s.get(("hs", b - 1, c)), m_modT)
            m = xfree[0] = AC.do(lambda e: e.activation(hf[:, c, :], XB[:], ACT.Identity, bias=modT[:, 0, c, b:b + 1],
                                                        scale=modT[:, 1, c, b:b + 1]))
            PL.wait(m, s.get(("proj", b - 1)))
            m = PL.do(lambda e: e.tensor_copy(hh[:, c, :], hf[:, c, :]))
            PL.wait(m)
            s["hs", b, c] = PL.do(lambda e: e.tensor_tensor(hl[:, c, :], hf[:, c, :], hh[:, c, :].bitcast(F32), ALU.subtract))

        def qk(b, c, kind):
            u = 2 * b + c
            sl = 2 * (u % 2) + kind
            wh, wl = W["wk" if kind else "wq"]
            PE.wait(s["hs", b, 0], s["hs", b, 1], xfree[0])
            m = terms3(XB[:], lambda k: wh[:, k, c * 128:(c + 1) * 128], lambda k: wl[:, k, c * 128:(c + 1) * 128],
                       lambda k: hh[:, k, :], lambda k: hl[:, k, :])
            sc = 1.0 if kind else 0.125
            AC.wait(m, s.get(("stw", u - 2, kind)))
            m1 = AC.do(lambda e: e.activation(ST[sl][:, 0, :], XB[:], ACT.Copy, scale=sc))
            DVE.wait(m1, m)
            m2 = xfree[0] = DVE.do(lambda e: e.scalar_tensor_tensor(out=ST[sl][:, 1, :], in0=XB[:], scalar=sc,
                                                                   in1=ST[sl][:, 0, :].bitcast(F32), op0=ALU.mult, op1=ALU.subtract))
            SP.wait(m1, m2)
            s["stw", u, kind] = SP.dma(c_w[sl], lambda e: e.dma_start(sdD[u, kind], ST[sl][:].bitcast(F32)))
            s["proj", b] = m

        def stack(u, half):
            base = 64 * (u % 2)
            SP.wait(s["stw", u, 0], s["stw", u, 1], s.get(("main", u - 2, 4 * half + 3)), m_ms)
            hs = slice(4 * half, 4 * half + 4)
            for kind, dst in ((0, QS), (1, KS)):
                src = sdD[u, kind].rearrange("(h d) k t -> k d h t", d=DH)
                for r, part in enumerate((0, 1, 0) if kind == 0 else (0, 0, 1)):
                    m = SP.dma(c_q[2 * (u % 2) + half], lambda e, r=r, part=part, dst=dst, src=src: e.dma_start(
                        dst[base + 16 * r:base + 16 * r + 16, hs, :].bitcast(F32), src[part, :, hs, :]))
            s["stack", u, half] = m

        def vproj(b, i):
            PE.wait(s["hs", b, 0], s["hs", b, 1], xfree[0])
            wh, wl = W["wv"]
            for j in range(2):
                t0 = (2 * i + j) * 128
                m = terms3(XB[:, j * 256:(j + 1) * 256], lambda k, t0=t0: hh[:, k, t0:t0 + 128],
                           lambda k, t0=t0: hl[:, k, t0:t0 + 128], lambda k: wh[:, k, :], lambda k: wl[:, k, :])
            AC.wait(m, s.get(("pv", 2 * (b - 2) + 1, 1)), m_ms)
            for j in range(2):
                k2 = 2 * i + j
                mm = AC.do(lambda e, k2=k2, j=j: e.activation(V[b % 2][:, k2, :, 0:DH],
                                                             XB[:, j * 256:(j + 1) * 256].rearrange("p (h d) -> p h d", d=DH), ACT.Copy))
            xfree[0] = mm
            s["V", b, i] = mm
            s["proj", b] = m

        def maxima(u, k):
            base = 64 * (u % 2)
            PE.wait(s["stack", u, k // 4])
            for bank, blocks in ((0, (3,)), (1, (2, 0)), (2, (1,))):
                PE.wait(mfree[bank])
                for i in blocks:
                    o, w = MSPAN[i]
                    m = PE.do(lambda e, i=i, o=o, w=w: e.matmul(MB[:, o:o + w], QS[base:base + 48, k, i * 128:(i + 1) * 128],
                                                               KS[base:base + 48, k, 0:w], start=True, stop=True))
                DVE.wait(m, s.get(("nmT", u - 1, k // 4)))
                for i in blocks:
                    o, w = MSPAN[i]
                    DVE.wait(s.get(("junk", i)))
                    mfree[bank] = s["junk", i] = DVE.do(lambda e, i=i, o=o, w=w: e.tensor_tensor_reduce(
                        junk[:, o:o + w], MB[:, o:o + w], MK[:, 512 - w:512], 1.0, -3e38, ALU.add, ALU.max,
                        NM[:, k // 4, 4 * (k % 4) + i:4 * (k % 4) + i + 1]))
            s["nm", u, k] = mfree[2]

        def put_max(u, half):
            base = 64 * (u % 2)
            PE.wait(mfree[0], mfree[1], mfree[2], s["nm", u, 4 * half + 3], xfree[0])
            m = s["nmT", u, half] = PE.do(lambda e: e.transpose(XB[0:16, 0:128], NM[:, half, :], ident))
            AC.wait(m, s.get(("nmd", u - 1, half)))
            m1 = AC.do(lambda e: e.activation(NMh[half][:], XB[0:16, 0:128], ACT.Copy, scale=-1.0))
            DVE.wait(m1, m)
            m2 = xfree[0] = DVE.do(lambda e: e.scalar_tensor_tensor(out=NMl[half][:], in0=XB[0:16, 0:128], scalar=-1.0,
                                                                   in1=NMh[half][:].bitcast(F32), op0=ALU.mult, op1=ALU.subtract))
            SP.wait(m1, m2, s.get(("main", u - 2, 4 * half + 3)))
            for r, src in ((48, NMh), (49, NMl)):
                m = SP.dma(c_nm[half], lambda e, r=r, src=src: e.dma_start(
                    QS[base + r:base + r + 1, 4 * half:4 * half + 4, :].rearrange("p h (i t) -> p (h i) t", t=128).bitcast(F32),
                    src[half][:].bitcast(F32)))
            s["nmd", u, half] = m

        def main(u, k):
            base = 64 * (u % 2)
            n = (8 * u + k)
            slot = n % NP
            PE.wait(s["stack", u, k // 4], s["nmd", u, k // 4])
            for bank, blocks in ((0, (0,)), (1, (1, 3)), (2, (2,))):
                PE.wait(lfree[bank])
                for j in blocks:
                    o, w = SPAN[j]
                    m = PE.do(lambda e, j=j, o=o, w=w: e.matmul(LB[:, o:o + w], KS[base:base + 50, k, j * 128:(j + 1) * 128],
                                                               QS[base:base + 50, k, 128 * j:512], start=True, stop=True))
                if bank == 0:
                    m0 = m
            s["main", u, k] = m
            AC.wait(m0, s.get(("pvn", n - NP)))
            lfree[0] = m1 = AC.do(lambda e: e.activation(P[slot][:, 0:512], LB[:, 0:512], ACT.Exp))
            AC.wait(m)
            m2 = AC.do(lambda e: e.activation(P[slot][:, 512:1280], LB[:, 512:1280], ACT.Exp))
            lfree[1] = lfree[2] = m2
            PL.wait(m2)
            d1 = P[slot][:, 0:1024].rearrange("p (a t) -> p a t", a=2)[:, :, 0:128]
            d2 = P[slot][:, 896:1152].rearrange("p (a t) -> p a t", a=2)
            for dd in (d1, d2):
                m = PL.do(lambda e, dd=dd: e.affine_select(out=dd, in_=dd, compare_op=ALU.is_ge, fill=0.0, base=0,
                                                          pattern=[[0, 2], [1, 128]], channel_multiplier=-1))
            s["P", n] = m

        def pv(u, g):
            b, c = u // 2, u % 2
            PE.wait(s["V", b, 0], s["V", b, 1], ufree[0])
            for h in range(4):
                PE.wait(s["P", 8 * u + 4 * g + h])
            for j in range(4):
                o, w = SPAN[j]
                for h in range(4):
                    slot = (8 * u + 4 * g + h) % NP
                    hd = 8 * c + 4 * g + h
                    m = PE.do(lambda e, j=j, o=o, w=w, h=h, slot=slot, hd=hd: e.matmul(
                        UB[32 * h:32 * h + 32, 128 * j:512], V[b % 2][:, j, hd, :], P[slot][:, o:o + w],
                        start=(j == 0), stop=(j == 3), skip_group_check=True))
            for h in range(4):
                s["pvn", 8 * u + 4 * g + h] = m
            s["pv", u, g] = m
            AC.wait(m, s.get(("uw", u - 1, g)))
            m = ufree[0] = AC.do(lambda e: e.activation(Us[g][:], UB[:], ACT.Copy))
            SP.wait(m)
            m = s["uw", u, g] = SP.dma(c_u[g], lambda e: e.dma_start(udD[u, g], Us[g][:]))
            SP.wait(m, s.get(("norm", u - 2)))
            src = udD[u, g].rearrange("(h r) t -> h r t", r=32)
            SP.dma(c_ur[u % 2], lambda e: e.dma_start(HT[u % 2][64 * g:64 * g + 64, :], src[:, 0:16, :]))
            s["ur", u] = SP.dma(c_ur[u % 2], lambda e: e.dma_start(DN[u % 2][64 * g:64 * g + 64, :], src[:, 16:32, :]))

        def normalise(u):
            b, c = u // 2, u % 2
            DVE.wait(s["ur", u])
            m = DVE.do(lambda e: e.reciprocal(DN[u % 2][:], DN[u % 2][:]))
            DVE.wait(m, s.get(("hn", u - 1)))
            m = s["norm", u] = DVE.do(lambda e: e.tensor_tensor(nf[:], HT[u % 2][:], DN[u % 2][:], ALU.mult))
            DVE.wait(m, s.get(("out", b - 1, 1)))
            m = DVE.do(lambda e: e.tensor_copy(HNh[:, c, :], nf[:]))
            DVE.wait(m)
            s["hn", u] = DVE.do(lambda e: e.tensor_tensor(HNl[:, c, :], nf[:], HNh[:, c, :].bitcast(F32), ALU.subtract))

        def outproj(b, i):
            wh, wl = W["wo"]
            PE.wait(s["hn", 2 * b], s["hn", 2 * b + 1], xfree[0])
            for j in range(2):
                t0 = (2 * i + j) * 128
                m = terms3(XB[:, j * 256:(j + 1) * 256], lambda k, t0=t0: HNh[:, k, t0:t0 + 128],
                           lambda k, t0=t0: HNl[:, k, t0:t0 + 128], lambda k: wh[:, k, :], lambda k: wl[:, k, :])
            s["out", b, i] = m
            DVE.wait(m, m_bt[b], s.get("x2p"))
            m = xfree[0] = DVE.do(lambda e: e.tensor_tensor(tf[:], XB[:].rearrange("p (k d) -> p k d", k=2),
                                                            BT[b % 2][:, 0:1, :].broadcast_to([128, 2, D]), ALU.mult))
            PL.wait(m)
            xs = X[:, b % 4, 2 * i:2 * i + 2, :]
            m = s["x2p"] = s["x2", b, i] = PL.do(lambda e: e.tensor_tensor(xs, xs, tf[:], ALU.add))
            DVE.wait(m)
            for k in (2 * i, 2 * i + 1):
                m = DVE.do(lambda e, k=k: e.bn_stats(st2[:, k, :], X[:, b % 4, k, :]))
            if i == 1:
                DVE.wait(m, s.get("h2n"))
                for k in range(4):
                    m = DVE.do(lambda e, k=k: e.bn_aggr(mv2[:, k, :], st2[:, k, :]))
                DVE.wait(m)
                m = DVE.do(lambda e: e.tensor_scalar(rs2[:], mv2[:, :, 1], EPS, None, ALU.add))
                PL.wait(m)
                m = s["rs2"] = PL.do(lambda e: e.tensor_tensor(rs2[:], rs2[:], halfc[:], ALU.pow))
                SP.wait(s["x2", b, 0], s["x2", b, 1])
                s["xd", b] = SP.dma(c_xd, lambda e: e.dma_start(xD[b], X[:, b % 4, :, :]))

        def norm2(b):
            DVE.wait(s["rs2"], s.get(("h2T", b - 1, 1)), s.get(("tabw", b - 1)))
            for k in range(4):
                DVE.wait(s.get("h2n"))
                m = DVE.do(lambda e, k=k: e.scalar_tensor_tensor(out=th[:], in0=X[:, b % 4, k, :], scalar=mv2[:, k, 0:1],
                                                                in1=BT[b % 2][:, 1, :], op0=ALU.subtract, op1=ALU.mult))
                DVE.wait(m)
                m = s["h2n"] = DVE.do(lambda e, k=k: e.scalar_tensor_tensor(out=H2[:, k, :], in0=th[:], scalar=rs2[:, k:k + 1],
                                                                           in1=BT[b % 2][:, 2, :], op0=ALU.mult, op1=ALU.add))
            s["h2", b] = m
            SP.wait(m)
            s["tabw", b] = SP.dma(c_h2, lambda e: e.dma_start(tabv[b][:, :, 0:D], H2[:]))
            if b + 4 < NB:
                load_x(b + 4, s["xd", b])
                SP.wait(m)
            if b + 2 < NB:
                load_bt(b + 2, m)

        def h2T(b, c):
            PE.wait(s["h2", b], xfree[0])
            for k in range(4):
                m = PE.do(lambda e, k=k: e.transpose(XB[:, k * 128:(k + 1) * 128], H2[:, k, c * 128:(c + 1) * 128], ident))
            s["h2T", b, c] = m
            AC.wait(m, s.get(("sc", b - 1)), s.get(("hd", b - 1)))
            m1 = AC.do(lambda e: e.activation(h2[:, 0, c, :], XB[:], ACT.Copy))
            DVE.wait(m1, m)
            m = s["h2s", b, c] = xfree[0] = DVE.do(lambda e: e.tensor_tensor(h2[:, 1, c, :], XB[:], h2[:, 0, c, :].bitcast(F32), ALU.subtract))

        def scores(b):
            PE.wait(s["h2s", b, 0], s["h2s", b, 1], xfree[0])
            o = 112 - 16 * b
            m = s["sc", b] = terms3(XB[:], lambda k: GPh[:, k, o:o + 128], lambda k: GPl[:, k, o:o + 128],
                                    lambda k: h2[:, 0, k, :], lambda k: h2[:, 1, k, :])
            DVE.wait(m, s.get("lg"))
            s["lg"] = xfree[0] = DVE.do(lambda e: e.tensor_tensor(LG[:], LG[:], XB[:], ALU.add))
            SP.wait(s["h2s", b, 1])
            s["hd", b] = SP.dma(c_hd, lambda e: e.dma_start(hD[b], h2[:].bitcast(F32)))

        norm1(0)
        hT(0, 0)
        hT(0, 1)
        qk(0, 0, 0)
        qk(0, 0, 1)
        stack(0, 0)
        stack(0, 1)
        qk(0, 1, 0)
        qk(0, 1, 1)
        stack(1, 0)
        stack(1, 1)
        norm1(1)
        vproj(0, 0)
        vproj(0, 1)
        hT(1, 0)
        hT(1, 1)
        for k in range(8):
            maxima(0, k)
            if k % 4 == 3:
                put_max(0, k // 4)

        nu = NU
        AC.wait(m_w, m_modD)
        nb = nu // 2
        for u in range(nu + 2):
            b = u // 2
            for k in range(8):
                if u < nu:
                    main(u, k)
                if u + 1 < nu:
                    maxima(u + 1, k)
                if k == 4 and u < nu:
                    pv(u, 0)
                if k == 0 and 1 <= u <= nu:
                    pv(u - 1, 1)
                if k == 4 and u + 1 < nu:
                    put_max(u + 1, 0)
                if k == 0 and 1 <= u < nu:
                    put_max(u, 1)
                if u % 2 == 0:
                    if b + 1 < nb and k < 6:
                        (lambda: qk(b + 1, 0, 0), lambda: qk(b + 1, 0, 1), lambda: qk(b + 1, 1, 0),
                         lambda: qk(b + 1, 1, 1), lambda: vproj(b + 1, 0), lambda: vproj(b + 1, 1))[k]()
                    if 1 <= b <= nb and k >= 6:
                        outproj(b - 1, k - 6)
                else:
                    if 1 <= b <= nb:
                        if k == 0:
                            norm2(b - 1)
                        if k in (1, 2):
                            h2T(b - 1, k - 1)
                        if k == 3:
                            scores(b - 1)
                    if b + 2 < nb:
                        if k == 4:
                            norm1(b + 2)
                        if k in (5, 6):
                            hT(b + 2, k - 5)
                if k == 4 and 1 <= u <= nu:
                    normalise(u - 1)
                if k in (3, 7) and 2 <= u + 2 < nu:
                    stack(u + 2, k // 4)

        counts = [c_in, c_mod, c_mr, c_gt, c_h2, c_hd, c_xd] + c_x + c_w + c_q + c_nm + c_u + c_ur + c_bt
        ends = [q.last() for q in (PE, DVE, AC, PL)] + [(c.sem, c.n) for c in counts]
        A.close()

        def sb(name, shape, dt=F32):
            return sb_in(ctx, name, shape, dt)

        WG = [[sb(f"WG{i}{p}", [128, 2, F], F32R) for p in "hl"] for i in range(2)]
        WU = [[sb(f"WU{i}{p}", [128, 2, F], F32R) for p in "hl"] for i in range(2)]
        WD = [sb(f"WD{p}", [128, 8, D], F32R) for p in "hl"]
        WR = [sb(f"WR{i}", [128, 2048]) for i in range(2)]
        SIL = [sb(f"SIL{i}", [128, 512]) for i in range(2)]
        HF = [sb(f"HF{i}", [128, 512]) for i in range(2)]
        HTh, HTl = sb("HTh", [128, 8, 512], F32R), sb("HTl", [128, 8, 512], F32R)
        XT = [sb(f"XT{i}", [128, 2, 2, 512], F32R) for i in range(2)]
        EO = sb("EO", [128, 4, D])
        tb = [sb(f"tb{i}", [128, D]) for i in range(2)]
        DB = [sb(f"DB{i}", [128, D]) for i in range(2)]
        OH = sb("OH", [128, 32, 128], BF16)
        V4 = sb("V4", [128, 512, 4, 2], BF16)
        R = sb("R", [128, 512], BF16)
        iotab = sb("iotab", [128, 128], BF16)
        IDX = [sb(f"IDX{i}", [128, 4], U32) for i in range(3)]

        B = ExitStack()
        XL = sb_in(B, "XL", [128, 4, D])
        GBt = [sb_in(B, f"GBt{i}", [128, D]) for i in range(2)]
        S = sb_in(B, "S", [128, 512])
        jk = sb_in(B, "jk", [128, 512], BF16)
        GT = sb_in(B, "GT", [128, 512])
        EQ = sb_in(B, "EQ", [128, 512])
        SC = sb_in(B, "SC", [128, 512])
        PT = sb_in(B, "PT", [128, 512])
        sm = sb_in(B, "sm", [128, 16])
        si = sb_in(B, "si", [128, 4], I32)
        B.close()
        XG = [sb(f"XG{i}", [128, 4, ROW]) for i in range(2)]

        c_wr = [count(f"c_wr{i}") for i in range(2)]
        c_xt = [count(f"c_xt{i}") for i in range(2)]
        c_xl, c_st, c_out, c_cp = count("c_xl"), count("c_st"), count("c_out"), count("c_cp")
        c_gb = [count(f"c_gb{i}") for i in range(2)]
        c_db = [count(f"c_db{i}") for i in range(2)]
        c_xg = [count(f"c_xg{i}") for i in range(2)]
        c_sc = count("c_sc")

        for lane in (PE, DVE, AC, PL, SP):
            lane.wait(*ends)
        setfree = [[ends[0]] * 2, [ends[0]] * 2]
        dfree = [None, None]
        wrfree = [None, None]
        npiece = [0]

        def piece(dst, src, k, n):
            i = npiece[0] % 2
            npiece[0] += 1
            SP.wait(wrfree[i])
            m = SP.dma(c_wr[i], lambda e: e.dma_start(WR[i][:, 0:k * n].rearrange("p (k n) -> p k n", k=k), src))
            rv = WR[i][:, 0:k * n].rearrange("p (k n) -> p k n", k=k)
            cuts = []
            if n >= 512:
                for kk in range(k):
                    for c in range(0, n, 512):
                        cuts.append((slice(kk, kk + 1), slice(c, c + 512)))
            else:
                for kk in range(0, k, 2):
                    cuts.append((slice(kk, kk + 2), slice(0, n)))

            def cut(j):
                ks, cs = cuts[j]

                def f(free=None):
                    AC.wait(m, free)
                    mh = AC.do(lambda e: e.activation(dst[0][:, ks, cs], rv[:, ks, cs], ACT.Copy))
                    DVE.wait(m, mh, free)
                    ml = DVE.do(lambda e: e.tensor_tensor(dst[1][:, ks, cs], rv[:, ks, cs], dst[0][:, ks, cs].bitcast(F32),
                                                          ALU.subtract))
                    wrfree[i] = ml
                    return ml
                return f
            return [cut(j) for j in range(len(cuts))]

        late = []

        def flush():
            while late:
                late.pop(0)()

        def glu(m, i, wg, wu, xt, ready, bg, bu, slot, hfree, mid):
            ps = (LB, MB)[i]
            PE.wait(ready, setfree[i][0])
            cs = slice(128 * m, 128 * m + 128)
            mg = terms3(ps[:, 0:512], lambda k: wg[0][:, k, cs], lambda k: wg[1][:, k, cs],
                        lambda k: xt[:, 0, k, :], lambda k: xt[:, 1, k, :])
            mid()
            PE.wait(setfree[i][1])
            mu = terms3(ps[:, 512:1024], lambda k: wu[0][:, k, cs], lambda k: wu[1][:, k, cs],
                        lambda k: xt[:, 0, k, :], lambda k: xt[:, 1, k, :])
            AC.wait(mg, s.get(("hf", i)))
            ms = setfree[i][0] = AC.do(lambda e: e.activation(SIL[i][:], ps[:, 0:512], ACT.Silu, bias=bg))
            flush()
            DVE.wait(mu, ms, s.get(("ht", i)))
            mf = setfree[i][1] = s["hf", i] = DVE.do(lambda e: e.scalar_tensor_tensor(
                out=HF[i][:], in0=ps[:, 512:1024], scalar=bu, in1=SIL[i][:], op0=ALU.add, op1=ALU.mult))

            def split():
                AC.wait(mf, hfree)
                mh = AC.do(lambda e: e.activation(HTh[:, slot, :], HF[i][:], ACT.Copy))
                PL.wait(mf, mh, hfree)
                s["H", slot] = s["ht", i] = PL.do(lambda e: e.tensor_tensor(HTl[:, slot, :], HF[i][:],
                                                                          HTh[:, slot, :].bitcast(F32), ALU.subtract))
            late.append(split)
            return mu

        def down(q, slots, last):
            ps = (LB, MB)[q % 2][:, 1024:1280]
            PE.wait(dfree[q % 2])
            ts = slice(128 * q, 128 * q + 128)
            seq = [(f, a, b_) for f in range(len(slots)) for a, b_ in ((HTh, WD[0]), (HTh, WD[1]), (HTl, WD[0]))]
            for n_, (f, a, b_) in enumerate(seq):
                if n_ % 3 == 0:
                    PE.wait(s["H", slots[f]])
                g_ = (lambda e, f=f, a=a, b_=b_, n_=n_: e.matmul(ps, a[:, slots[f], ts], b_[:, f, :],
                                                                start=(n_ == 0), stop=(n_ == len(seq) - 1)))
                if n_ == len(seq) - 1:
                    m = PE.do(g_)
                else:
                    PE.quiet(g_)
            return ps, m

        cnt, need, offe, offs, cc = (sm[:, i:i + 1] for i in range(5))
        cur, cand, kept = (si[:, i:i + 1] for i in range(3))
        z = sm[:, 8:9]
        topk = []
        c = {}

        def score_v():
            AC.wait(*ends)
            m = AC.do(lambda e: e.activation(S[:], LG[:], ACT.Exp, scale=-1.0))
            DVE.wait(m)
            m = DVE.do(lambda e: e.tensor_scalar(S[:], S[:], 1.0, None, ALU.add))
            DVE.wait(m)
            m = c["S"] = DVE.do(lambda e: e.reciprocal(S[:], S[:]))
            DVE.do(lambda e: e.tensor_copy(iotab[:], iotaf))
            c["cur"] = DVE.do(lambda e: e.memset(cur, 0))

        def score_p():
            PE.wait(c["S"])
            for k in range(4):
                m = PE.do(lambda e, k=k: e.transpose(UB[:, k * 128:(k + 1) * 128], S[:, k * 128:(k + 1) * 128], ident))
            c["ST"] = m

        def spread_v():
            DVE.wait(c["ST"])
            m = c["PT"] = DVE.do(lambda e: e.tensor_copy(PT[:], UB[:]))
            SP.wait(m)
            for k in range(4):
                dst = tab.rearrange("(b k p) r -> k p b r", k=4, p=128)[k, :, :, D:D + NE]
                c["stored"] = SP.dma(c_st, lambda e, k=k, dst=dst: e.dma_start(
                    dst, PT[:, k * 128:(k + 1) * 128].rearrange("p (b e) -> p b e", e=NE)))

        topk.append((score_v, score_p))
        topk.append((spread_v, lambda: None))

        def bit(n):
            def v():
                if n < 29:
                    DVE.wait(c["mm"])
                    m = DVE.do(lambda e: e.tensor_scalar(kept, XB[:, 0:1], float(CAP), float(1 << (n + 1)), ALU.is_ge, ALU.mult))
                    DVE.wait(m, c["cur"])
                    m = c["cur"] = DVE.do(lambda e: e.tensor_tensor(cur, cur, kept, ALU.bitwise_or))
                DVE.wait(c["cur"])
                if n < 0:
                    return
                m = DVE.do(lambda e: e.tensor_scalar(cand, cur, 1 << n, None, ALU.bitwise_or))
                DVE.wait(m, c.get("cnt"))
                c["cnt"] = DVE.do(lambda e: e.tensor_scalar(jk[:], S[:], cand.bitcast(F32), None, ALU.is_ge, ALU.add, accum_out=cnt))

            def p():
                if n < 0:
                    return
                PE.wait(c["cnt"])
                c["mm"] = PE.do(lambda e: e.matmul(XB[:, 0:1], Gm, cnt, start=True, stop=True))
            return v, p

        for n in range(29, -2, -1):
            topk.append(bit(n))
        thr = cur.bitcast(F32)

        def sel_v():
            DVE.do(lambda e: e.memset(SC[:], 0.0))
            DVE.wait(c["cnt"])
            c["c1"] = DVE.do(lambda e: e.tensor_scalar(GT[:], S[:], thr, None, ALU.is_gt, ALU.add, accum_out=cc))
            m = DVE.do(lambda e: e.tensor_scalar(EQ[:], S[:], thr, None, ALU.is_equal))
            DVE.wait(m, c["stored"])
            c["sE"] = DVE.do(lambda e: e.tensor_tensor_scan(PT[:], EQ[:], SC[:], 0.0, ALU.add, ALU.add))

        def sel_p():
            PE.wait(c["c1"], c["sE"])
            PE.do(lambda e: e.matmul(XB[:, 1:2], Gm, cc, start=True, stop=True))
            c["mm"] = PE.do(lambda e: e.matmul(XB[:, 2:3], Lm, PT[:, 511:512], start=True, stop=True))

        def tie_v():
            DVE.wait(c["mm"])
            DVE.do(lambda e: e.tensor_scalar(need, XB[:, 1:2], -1.0, float(CAP), ALU.mult, ALU.add))
            m = DVE.do(lambda e: e.tensor_copy(offe, XB[:, 2:3]))
            DVE.wait(m, c["sE"])
            m = DVE.do(lambda e: e.tensor_scalar(PT[:], PT[:], offe, need, ALU.add, ALU.is_le))
            DVE.wait(m)
            m = DVE.do(lambda e: e.tensor_tensor(EQ[:], EQ[:], PT[:], ALU.mult))
            DVE.wait(m)
            m = DVE.do(lambda e: e.tensor_tensor(GT[:], GT[:], EQ[:], ALU.add))
            DVE.wait(m)
            c["sS"] = DVE.do(lambda e: e.tensor_tensor_scan(PT[:], GT[:], SC[:], 0.0, ALU.add, ALU.add))

        def tie_p():
            PE.wait(c["sS"])
            c["mm"] = PE.do(lambda e: e.matmul(XB[:, 3:4], Lm, PT[:, 511:512], start=True, stop=True))

        def pos_v():
            SP.wait(c["sS"])
            SP.dma(c_cp, lambda e: e.dma_start(S[:], cpos[:, 512:1024]))
            c["tk"] = SP.dma(c_cp, lambda e: e.dma_start(SC[:], cpos[:, 1024:1536]))
            DVE.wait(c["mm"])
            m = DVE.do(lambda e: e.tensor_copy(offs, XB[:, 3:4]))
            DVE.wait(m)
            c["pos"] = DVE.do(lambda e: e.scalar_tensor_tensor(out=EQ[:], in0=PT[:], scalar=offs, in1=GT[:],
                                                               op0=ALU.add, op1=ALU.mult))

        def pos_p():
            PE.wait(c["pos"], c["PT"])
            for k in range(4):
                m = PE.do(lambda e, k=k: e.transpose(UB[:, k * 128:(k + 1) * 128], EQ[:, k * 128:(k + 1) * 128], ident))
            c["mm"] = m

        def val_v():
            mt = c["tk"]
            DVE.wait(c["mm"])
            m = c["ub"] = DVE.do(lambda e: e.tensor_scalar(PT[:], UB[:], -1.0, None, ALU.add))
            DVE.wait(m)
            m = DVE.do(lambda e: e.tensor_scalar(GT[:], PT[:], 128.0, None, ALU.is_ge))
            for v_ in (256.0, 384.0):
                DVE.wait(m)
                m = DVE.do(lambda e, v_=v_: e.scalar_tensor_tensor(out=GT[:], in0=PT[:], scalar=v_, in1=GT[:], op0=ALU.is_ge, op1=ALU.add))
            DVE.wait(m, mt)
            c["R"] = DVE.do(lambda e: e.scalar_tensor_tensor(out=R[:], in0=GT[:], scalar=-128.0, in1=PT[:], op0=ALU.mult, op1=ALU.add))
            for q in range(4):
                for v_, src in enumerate((S, SC)):
                    m = DVE.do(lambda e, q=q, v_=v_, src=src: e.scalar_tensor_tensor(
                        out=V4[:, :, q, v_], in0=GT[:], scalar=float(q), in1=src[:], op0=ALU.is_equal, op1=ALU.mult))
            c["V4"] = m

        topk += [(sel_v, sel_p), (tie_v, tie_p), (pos_v, pos_p), (val_v, lambda: None)]

        def onehot(e_, part):
            ks = slice(8 * part, 8 * part + 8)
            rv = R[:].rearrange("p (k e) -> p k e", e=NE)[:, ks, e_:e_ + 1].broadcast_to([128, 8, 128])
            DVE.wait(c["R"], s.get(("idx", e_ - 1)))
            s["oh", e_] = DVE.do(lambda e: e.tensor_tensor(OH[:, ks, :], rv, iotab[:].unsqueeze(1).broadcast_to([128, 8, 128]),
                                                           ALU.is_equal))

        def index(e_):
            PE.wait(s["oh", e_], c["V4"], c["ub"])
            PE.wait(s.get(("idxc", e_ - 1)))
            for k in range(32):
                f = (lambda e, k=k: e.matmul(UB[:, 0:8], OH[:, k, :], V4[:, k * 16 + e_, :, :].rearrange("p q v -> p (q v)"),
                                             start=(k == 0), stop=(k == 31)))
                if k < 31:
                    PE.quiet(f)
                else:
                    m = s["idx", e_] = PE.do(f)
            DVE.wait(m, s.get(("gx", e_ - 3)), s.get(("scat", e_ - 3)))
            uv = UB[:, 0:8].rearrange("p (q v) -> p q v", v=2)
            m = DVE.do(lambda e: e.tensor_copy(sm2[:], UB[:, 0:8]))
            DVE.wait(m)
            sv = sm2[:].rearrange("p (q v) -> p q v", v=2)
            m = s["idxc", e_] = DVE.do(lambda e: e.scalar_tensor_tensor(out=IDX[e_ % 3][:], in0=sv[:, :, 1], scalar=128.0,
                                                                       in1=sv[:, :, 0], op0=ALU.mult, op1=ALU.add))
            PL.wait(m, c["stored"], s.get(("eo", e_ - 2)))
            for q in range(4):
                s["gx", e_] = PL.dma(c_xg[e_ % 2], lambda e, q=q: e.indirect_dma_start(
                    out=XG[e_ % 2][:, q, :], out_offset=None, in_=tab,
                    in_offset=bass.IndirectOffsetOnAxis(ap=IDX[e_ % 3][:, q:q + 1], axis=0)))

        sm2 = sb("sm2", [128, 8])

        def turn(e_, ck):
            PE.wait(s["gx", e_], s.get("xb"))
            for q in range(4):
                m = PE.do(lambda e, q=q: e.transpose(XB[:, q * 128:(q + 1) * 128], XG[e_ % 2][:, q, ck * 128:(ck + 1) * 128], ident))
            AC.wait(m, s.get(("glu", e_ - 2)))
            m1 = AC.do(lambda e: e.activation(XT[e_ % 2][:, 0, ck, :], XB[:], ACT.Copy))
            DVE.wait(m, m1)
            s["xt", e_] = s["xb"] = DVE.do(lambda e: e.tensor_tensor(XT[e_ % 2][:, 1, ck, :], XB[:],
                                                                     XT[e_ % 2][:, 0, ck, :].bitcast(F32), ALU.subtract))

        def kn(src):
            return src.rearrange("(k p) n -> p k n", p=128)

        for dst, src, k, n in (([w[:, :, 0:SH] for w in WG[1]], sg, 2, SH), ([w[:, :, 0:SH] for w in WU[1]], su, 2, SH),
                               ([w[:, 0:4, :] for w in WD], sd, 4, D)):
            for f in piece(dst, kn(src), k, n):
                mw = f()
        s["wd"] = s["w"] = mw

        def load_h(b):
            SP.wait(s.get(("glub", b - 2)))
            s["xtb", b] = SP.dma(c_xt[b % 2], lambda e: e.dma_start(XT[b % 2][:].bitcast(F32), hD[b]))
            SP.wait(s.get(("xlf", b - 2)))
            s["gbt", b] = SP.dma(c_gb[b % 2], lambda e: e.dma_start(GBt[b % 2][:], modD[b, 5:6, :].broadcast_to([128, D])))

        steps = list(topk)

        def step_v():
            if steps:
                steps[0][0]()

        def step_p():
            if steps:
                steps.pop(0)[1]()

        load_h(0)
        step_v()
        step_p()
        cuts0 = []
        for b in range(NB):
            if b + 1 < NB:
                load_h(b + 1)
            if b == 0:
                pass
            for m_ in range(4):
                i = m_ % 2
                slot = 4 * (b % 2) + m_
                step_v()

                def mid():
                    step_p()
                    step_v()
                PE.wait(mw)
                s["glub", b] = glu(m_, i, [w[:, :, 0:SH] for w in WG[1]], [w[:, :, 0:SH] for w in WU[1]], XT[b % 2],
                                   s["xtb", b], 0.0, 0.0, slot, s.get(("downb", b - 2)), mid)
                step_p()
                if b == 4 and m_ == 0:
                    cuts0 += piece(WG[0], kn(gw[0]), 2, F)
                    cuts0 += piece(WU[0], kn(uw[0]), 2, F)
                if b > 4 and cuts0:
                    s["w"] = cuts0.pop(0)()
            flush()
            SP.wait(s.get(("xlf", b - 1)))
            s["xl", b] = SP.dma(c_xl, lambda e, b=b: e.dma_start(XL[:], xD[b]))
            for q in range(4):
                ps, m = down(q, [4 * (b % 2) + j for j in range(4)], None)
                s["downb", b] = m
                DVE.wait(m, s["gbt", b], s.get(("tb", q % 2)))
                m = DVE.do(lambda e, ps=ps, q=q, b=b: e.tensor_tensor(tb[q % 2][:], ps, GBt[b % 2][:], ALU.mult))
                dfree[q % 2] = m
                DVE.wait(m, s["xl", b], s.get(("outb", b - 1)))
                m = s["tb", q % 2] = DVE.do(lambda e, q=q: e.tensor_tensor(EO[:, q, :], tb[q % 2][:], XL[:, q, :], ALU.add))
                step_v()
                step_p()
            s["xlf", b] = m
            SP.wait(m)
            s["outb", b] = SP.dma(c_out, lambda e, b=b: e.dma_start(outv[b], EO[:]))
        while steps:
            step_v()
            step_p()
        while cuts0:
            s["w"] = cuts0.pop(0)()

        for n_ in range(2):
            s["eo", n_ - 2] = s["xlf", NB - 1]
            s["glu", n_ - 2] = s["glub", NB - 2 + n_]
        PL.wait(c["V4"], c["stored"], s["outb", NB - 1])
        for p_ in range(4):
            onehot(0, p_)
        index(0)
        turn(0, 0)
        turn(0, 1)
        cutsd = piece(WD, kn(dw[0]), 8, D)
        s["downb", -1] = s["downb", NB - 1]
        dlast = s["downb", NB - 1]

        def load_db(e_):
            SP.wait(s.get(("eo", e_ - 2)))
            s["db", e_] = SP.dma(c_db[e_ % 2], lambda e: e.dma_start(DB[e_ % 2][:], db[e_:e_ + 1, :].broadcast_to([128, D])))

        load_db(0)
        scat = [s["outb", NB - 1]]
        for e_ in range(NE):
            nxt = e_ + 1 < NE
            if nxt:
                load_db(e_ + 1)
            wfree = s.get(("glu", e_ - 1))
            ready_w = s["w"]
            cutsn = []
            for m_ in range(8):
                PE.wait(ready_w)
                s["glu", e_] = glu(m_, m_ % 2, WG[e_ % 2], WU[e_ % 2], XT[e_ % 2], s["xt", e_],
                                   gbT[:, e_, m_:m_ + 1], ubT[:, e_, m_:m_ + 1], m_, dlast, lambda: None)
                if cutsd:
                    s["wd"] = cutsd.pop(0)(dlast)
                if m_ == 1 and nxt:
                    cutsn += piece(WG[(e_ + 1) % 2], kn(gw[e_ + 1]), 2, F)
                if m_ == 3 and nxt:
                    cutsn += piece(WU[(e_ + 1) % 2], kn(uw[e_ + 1]), 2, F)
                if m_ >= 4 and cutsn:
                    s["w"] = cutsn.pop(0)(wfree)
                if nxt and m_ < 4:
                    onehot(e_ + 1, m_)
                if nxt and m_ == 4:
                    index(e_ + 1)
            flush()
            if nxt:
                turn(e_ + 1, 0)
                turn(e_ + 1, 1)
            PE.wait(s["wd"])
            PL.wait(scat[0])
            for q in range(4):
                ps, m = down(q, list(range(8)), None)
                dlast = m
                DVE.wait(m, s["db", e_], s.get(("tb", q % 2)))
                m = DVE.do(lambda e, ps=ps, q=q, e_=e_: e.tensor_tensor(tb[q % 2][:], ps, DB[e_ % 2][:], ALU.add))
                dfree[q % 2] = m
                DVE.wait(m, scat[0])
                xg = XG[e_ % 2]
                m = s["tb", q % 2] = DVE.do(lambda e, q=q, xg=xg, e_=e_: e.scalar_tensor_tensor(
                    out=EO[:, q, :], in0=tb[q % 2][:], scalar=xg[:, q, D + e_:D + e_ + 1], in1=xg[:, q, D + NE:ROW],
                    op0=ALU.mult, op1=ALU.mult))
                PL.wait(m)
                sc_ = PL.dma(c_sc, lambda e, q=q, e_=e_: e.indirect_dma_start(
                    out=out2, out_offset=bass.IndirectOffsetOnAxis(ap=IDX[e_ % 3][:, q:q + 1], axis=0),
                    in_=EO[:, q, :], in_offset=None, compute_op=ALU.add))
                if cutsn:
                    s["w"] = cutsn.pop(0)(wfree)
            scat[0] = s["scat", e_] = sc_
            s["eo", e_] = m
            while cutsn:
                s["w"] = cutsn.pop(0)(wfree)
            if nxt:
                cutsd = piece(WD, kn(dw[e_ + 1]), 8, D)
        PL.wait(scat[0])

        block = ctx.enter_context(nc.Block())

        @block.sync
        def _(e):
            SP.emit(e)

        @block.scalar
        def _(e):
            AC.emit(e)

        @block.gpsimd
        def _(e):
            PL.emit(e)

        @block.vector
        def _(e):
            DVE.emit(e)

        @block.tensor
        def _(e):
            PE.emit(e)


def constants():
    import numpy as np

    p = np.arange(128)
    cst = np.zeros((128, 512), np.float32)
    cst[:, 0:128] = np.eye(128)
    cst[:, 128:256] = (p[:, None] % 16) == (p[None, :] % 16)
    cst[:, 256:384] = ((p[:, None] % 16) == (p[None, :] % 16)) & (p[:, None] // 16 < p[None, :] // 16)
    cst[:, 384:512] = p[None, :]
    cpos = np.zeros((128, 512 * 3), np.float32)
    cpos[:, 384:512] = np.where(p[None, :] > p[:, None], NEG, 0.0)
    cpos[:, 512:1024] = p[:, None]
    j = np.arange(512)
    cpos[:, 1024:1536] = ((j % 128) // 16 * 4 + j // 128)[None, :]
    return cst, cpos


def kernel(**inputs):
    import numpy as _np
    import concourse.bacc as _bacc
    from concourse import mybir as _mybir
    from concourse.bass_utils import run_bass_kernel_spmd as _run

    def c(a):
        return _np.ascontiguousarray(a)

    g = {n[3:]: _np.asarray(a) for n, a in inputs.items()}
    cst, cpos = constants()
    laid = {
        "x": c(g["attn_hidden_states"]),
        "wq": c(g["attn_Wq"].T),
        "wkd": c(g["attn_Wk_down"]),
        "wvd": c(g["attn_Wv_down"]),
        "q2l": c(g["attn_q_to_latent"].transpose(2, 0, 1).reshape(64, NH * DH)),
        "vup": c(g["attn_v_up"].transpose(1, 0, 2).reshape(64, NH * DH)),
        "wo": c(g["attn_Wout"].T),
        "gate": c(g["ffn_gate_w"].T),
        "uw": c(g["ffn_up_w"].transpose(0, 2, 1)),
        "ub": c(g["ffn_up_b"].reshape(NE, 8, 128).transpose(2, 0, 1).reshape(128, NE * 8)),
        "gw": c(g["ffn_gw"].transpose(0, 2, 1)),
        "gb": c(g["ffn_gb"].reshape(NE, 8, 128).transpose(2, 0, 1).reshape(128, NE * 8)),
        "dw": c(g["ffn_down_w"].transpose(0, 2, 1)),
        "db": c(g["ffn_down_b"]),
        "sg": c(g["ffn_sh_gate_w"].T),
        "su": c(g["ffn_sh_up_w"].T),
        "sd": c(g["ffn_sh_down_w"].T),
        "ct": c(g["c"].T),
        "wmod": c(g["wmod"]),
        "cst": cst,
        "cpos": cpos,
    }
    nc = _bacc.Bacc("TRN2", target_bir_lowering=False, num_devices=1)
    arrays, args = {}, {}
    for name, a in laid.items():
        arrays["in_" + name] = a
        args[name] = nc.dram_tensor("in_" + name, a.shape, _mybir.dt.from_np(a.dtype), kind="ExternalInput").ap()
    out = nc.dram_tensor("out_y", (NB, T, D), F32, kind="ExternalOutput").ap()
    block_program(nc, out=out, **args)
    r = _run(nc, [arrays], core_ids=[0])
    return r.results[0]["out_y"]
```

```python
from contextlib import ExitStack

import concourse.bass as bass
from concourse import mybir

ALU = mybir.AluOpType
ACT = mybir.ActivationFunctionType
F32 = mybir.dt.float32
F32R = mybir.dt.float32r
BF16 = mybir.dt.bfloat16
I32 = mybir.dt.int32
U32 = mybir.dt.uint32

NB = 8
T = 512
D = 256
NH = 16
DH = 16
NU = 16
NE = 16
F = 1024
SH = 512
CAP = 512
EPS = 1e-5
NEG = -1e30
ROW = D + NE + D

SPAN = {0: (0, 512), 1: (512, 384), 3: (896, 128), 2: (1024, 256)}
MSPAN = {3: (0, 512), 2: (512, 384), 0: (896, 128), 1: (1024, 256)}


class Lane:

    def __init__(self, sem):
        self.sem, self.n, self.ops, self.seen = sem, 0, [], {}

    def wait(self, *marks):
        for m in marks:
            if m is None:
                continue
            sem, v = m
            if self.seen.get(sem.name, 0) < v:
                self.seen[sem.name] = v
                self.ops.append((None, sem, v))

    def do(self, f):
        self.n += 1
        self.ops.append((f, self.sem, 1))
        return (self.sem, self.n)

    def quiet(self, f):
        self.ops.append((f, None, 0))

    def dma(self, c, f):
        c.n += 16
        self.ops.append((f, c.sem, 16))
        return (c.sem, c.n)

    def last(self):
        return (self.sem, self.n)

    def emit(self, eng):
        for f, sem, v in self.ops:
            if f is None:
                eng.wait_ge(sem, v)
            elif sem is None:
                f(eng)
            else:
                f(eng).then_inc(sem, v)


class Count:

    def __init__(self, sem):
        self.sem, self.n = sem, 0


def block_program(nc, x, wq, wkd, wvd, q2l, vup, wo, gate, uw, ub, gw, gb, dw, db, sg, su, sd, ct, wmod,
                  cst, cpos, out):
    ctx = ExitStack()
    with ctx:
        def sem(name):
            return ctx.enter_context(nc.semaphore(name))

        def sb_in(stack, name, shape, dt=F32):
            return stack.enter_context(nc.sbuf_tensor(name, shape, dt))

        def dram(name, shape, dt=F32):
            return nc.dram_tensor(name, shape, dt).ap()

        PE, DVE, AC, PL, SP = (Lane(sem(n)) for n in ("s_pe", "s_dve", "s_act", "s_pool", "s_sp"))

        def count(name):
            return Count(sem(name))

        LB = ctx.enter_context(nc.psum_tensor("LB", [128, 1536], F32))
        MB = ctx.enter_context(nc.psum_tensor("MB", [128, 1536], F32))
        UB = ctx.enter_context(nc.psum_tensor("UB", [128, 512], F32))
        XB = ctx.enter_context(nc.psum_tensor("XB", [128, 512], F32))

        modD = dram("modD", [NB, 6, D])
        sdD = dram("sdD", [NU, 2, 128, 2, 512])
        udD = dram("udD", [NU, 2, 128, 512])
        rdD = dram("rdD", [NU, 8, 512])
        hD = dram("hD", [NB, 128, 2, 2, 512])
        xD = dram("xD", [NB, 128, 4, D])
        tab = dram("tab", [NB * T, ROW])
        tabv = tab.rearrange("(b k p) r -> b p k r", k=4, p=128)
        outv = out.rearrange("b (k p) d -> b p k d", p=128)
        out2 = out.rearrange("b t d -> (b t) d")
        xv = x.rearrange("b (k p) d -> b p k d", p=128)

        C = sb_in(ctx, "C", [128, 512])
        ident, Gm, Lm, iotaf = C[:, 0:128], C[:, 128:256], C[:, 256:384], C[:, 384:512]
        LG = sb_in(ctx, "LG", [128, 512])
        ubT = sb_in(ctx, "ubT", [128, NE, 8])
        gbT = sb_in(ctx, "gbT", [128, NE, 8])

        A = ExitStack()

        def sa(name, shape, dt=F32):
            return sb_in(A, name, shape, dt)

        W = {"wo": (sa("woh", [128, 2, 256], F32R), sa("wol", [128, 2, 256], F32R))}
        GPh, GPl = sa("GPh", [128, 2, 240], F32R), sa("GPl", [128, 2, 240], F32R)
        X = sa("X", [128, 4, 4, D])
        HT = [sa(f"HT{i}", [128, 512]) for i in range(2)]
        DN = [sa(f"DN{i}", [128, 512]) for i in range(2)]
        D8 = [sa(f"D8{i}", [128, 32]) for i in range(2)]
        nf = sa("nf", [128, 512])
        HNh = sa("HNh", [128, 2, 512], F32R)
        HNl = sa("HNl", [128, 2, 512], F32R)
        BT = [sa(f"BT{i}", [128, 3, D]) for i in range(2)]
        tf = sa("tf", [128, 2, D])
        th = sa("th", [128, 4, D])
        H2 = sa("H2", [128, 4, D])
        h2 = sa("h2", [128, 2, 2, 512], F32R)
        halfc = sa("halfc", [128, 4])
        st2 = sa("st2", [128, 4, 6])
        mv2 = sa("mv2", [128, 4, 2])
        rs2 = sa("rs2", [128, 4])
        nm2 = sa("nm2", [128, 4])

        for n in ("wq", "wk", "wv"):
            W[n] = (sa(n + "h", [128, 2, 256], F32R), sa(n + "l", [128, 2, 256], F32R))
        MK = sa("MK", [128, 512])
        modT = sa("modT", [128, 2, 2, NB])
        QS = sa("QS", [128, 8, 512], F32R)
        KS = sa("KS", [128, 8, 512], F32R)
        xh = sa("xh", [128, 4, D])
        st = sa("st", [128, 4, 6])
        mv = sa("mv", [128, 4, 2])
        rs = sa("rs", [128, 4])
        nm1 = sa("nm1", [128, 4])
        hf = sa("hf", [128, 2, 512])
        hh = sa("hh", [128, 2, 512], F32R)
        hl = sa("hl", [128, 2, 512], F32R)
        ST = [sa(f"ST{i}", [128, 2, 512], F32R) for i in range(4)]
        V = [sa(f"V{i}", [128, 4, NH, 32]) for i in range(2)]
        NM = sa("NM", [128, 2, 16])
        NMh = [sa(f"NMh{i}", [16, 128], F32R) for i in range(2)]
        NMl = [sa(f"NMl{i}", [16, 128], F32R) for i in range(2)]
        junk = sa("junk", [128, 1280], BF16)
        Us = [sa(f"Us{i}", [128, 512]) for i in range(2)]
        pro = ExitStack()
        wqr, wor = sb_in(pro, "wqr", [128, 512]), sb_in(pro, "wor", [128, 512])
        kdr = sb_in(pro, "kdr", [64, 4, 256])
        grr = sb_in(pro, "grr", [128, 96])
        modS = sb_in(pro, "modS", [NB, 6 * D])
        modA = sb_in(pro, "modA", [NB, 2, D])
        modB = sb_in(pro, "modB", [NB, 2, D])
        WM = sb_in(pro, "WM", [128, 2, 3 * 512])
        pro.close()
        NP = 6
        P = [sa(f"P{i}", [128, 1280]) for i in range(NP)]

        c_in, c_mod, c_mr = count("c_in"), count("c_mod"), count("c_mr")
        c_in0, c_in1, c_in2 = count("c_in0"), count("c_in1"), count("c_in2")
        c_x = [count(f"c_x{i}") for i in range(4)]
        c_w = [count(f"c_w{i}") for i in range(4)]
        c_q = [count(f"c_q{i}") for i in range(4)]
        c_nm = [count(f"c_nm{i}") for i in range(2)]
        c_u = [count(f"c_u{i}") for i in range(2)]
        c_ur = [count(f"c_ur{i}") for i in range(2)]
        c_bt = [count(f"c_bt{i}") for i in range(2)]
        c_gt = count("c_gt")
        c_d8 = [count(f"c_d8{i}") for i in range(2)]
        c_rd = [count(f"c_rd{i}") for i in range(2)]
        c_h2, c_hd, c_xd = count("c_h2"), count("c_hd"), count("c_xd")

        raw = {"wq": wqr[:], "wo": wor[:]}
        kd, vd, q2, vu = (kdr[:, i, :] for i in range(4))
        gr = grr[:, 0:32]
        cT = grr[:, 32:48]
        sT = grr[:, 64:80]

        m_xl, m_bt = {}, {}

        def load_x(b, free=None):
            SP.wait(free)
            m_xl[b] = SP.dma(c_x[b % 4], lambda e: e.dma_start(X[:, b % 4, :, :], xv[b]))

        def load_bt(b, free=None):
            SP.wait(free, m_modD)
            for i, r in enumerate((2, 4, 3)):
                m_bt[b] = SP.dma(c_bt[b % 2], lambda e, i=i, r=r: e.dma_start(
                    BT[b % 2][:, i, :], modD[b, r:r + 1, :].broadcast_to([128, D])))
            SP.dma(c_gt, lambda e: e.dma_start(tab[b * T:(b + 1) * T, D + NE:ROW], modD[b, 5:6, :].broadcast_to([T, D])))

        wmv = wmod.rearrange("(k p) n -> p k n", p=128)
        load_x(0)
        SP.dma(c_in0, lambda e: e.dma_start(cT.rearrange("p (k b) -> p k b", k=2), ct.rearrange("(k p) b -> p k b", p=128)))
        m_wm = SP.dma(c_in0, lambda e: e.dma_start(WM[:, :, 0:512], wmv[:, :, 0:512]))
        m_cst = SP.dma(c_in1, lambda e: e.dma_start(C[:], cst))
        for dst, src in ((kd, wkd), (vd, wvd), (q2, q2l), (vu, vup)):
            m_kv = SP.dma(c_in2, lambda e, dst=dst, src=src: e.dma_start(dst, src))
        for n, src in (("wq", wq), ("wo", wo)):
            SP.dma(c_in, lambda e, n=n, src=src: e.dma_start(raw[n].rearrange("p (k n) -> p k n", k=2), src.rearrange("(k p) n -> p k n", p=128)))
        SP.dma(c_in, lambda e: e.dma_start(gr.rearrange("p (k n) -> p k n", k=2), gate.rearrange("(k p) n -> p k n", p=128)))
        SP.dma(c_in, lambda e: e.dma_start(MK[:], cpos[:, 0:512]))
        SP.dma(c_in, lambda e: e.dma_start(ubT[:].rearrange("p e m -> p (e m)"), ub))
        m_in = SP.dma(c_in, lambda e: e.dma_start(gbT[:].rearrange("p e m -> p (e m)"), gb))
        load_x(1)
        m_wm2 = SP.dma(c_mod, lambda e: e.dma_start(WM[:, :, 512:], wmv[:, :, 512:]))
        for b in range(2, 4):
            load_x(b)

        m_half = PL.do(lambda e: e.memset(halfc[:], -0.5))
        PL.wait(m_half)
        m = PL.do(lambda e: e.memset(KS[32:64, :, :].bitcast(F32), 1.0))
        PL.wait(m)
        m_ks = PL.do(lambda e: e.memset(KS[96:128, :, :].bitcast(F32), 1.0))
        PL.wait(m_ks)
        for i in range(2):
            m_vs = PL.do(lambda e, i=i: e.memset(V[i][:], 1.0))
        PL.do(lambda e: e.memset(GPh[:].bitcast(F32), 0.0))
        PL.do(lambda e: e.memset(GPl[:].bitcast(F32), 0.0))
        m_gp = PL.do(lambda e: e.memset(LG[:], 0.0))
        PL.wait(m_gp)
        s = {}

        AC.wait(m_wm)
        m = AC.do(lambda e: e.activation(sT, cT, ACT.Exp, scale=-1.0))
        DVE.wait(m)
        m = DVE.do(lambda e: e.tensor_scalar(sT, sT, 1.0, None, ALU.add))
        DVE.wait(m)
        m = DVE.do(lambda e: e.reciprocal(sT, sT))
        DVE.wait(m)
        m_sT = DVE.do(lambda e: e.tensor_tensor(sT, sT, cT, ALU.mult))
        PE.wait(m_sT, m_wm)
        for c4 in range(4):
            for k in range(2):
                m = PE.do(lambda e, c4=c4, k=k: e.matmul(UB[:, c4 * 8:c4 * 8 + 8], WM[:, k, c4 * 128:(c4 + 1) * 128],
                                                        sT[:, 8 * k:8 * k + 8], start=(k == 0), stop=(k == 1)))
        m_modp = m

        PE.wait(m_kv)
        for dst, (a, r) in ((0, (kd, q2)), (1, (vd, vu))):
            for c in range(2):
                m_fold = PE.do(lambda e, dst=dst, a=a, r=r, c=c: e.matmul(
                    MB[:, dst * 512 + c * 256:dst * 512 + c * 256 + 256], a[:, c * 128:(c + 1) * 128], r, start=True, stop=True))
        srcs = {"wk": MB[:, 0:512], "wv": MB[:, 512:1024], "wq": raw["wq"], "wo": raw["wo"]}

        def split_weight(n):
            DVE.wait(m_fold, m_in)
            h_, l_ = (W[n][i][:].rearrange("p k n -> p (k n)") for i in range(2))
            m = DVE.do(lambda e: e.tensor_copy(h_, srcs[n]))
            DVE.wait(m)
            return DVE.do(lambda e: e.tensor_tensor(l_, srcs[n], h_.bitcast(F32), ALU.subtract))

        def column_mod():
            DVE.wait(m_modp)
            m = DVE.do(lambda e: e.tensor_copy(modT[:].rearrange("p a c b -> p (a c b)"), UB[:, 0:32]))
            DVE.wait(m)
            return m, DVE.do(lambda e: e.tensor_scalar(modT[:, 1, :, :], modT[:, 1, :, :], 1.0, None, ALU.add))

        def split_gate():
            grv = gr.rearrange("p (k n) -> p k n", k=2)
            DVE.wait(m_in, m_gp)
            m = DVE.do(lambda e: e.tensor_copy(GPh[:, :, 112:128], grv))
            DVE.wait(m)
            return DVE.do(lambda e: e.tensor_tensor(GPl[:, :, 112:128], grv, GPh[:, :, 112:128].bitcast(F32), ALU.subtract))

        def row_mod():
            PE.wait(m_wm2)
            for g in range(3):
                for k in range(2):
                    m = PE.do(lambda e, g=g, k=k: e.matmul(LB[0:NB, g * 512:(g + 1) * 512], sT[:, 8 * k:8 * k + 8],
                                                          WM[:, k, g * 512:(g + 1) * 512], start=(k == 0), stop=(k == 1)))
            DVE.wait(m)
            m = m_l = DVE.do(lambda e: e.tensor_copy(modS[:], LB[0:NB, :]))
            DVE.wait(m)
            gates = modS[:].rearrange("p (a r d) -> p a r d", a=2, r=3)[:, :, 2, :]
            m = DVE.do(lambda e: e.scalar_tensor_tensor(out=modA[:], in0=gates, scalar=-1.0, in1=gates, op0=ALU.mult, op1=ALU.max))
            DVE.do(lambda e: e.tensor_scalar(modB[:], gates, 0.0, 2.0, ALU.is_ge, ALU.mult))
            DVE.wait(m)
            DVE.do(lambda e: e.tensor_scalar(modA[:], modA[:], 0.25, None, ALU.max))
            DVE.wait(DVE.last())
            m = DVE.do(lambda e: e.tensor_scalar(modB[:], modB[:], -1.0, None, ALU.add))
            DVE.wait(m)
            DVE.do(lambda e: e.tensor_tensor(gates, modA[:], modB[:], ALU.mult))
            m = DVE.do(lambda e: e.tensor_scalar(modS[:, 4 * D:5 * D], modS[:, 4 * D:5 * D], 1.0, None, ALU.add))
            SP.wait(m)
            return m_l, SP.dma(c_mr, lambda e: e.dma_start(modD.rearrange("b r d -> b (r d)"), modS[:]))

        xfree = [None]
        ufree = [None]
        lfree = [None] * 3
        mfree = [None] * 3

        def terms3(ps, lh, ll, rh, rl):
            seq = [(c, a, b) for c in range(2) for a, b in ((lh, rh), (lh, rl), (ll, rh))]
            for i, (c, a, b) in enumerate(seq):
                f = (lambda e, i=i, c=c, a=a, b=b: e.matmul(ps, a(c), b(c), start=(i == 0), stop=(i == 5)))
                if i < 5:
                    PE.quiet(f)
                else:
                    m = PE.do(f)
            return m

        def stats(b, blocks, stt, mvt):
            for k in blocks:
                m = DVE.do(lambda e, k=k: e.bn_stats(stt[:, k, :], X[:, b % 4, k, :]))
            return m

        def moments(stt, mvt, rst, nmt, after, free):
            DVE.wait(after, free)
            for k in range(4):
                m = DVE.do(lambda e, k=k: e.bn_aggr(mvt[:, k, :], stt[:, k, :]))
            DVE.wait(m)
            DVE.do(lambda e: e.tensor_scalar(rst[:], mvt[:, :, 1], EPS, None, ALU.add))
            m = DVE.do(lambda e: e.tensor_scalar(nmt[:], mvt[:, :, 0], -1.0, None, ALU.mult))
            PL.wait(m, m_half)
            m = PL.do(lambda e: e.tensor_tensor(rst[:], rst[:], halfc[:], ALU.pow))
            PL.wait(m)
            return PL.do(lambda e: e.tensor_tensor(nmt[:], nmt[:], rst[:], ALU.mult))

        def stats1(b):
            DVE.wait(m_xl[b], s.get("rs1"))
            s["s1", b] = stats(b, range(4), st, mv)

        def moments1(b):
            s["m1", b] = s["rs1"] = moments(st, mv, rs, nm1, s["s1", b], s.get(("xh", b - 1)))

        def scale1(b, half):
            AC.wait(s["m1", b], s.get(("hTp", b - 1)), m_xl[b])
            for k in (2 * half, 2 * half + 1):
                m = AC.do(lambda e, k=k: e.activation(xh[:, k, :], X[:, b % 4, k, :], ACT.Identity, bias=nm1[:, k:k + 1],
                                                      scale=rs[:, k:k + 1]))
            s["xh", b] = m

        def hT(b, c, bk=0):
            ps, free = ((XB, xfree), (UB, ufree))[bk]
            PE.wait(s["xh", b], free[0], m_cst)
            for k in range(4):
                m = PE.do(lambda e, k=k: e.transpose(ps[:, k * 128:(k + 1) * 128], xh[:, k, c * 128:(c + 1) * 128], ident))
            s["hTp", b] = m
            AC.wait(m, s.get(("hs", b - 1, c)), m_modT)
            m = free[0] = AC.do(lambda e: e.activation(hf[:, c, :], ps[:], ACT.Identity, bias=modT[:, 0, c, b:b + 1],
                                                        scale=modT[:, 1, c, b:b + 1]))
            DVE.wait(m, s.get(("proj", b - 1)))
            m = DVE.do(lambda e: e.tensor_copy(hh[:, c, :], hf[:, c, :]))
            PL.wait(m, s.get(("proj", b - 1)))
            s["hs", b, c] = PL.do(lambda e: e.tensor_tensor(hl[:, c, :], hf[:, c, :], hh[:, c, :].bitcast(F32), ALU.subtract))

        def qk(b, c, kind, bk=0):
            ps, free = ((XB, xfree), (UB, ufree))[bk]
            u = 2 * b + c
            sl = 2 * (u % 2) + kind
            wh, wl = W["wk" if kind else "wq"]
            PE.wait(s["hs", b, 0], s["hs", b, 1], free[0])
            m = terms3(ps[:], lambda k: wh[:, k, c * 128:(c + 1) * 128], lambda k: wl[:, k, c * 128:(c + 1) * 128],
                       lambda k: hh[:, k, :], lambda k: hl[:, k, :])
            sc = 1.0 if kind else 0.125
            AC.wait(m, s.get(("stw", u - 2, kind)))
            m1 = AC.do(lambda e: e.activation(ST[sl][:, 0, :], ps[:], ACT.Copy, scale=sc))
            DVE.wait(m1, m)
            m2 = free[0] = DVE.do(lambda e: e.scalar_tensor_tensor(out=ST[sl][:, 1, :], in0=ps[:], scalar=sc,
                                                                   in1=ST[sl][:, 0, :].bitcast(F32), op0=ALU.mult, op1=ALU.subtract))
            SP.wait(m1, m2)
            s["stw", u, kind] = SP.dma(c_w[sl], lambda e: e.dma_start(sdD[u, kind], ST[sl][:].bitcast(F32)))
            s["proj", b] = m

        def stack(u, half):
            base = 64 * (u % 2)
            SP.wait(s["stw", u, 0], s["stw", u, 1], s.get(("main", u - 2, 4 * half + 3)), m_ks)
            hs = slice(4 * half, 4 * half + 4)
            for kind, dst in ((0, QS), (1, KS)):
                src = sdD[u, kind].rearrange("(h d) k t -> k d h t", d=DH)
                for r, part in enumerate((0, 1, 0) if kind == 0 else (0, 0, 1)):
                    m = SP.dma(c_q[2 * (u % 2) + half], lambda e, r=r, part=part, dst=dst, src=src: e.dma_start(
                        dst[base + 16 * r:base + 16 * r + 16, hs, :].bitcast(F32), src[part, :, hs, :]))
            s["stack", u, half] = m

        def vproj(b, i, bk=0):
            ps, free = ((XB, xfree), (UB, ufree))[bk]
            PE.wait(s["hs", b, 0], s["hs", b, 1], free[0])
            wh, wl = W["wv"]
            for j in range(2):
                t0 = (2 * i + j) * 128
                m = terms3(ps[:, j * 256:(j + 1) * 256], lambda k, t0=t0: hh[:, k, t0:t0 + 128],
                           lambda k, t0=t0: hl[:, k, t0:t0 + 128], lambda k: wh[:, k, :], lambda k: wl[:, k, :])
            AC.wait(m, s.get(("pv", 2 * (b - 2) + 1, 1)), m_vs)
            for j in range(2):
                k2 = 2 * i + j
                mm = AC.do(lambda e, k2=k2, j=j: e.activation(V[b % 2][:, k2, :, 0:DH],
                                                             ps[:, j * 256:(j + 1) * 256].rearrange("p (h d) -> p h d", d=DH), ACT.Copy))
            free[0] = mm
            s["V", b, i] = mm
            s["proj", b] = m

        def maxima(u, k):
            base = 64 * (u % 2)
            PE.wait(s["stack", u, k // 4])
            for bank, blocks in ((0, (3,)), (1, (2, 0)), (2, (1,))):
                PE.wait(mfree[bank])
                for i in blocks:
                    o, w = MSPAN[i]
                    m = PE.do(lambda e, i=i, o=o, w=w: e.matmul(MB[:, o:o + w], QS[base:base + 48, k, i * 128:(i + 1) * 128],
                                                               KS[base:base + 48, k, 0:w], start=True, stop=True))
                DVE.wait(m, s.get(("nmT", u - 1, k // 4)))
                for i in blocks:
                    o, w = MSPAN[i]
                    DVE.wait(s.get(("junk", i)))
                    mfree[bank] = s["junk", i] = DVE.do(lambda e, i=i, o=o, w=w: e.tensor_tensor_reduce(
                        junk[:, o:o + w], MB[:, o:o + w], MK[:, 512 - w:512], 1.0, -3e38, ALU.add, ALU.max,
                        NM[:, k // 4, 4 * (k % 4) + i:4 * (k % 4) + i + 1]))
            s["nm", u, k] = mfree[2]
            if k % 4 == 3:
                s["nmall", u, k // 4] = list(mfree)

        def put_max(u, half):
            base = 64 * (u % 2)
            PE.wait(*s["nmall", u, half], mfree[2])
            m = s["nmT", u, half] = PE.do(lambda e: e.transpose(MB[0:16, 1280:1408], NM[:, half, :], ident))
            AC.wait(m, s.get(("nmd", u - 1, half)))
            m1 = AC.do(lambda e: e.activation(NMh[half][:], MB[0:16, 1280:1408], ACT.Copy, scale=-1.0))
            DVE.wait(m1, m)
            m2 = mfree[2] = DVE.do(lambda e: e.scalar_tensor_tensor(out=NMl[half][:], in0=MB[0:16, 1280:1408], scalar=-1.0,
                                                                   in1=NMh[half][:].bitcast(F32), op0=ALU.mult, op1=ALU.subtract))
            SP.wait(m1, m2, s.get(("main", u - 2, 4 * half + 3)))
            for r, src in ((48, NMh), (49, NMl)):
                m = SP.dma(c_nm[half], lambda e, r=r, src=src: e.dma_start(
                    QS[base + r:base + r + 1, 4 * half:4 * half + 4, :].rearrange("p h (i t) -> p (h i) t", t=128).bitcast(F32),
                    src[half][:].bitcast(F32)))
            s["nmd", u, half] = m

        def main(u, k):
            base = 64 * (u % 2)
            n = (8 * u + k)
            slot = n % NP
            PE.wait(s["stack", u, k // 4], s["nmd", u, k // 4])
            for bank, blocks in ((0, (0,)), (1, (1, 3)), (2, (2,))):
                PE.wait(lfree[bank])
                for j in blocks:
                    o, w = SPAN[j]
                    m = PE.do(lambda e, j=j, o=o, w=w: e.matmul(LB[:, o:o + w], KS[base:base + 50, k, j * 128:(j + 1) * 128],
                                                               QS[base:base + 50, k, 128 * j:512], start=True, stop=True))
                if bank == 0:
                    m0 = m
            s["main", u, k] = m
            AC.wait(m0, s.get(("pvn", n - NP)))
            lfree[0] = m1 = AC.do(lambda e: e.activation(P[slot][:, 0:512], LB[:, 0:512], ACT.Exp))
            AC.wait(m)
            m2 = AC.do(lambda e: e.activation(P[slot][:, 512:1280], LB[:, 512:1280], ACT.Exp))
            lfree[1] = lfree[2] = m2
            PL.wait(m2)
            d1 = P[slot][:, 0:1024].rearrange("p (a t) -> p a t", a=2)[:, :, 0:128]
            d2 = P[slot][:, 896:1152].rearrange("p (a t) -> p a t", a=2)
            for dd in (d1, d2):
                m = PL.do(lambda e, dd=dd: e.affine_select(out=dd, in_=dd, compare_op=ALU.is_ge, fill=0.0, base=0,
                                                          pattern=[[0, 2], [1, 128]], channel_multiplier=-1))
            s["P", n] = m

        def pv(u, g):
            b, c = u // 2, u % 2
            PE.wait(s["V", b, 0], s["V", b, 1], ufree[0])
            for h in range(4):
                PE.wait(s["P", 8 * u + 4 * g + h])
            for j in range(4):
                o, w = SPAN[j]
                for h in range(4):
                    slot = (8 * u + 4 * g + h) % NP
                    hd = 8 * c + 4 * g + h
                    m = PE.do(lambda e, j=j, o=o, w=w, h=h, slot=slot, hd=hd: e.matmul(
                        UB[32 * h:32 * h + 32, 128 * j:512], V[b % 2][:, j, hd, :], P[slot][:, o:o + w],
                        start=(j == 0), stop=(j == 3), skip_group_check=True))
            for h in range(4):
                s["pvn", 8 * u + 4 * g + h] = m
            s["pv", u, g] = m
            AC.wait(m, s.get(("uw", u - 1, g)))
            m = ufree[0] = AC.do(lambda e: e.activation(Us[g][:], UB[:], ACT.Copy))
            SP.wait(m)
            s["uw", u, g] = SP.dma(c_u[g], lambda e: e.dma_start(udD[u, g], Us[g][:]))

        def denominators(u):
            SP.wait(s["uw", u, 0], s["uw", u, 1], s.get(("rdw", u - 2)))
            for g in range(2):
                src = udD[u, g].rearrange("(h r) (c t) -> h r c t", r=32, t=32)[:, DH, :, :]
                m = SP.dma(c_d8[u % 2], lambda e, g=g, src=src: e.dma_start(D8[u % 2][64 * g:64 * g + 64, :], src))
            s["d8", u] = m

        def inverses(u):
            DVE.wait(s["d8", u])
            m = DVE.do(lambda e: e.reciprocal(D8[u % 2][:], D8[u % 2][:]))
            SP.wait(m)
            s["rdw", u] = SP.dma(c_rd[u % 2], lambda e: e.dma_start(rdD[u].rearrange("h (c t) -> (h c) t", t=32), D8[u % 2][:]))

        def gather_heads(u):
            SP.wait(s["rdw", u], s.get(("norm", u - 2)))
            for g in range(2):
                src = udD[u, g].rearrange("(h r) t -> h r t", r=32)
                SP.dma(c_ur[u % 2], lambda e, g=g, src=src: e.dma_start(HT[u % 2][64 * g:64 * g + 64, :], src[:, 0:DH, :]))
            s["ur", u] = SP.dma(c_ur[u % 2], lambda e: e.dma_start(
                DN[u % 2][:], rdD[u].unsqueeze(1).broadcast_to([8, DH, 512])))

        def normalise(u):
            b, c = u // 2, u % 2
            PL.wait(s["ur", u], s.get(("hn", u - 1)))
            s["norm", u] = PL.do(lambda e: e.tensor_tensor(nf[:], HT[u % 2][:], DN[u % 2][:], ALU.mult))

        def split_heads(u):
            b, c = u // 2, u % 2
            m = s["norm", u]
            AC.wait(m, s.get(("out", b - 1, 1)))
            mh = AC.do(lambda e: e.activation(HNh[:, c, :], nf[:], ACT.Copy))
            PL.wait(mh, s.get(("out", b - 1, 1)))
            s["hn", u] = PL.do(lambda e: e.tensor_tensor(HNl[:, c, :], nf[:], HNh[:, c, :].bitcast(F32), ALU.subtract))

        def outproj(b, i, bk=0):
            ps, free = ((XB, xfree), (UB, ufree))[bk]
            wh, wl = W["wo"]
            PE.wait(s["hn", 2 * b], s["hn", 2 * b + 1], free[0])
            for j in range(2):
                t0 = (2 * i + j) * 128
                m = terms3(ps[:, j * 256:(j + 1) * 256], lambda k, t0=t0: HNh[:, k, t0:t0 + 128],
                           lambda k, t0=t0: HNl[:, k, t0:t0 + 128], lambda k: wh[:, k, :], lambda k: wl[:, k, :])
            s["out", b, i] = m
            DVE.wait(m, m_bt[b], s.get("x2p"))
            m = free[0] = DVE.do(lambda e: e.tensor_tensor(tf[:], ps[:].rearrange("p (k d) -> p k d", k=2),
                                                            BT[b % 2][:, 0:1, :].broadcast_to([128, 2, D]), ALU.mult))
            PL.wait(m)
            xs = X[:, b % 4, 2 * i:2 * i + 2, :]
            m = s["x2p"] = s["x2", b, i] = PL.do(lambda e: e.tensor_tensor(xs, xs, tf[:], ALU.add))

        def stats2(b, i):
            DVE.wait(s["x2", b, i], s.get("rs2"))
            s["s2", b] = stats(b, (2 * i, 2 * i + 1), st2, mv2)
            if i == 1:
                SP.wait(s["x2", b, 0], s["x2", b, 1])
                s["xd", b] = SP.dma(c_xd, lambda e: e.dma_start(xD[b], X[:, b % 4, :, :]))

        def moments2(b):
            s["rs2"] = moments(st2, mv2, rs2, nm2, s["s2", b], s.get("th"))

        def scale2(b, half):
            AC.wait(s["rs2"], s.get(("h2", b - 1)))
            for k in (2 * half, 2 * half + 1):
                m = AC.do(lambda e, k=k: e.activation(th[:, k, :], X[:, b % 4, k, :], ACT.Identity, bias=nm2[:, k:k + 1],
                                                      scale=rs2[:, k:k + 1]))
            s["th"] = s["th", b, half] = m

        def shift2(b, half):
            ks = slice(2 * half, 2 * half + 2)
            PL.wait(s["th", b, half], s.get(("h2T", b - 1, 1)), s.get(("tabw", b - 1)), m_bt[b])
            m = PL.do(lambda e: e.tensor_tensor(th[:, ks, :], th[:, ks, :], BT[b % 2][:, 1:2, :].broadcast_to([128, 2, D]), ALU.mult))
            PL.wait(m)
            m = PL.do(lambda e: e.tensor_tensor(H2[:, ks, :], th[:, ks, :], BT[b % 2][:, 2:3, :].broadcast_to([128, 2, D]), ALU.add))
            s["h2", b] = m
            if half == 1:
                SP.wait(m)
                s["tabw", b] = SP.dma(c_h2, lambda e: e.dma_start(tabv[b][:, :, 0:D], H2[:]))
                if b + 2 < NB:
                    load_bt(b + 2, m)

        def h2T(b, c, bk=0):
            ps, free = ((XB, xfree), (UB, ufree))[bk]
            PE.wait(s["h2", b], free[0])
            for k in range(4):
                m = PE.do(lambda e, k=k: e.transpose(ps[:, k * 128:(k + 1) * 128], H2[:, k, c * 128:(c + 1) * 128], ident))
            s["h2T", b, c] = m
            AC.wait(m, s.get(("sc", b - 1)), s.get(("hd", b - 1)))
            m1 = AC.do(lambda e: e.activation(h2[:, 0, c, :], ps[:], ACT.Copy))
            DVE.wait(m1, m)
            m = s["h2s", b, c] = free[0] = DVE.do(lambda e: e.tensor_tensor(h2[:, 1, c, :], ps[:], h2[:, 0, c, :].bitcast(F32), ALU.subtract))

        def scores(b, bk=0):
            ps, free = ((XB, xfree), (UB, ufree))[bk]
            PE.wait(s["h2s", b, 0], s["h2s", b, 1], free[0])
            o = 112 - 16 * b
            m = s["sc", b] = terms3(ps[:], lambda k: GPh[:, k, o:o + 128], lambda k: GPl[:, k, o:o + 128],
                                    lambda k: h2[:, 0, k, :], lambda k: h2[:, 1, k, :])
            DVE.wait(m, s.get("lg"))
            s["lg"] = free[0] = DVE.do(lambda e: e.tensor_tensor(LG[:], LG[:], ps[:], ALU.add))
            SP.wait(s["h2s", b, 1])
            s["hd", b] = SP.dma(c_hd, lambda e: e.dma_start(hD[b], h2[:].bitcast(F32)))

        stats1(0)
        moments1(0)
        m, m_modT = column_mod()
        ufree[0] = m
        scale1(0, 0)
        scale1(0, 1)
        for c in range(2):
            hT(0, c, c)
        split_weight("wq")
        m_qk = split_weight("wk")
        PE.wait(m_qk)
        for c in range(2):
            qk(0, c, 0, 0)
            qk(0, c, 1, 1)
            stack(c, 0)
            stack(c, 1)
        m_v = split_weight("wv")
        mfree[0] = mfree[1] = mfree[2] = m_v
        stats1(1)
        moments1(1)
        scale1(1, 0)
        scale1(1, 1)
        PE.wait(m_v)
        for k in range(8):
            maxima(0, k)
            if k == 0:
                vproj(0, 0, 0)
            if k == 1:
                vproj(0, 1, 1)
            if k in (2, 3):
                hT(1, k - 2, k - 2)
            if k == 4:
                put_max(0, 0)
        m, m_modD = row_mod()
        lfree[0] = lfree[1] = lfree[2] = m
        split_weight("wo")
        m_w = split_gate()
        load_bt(0)
        load_bt(1)
        AC.wait(m_w, m_modD)
        PE.wait(m_w)

        def chores(u, k):
            b = u // 2
            new, old, old2 = b + 1 < NB, 1 <= b <= NB, 2 <= b <= NB + 1
            if u % 2 == 0:
                if new and k < 4:
                    qk(b + 1, k // 2, k % 2, int(k == 2))
                if new and k in (4, 5):
                    vproj(b + 1, k - 4, 0)
                if old2 and k in (6, 7):
                    h2T(b - 2, k - 6, int(k == 6))
                if b + 2 < NB and k in (5, 6, 7):
                    (lambda: stats1(b + 2), lambda: moments1(b + 2), lambda: scale1(b + 2, 0))[k - 5]()
                if old2 and k == 0:
                    scale2(b - 2, 1)
                    if b + 2 < NB:
                        SP.wait(s["th", b - 2, 1])
                        load_x(b + 2, s["xd", b - 2])
                if old2 and k in (0, 2):
                    shift2(b - 2, k // 2)
            else:
                if b + 2 < NB and k == 0:
                    scale1(b + 2, 1)
                if b + 2 < NB and k in (1, 2):
                    hT(b + 2, k - 1, int(k == 2))
                if old and k in (3, 4):
                    outproj(b - 1, k - 3, 0)
                if old and k in (4, 5):
                    stats2(b - 1, k - 4)
                if old2 and k == 5:
                    scores(b - 2)
                if old and k == 6:
                    moments2(b - 1)
                if old and k == 7:
                    scale2(b - 1, 0)

        for u in range(NU):
            for k in range(8):
                if k == 1:
                    put_max(u, 1)
                if k == 5 and u + 1 < NU:
                    put_max(u + 1, 0)
                chores(u, k)
                main(u, k)
                if u + 1 < NU:
                    maxima(u + 1, k)
                if k == 4:
                    pv(u, 0)
                if k == 0 and u:
                    pv(u - 1, 1)
                if u and k in (1, 3, 4, 6, 7):
                    {1: denominators, 3: inverses, 4: gather_heads, 6: normalise, 7: split_heads}[k](u - 1)
                if k in (3, 7) and 2 <= u + 2 < NU:
                    stack(u + 2, k // 4)

        chores(NU, 0)
        pv(NU - 1, 1)
        counts = [c_in, c_in0, c_in1, c_in2, c_mod, c_mr, c_gt, c_h2, c_hd, c_xd] + c_x + c_w + c_q + c_nm + c_u + c_ur + c_bt + c_d8 + c_rd

        def so_far():
            return [q.last() for q in (PE, DVE, AC, PL)] + [(c_.sem, c_.n) for c_ in counts]

        high = so_far()
        A.close()

        def sb(name, shape, dt=F32):
            return sb_in(ctx, name, shape, dt)

        WG0 = [sb(f"WG0{p}", [128, 2, F], F32R) for p in "hl"]
        WU0 = [sb(f"WU0{p}", [128, 2, F], F32R) for p in "hl"]
        OH = sb("OH", [128, 32, 128], BF16)
        V4 = sb("V4", [128, 512, 4, 2], BF16)
        R = sb("R", [128, 512], BF16)
        iotab = sb("iotab", [128, 128], BF16)
        IDX = [sb(f"IDX{i}", [128, 4], U32) for i in range(3)]
        sm2 = sb("sm2", [128, 8])
        pad = sb("pad", [128, 512])
        B = ExitStack()
        S = sb_in(B, "S", [128, 512])
        jk = sb_in(B, "jk", [128, 512], BF16)
        GT = sb_in(B, "GT", [128, 512])
        EQ = sb_in(B, "EQ", [128, 512])
        SC = sb_in(B, "SC", [128, 512])
        PT = sb_in(B, "PT", [128, 512])
        sm = sb_in(B, "sm", [128, 16])
        si = sb_in(B, "si", [128, 4], I32)
        B.close()
        XG = [sb(f"XG{i}", [128, 4, ROW]) for i in range(2)]
        WG = [WG0, [sb(f"WG1{p}", [128, 2, F], F32R) for p in "hl"]]
        WU = [WU0, [sb(f"WU1{p}", [128, 2, F], F32R) for p in "hl"]]
        WD = [sb(f"WD{p}", [128, 8, D], F32R) for p in "hl"]
        WR = [sb(f"WR{i}", [128, 2048]) for i in range(2)]
        SIL = [sb(f"SIL{i}", [128, 512]) for i in range(2)]
        HF = [sb(f"HF{i}", [128, 512]) for i in range(2)]
        HTh, HTl = sb("HTh", [128, 8, 512], F32R), sb("HTl", [128, 8, 512], F32R)
        XT = [sb(f"XT{i}", [128, 2, 2, 512], F32R) for i in range(2)]
        EO = sb("EO", [128, 4, D])
        tb = [sb(f"tb{i}", [128, D]) for i in range(2)]
        DB = [sb(f"DB{i}", [128, D]) for i in range(2)]
        XL = sb("XL", [128, 4, D])
        GBt = sb("GBt", [128, D])

        c_wr = [count(f"c_wr{i}") for i in range(2)]
        c_xt = [count(f"c_xt{i}") for i in range(2)]
        c_xl, c_st, c_out, c_cp = count("c_xl"), count("c_st"), count("c_out"), count("c_cp")
        c_gb = count("c_gb")
        c_db = [count(f"c_db{i}") for i in range(2)]
        c_xg = [count(f"c_xg{i}") for i in range(2)]
        c_sc = count("c_sc")

        for lane in (PE, DVE, AC, PL, SP):
            lane.wait(*high)
        setfree = [[None] * 2, [None] * 2]
        dfree = [None, None]
        wrfree = [None, None]
        npiece = [0]

        def piece(dst, src, k, n):
            i = npiece[0] % 2
            npiece[0] += 1
            SP.wait(wrfree[i])
            m = SP.dma(c_wr[i], lambda e: e.dma_start(WR[i][:, 0:k * n].rearrange("p (k n) -> p k n", k=k), src))
            rv = WR[i][:, 0:k * n].rearrange("p (k n) -> p k n", k=k)
            cuts = []
            if n >= 512:
                for kk in range(k):
                    for c in range(0, n, 512):
                        cuts.append((slice(kk, kk + 1), slice(c, c + 512)))
            else:
                for kk in range(0, k, 2):
                    cuts.append((slice(kk, kk + 2), slice(0, n)))

            def cut(j):
                ks, cs = cuts[j]

                def f(free=None):
                    AC.wait(m, free)
                    mh = AC.do(lambda e: e.activation(dst[0][:, ks, cs], rv[:, ks, cs], ACT.Copy))
                    DVE.wait(m, mh, free)
                    ml = DVE.do(lambda e: e.tensor_tensor(dst[1][:, ks, cs], rv[:, ks, cs], dst[0][:, ks, cs].bitcast(F32),
                                                          ALU.subtract))
                    wrfree[i] = ml
                    return ml
                return f
            return [cut(j) for j in range(len(cuts))]

        late = []

        def flush():
            while late:
                late.pop(0)()

        def glu(m, i, wg, wu, xt, ready, bg, bu, slot, hfree, mid):
            ps = (LB, MB)[i]
            PE.wait(ready, setfree[i][0])
            cs = slice(128 * m, 128 * m + 128)
            mg = terms3(ps[:, 0:512], lambda k: wg[0][:, k, cs], lambda k: wg[1][:, k, cs],
                        lambda k: xt[:, 0, k, :], lambda k: xt[:, 1, k, :])
            mid()
            PE.wait(setfree[i][1])
            mu = terms3(ps[:, 512:1024], lambda k: wu[0][:, k, cs], lambda k: wu[1][:, k, cs],
                        lambda k: xt[:, 0, k, :], lambda k: xt[:, 1, k, :])
            AC.wait(mg, s.get(("hf", i)))
            ms = setfree[i][0] = AC.do(lambda e: e.activation(SIL[i][:], ps[:, 0:512], ACT.Silu, bias=bg))
            flush()
            DVE.wait(mu, ms, s.get(("ht", i)))
            mf = setfree[i][1] = s["hf", i] = DVE.do(lambda e: e.scalar_tensor_tensor(
                out=HF[i][:], in0=ps[:, 512:1024], scalar=bu, in1=SIL[i][:], op0=ALU.add, op1=ALU.mult))

            def split():
                AC.wait(mf, hfree)
                mh = AC.do(lambda e: e.activation(HTh[:, slot, :], HF[i][:], ACT.Copy))
                PL.wait(mf, mh, hfree)
                s["H", slot] = s["ht", i] = PL.do(lambda e: e.tensor_tensor(HTl[:, slot, :], HF[i][:],
                                                                          HTh[:, slot, :].bitcast(F32), ALU.subtract))
            late.append(split)
            return mu

        def down(q, slots, fs=None):
            n = len(slots)
            ps = (LB, MB)[q % 2][:, 1024:1280]
            PE.wait(dfree[q % 2])
            ts = slice(128 * q, 128 * q + 128)
            for f in fs or range(n):
                PE.wait(s["H", slots[f]])
                for t_, (a, b_) in enumerate(((HTh, WD[0]), (HTh, WD[1]), (HTl, WD[0]))):
                    g_ = (lambda e, f=f, a=a, b_=b_, t_=t_: e.matmul(ps, a[:, slots[f], ts], b_[:, f, :],
                                                                    start=(f == 0 and t_ == 0), stop=(f == n - 1 and t_ == 2),
                                                                    skip_group_check=True))
                    if t_ == 2:
                        m = PE.do(g_)
                    else:
                        PE.quiet(g_)
            return ps, m

        cnt, need, offe, offs, cc = (sm[:, i:i + 1] for i in range(5))
        cur, cand, kept = (si[:, i:i + 1] for i in range(3))
        z = sm[:, 8:9]
        topk = []
        c = {}

        def score_v():
            for q in (AC, DVE, PL):
                q.wait(*low)
            m = AC.do(lambda e: e.activation(S[:], LG[:], ACT.Exp, scale=-1.0))
            DVE.wait(m)
            m = DVE.do(lambda e: e.tensor_scalar(S[:], S[:], 1.0, None, ALU.add))
            DVE.wait(m)
            m = c["S"] = DVE.do(lambda e: e.reciprocal(S[:], S[:]))
            DVE.do(lambda e: e.tensor_copy(iotab[:], iotaf))
            c["cur"] = DVE.do(lambda e: e.memset(cur, 0))

        def score_p():
            PE.wait(c["S"])
            for k in range(4):
                m = PE.do(lambda e, k=k: e.transpose(UB[:, k * 128:(k + 1) * 128], S[:, k * 128:(k + 1) * 128], ident))
            c["ST"] = m

        def spread_v():
            DVE.wait(c["ST"])
            m = c["PT"] = DVE.do(lambda e: e.tensor_copy(PT[:], UB[:]))
            SP.wait(m)
            for k in range(4):
                dst = tab.rearrange("(b k p) r -> k p b r", k=4, p=128)[k, :, :, D:D + NE]
                c["stored"] = SP.dma(c_st, lambda e, k=k, dst=dst: e.dma_start(
                    dst, PT[:, k * 128:(k + 1) * 128].rearrange("p (b e) -> p b e", e=NE)))

        topk.append((score_v, score_p))
        topk.append((spread_v, lambda: None))

        def bit(n):
            def v():
                if n < 29:
                    DVE.wait(c["mm"])
                    m = DVE.do(lambda e: e.tensor_scalar(kept, XB[:, 0:1], float(CAP), float(1 << (n + 1)), ALU.is_ge, ALU.mult))
                    DVE.wait(m, c["cur"])
                    m = c["cur"] = DVE.do(lambda e: e.tensor_tensor(cur, cur, kept, ALU.bitwise_or))
                DVE.wait(c["cur"])
                if n < 0:
                    return
                m = DVE.do(lambda e: e.tensor_scalar(cand, cur, 1 << n, None, ALU.bitwise_or))
                DVE.wait(m, c.get("cnt"))
                c["cnt"] = DVE.do(lambda e: e.tensor_scalar(jk[:], S[:], cand.bitcast(F32), None, ALU.is_ge, ALU.add, accum_out=cnt))

            def p():
                if n < 0:
                    return
                PE.wait(c["cnt"])
                c["mm"] = PE.do(lambda e: e.matmul(XB[:, 0:1], Gm, cnt, start=True, stop=True))
            return v, p

        for n in range(29, -2, -1):
            topk.append(bit(n))
        thr = cur.bitcast(F32)

        def sel_v():
            DVE.do(lambda e: e.memset(SC[:], 0.0))
            DVE.wait(c["cnt"])
            c["c1"] = DVE.do(lambda e: e.tensor_scalar(GT[:], S[:], thr, None, ALU.is_gt, ALU.add, accum_out=cc))
            m = DVE.do(lambda e: e.tensor_scalar(EQ[:], S[:], thr, None, ALU.is_equal))
            DVE.wait(m, c["stored"])
            c["sE"] = DVE.do(lambda e: e.tensor_tensor_scan(PT[:], EQ[:], SC[:], 0.0, ALU.add, ALU.add))

        def sel_p():
            PE.wait(c["c1"], c["sE"])
            PE.do(lambda e: e.matmul(XB[:, 1:2], Gm, cc, start=True, stop=True))
            c["mm"] = PE.do(lambda e: e.matmul(XB[:, 2:3], Lm, PT[:, 511:512], start=True, stop=True))

        def tie_v():
            DVE.wait(c["mm"])
            DVE.do(lambda e: e.tensor_scalar(need, XB[:, 1:2], -1.0, float(CAP), ALU.mult, ALU.add))
            m = DVE.do(lambda e: e.tensor_copy(offe, XB[:, 2:3]))
            DVE.wait(m, c["sE"])
            m = DVE.do(lambda e: e.tensor_scalar(PT[:], PT[:], offe, need, ALU.add, ALU.is_le))
            DVE.wait(m)
            m = DVE.do(lambda e: e.tensor_tensor(EQ[:], EQ[:], PT[:], ALU.mult))
            DVE.wait(m)
            m = DVE.do(lambda e: e.tensor_tensor(GT[:], GT[:], EQ[:], ALU.add))
            DVE.wait(m)
            c["sS"] = DVE.do(lambda e: e.tensor_tensor_scan(PT[:], GT[:], SC[:], 0.0, ALU.add, ALU.add))

        def tie_p():
            PE.wait(c["sS"])
            c["mm"] = PE.do(lambda e: e.matmul(XB[:, 3:4], Lm, PT[:, 511:512], start=True, stop=True))

        def pos_v():
            SP.wait(c["sS"])
            SP.dma(c_cp, lambda e: e.dma_start(S[:], cpos[:, 512:1024]))
            c["tk"] = SP.dma(c_cp, lambda e: e.dma_start(SC[:], cpos[:, 1024:1536]))
            DVE.wait(c["mm"])
            m = DVE.do(lambda e: e.tensor_copy(offs, XB[:, 3:4]))
            DVE.wait(m)
            c["pos"] = DVE.do(lambda e: e.scalar_tensor_tensor(out=EQ[:], in0=PT[:], scalar=offs, in1=GT[:],
                                                               op0=ALU.add, op1=ALU.mult))

        def pos_p():
            PE.wait(c["pos"], c["PT"])
            for k in range(4):
                m = PE.do(lambda e, k=k: e.transpose(UB[:, k * 128:(k + 1) * 128], EQ[:, k * 128:(k + 1) * 128], ident))
            c["mm"] = m

        def val_v():
            mt = c["tk"]
            DVE.wait(c["mm"])
            m = c["ub"] = DVE.do(lambda e: e.tensor_scalar(PT[:], UB[:], -1.0, None, ALU.add))
            DVE.wait(m)
            m = DVE.do(lambda e: e.tensor_scalar(GT[:], PT[:], 128.0, None, ALU.is_ge))
            for v_ in (256.0, 384.0):
                DVE.wait(m)
                m = DVE.do(lambda e, v_=v_: e.scalar_tensor_tensor(out=GT[:], in0=PT[:], scalar=v_, in1=GT[:], op0=ALU.is_ge, op1=ALU.add))
            DVE.wait(m, mt)
            c["R"] = DVE.do(lambda e: e.scalar_tensor_tensor(out=R[:], in0=GT[:], scalar=-128.0, in1=PT[:], op0=ALU.mult, op1=ALU.add))
            for q in range(4):
                for v_, src in enumerate((S, SC)):
                    m = DVE.do(lambda e, q=q, v_=v_, src=src: e.scalar_tensor_tensor(
                        out=V4[:, :, q, v_], in0=GT[:], scalar=float(q), in1=src[:], op0=ALU.is_equal, op1=ALU.mult))
            c["V4"] = m

        topk += [(sel_v, sel_p), (tie_v, tie_p), (pos_v, pos_p), (val_v, lambda: None)]

        def onehot(e_, part):
            ks = slice(8 * part, 8 * part + 8)
            rv = R[:].rearrange("p (k e) -> p k e", e=NE)[:, ks, e_:e_ + 1].broadcast_to([128, 8, 128])
            DVE.wait(c["R"], s.get(("idx", e_ - 1)))
            s["oh", e_] = DVE.do(lambda e: e.tensor_tensor(OH[:, ks, :], rv, iotab[:].unsqueeze(1).broadcast_to([128, 8, 128]),
                                                           ALU.is_equal))

        def index(e_):
            PE.wait(s["oh", e_], c["V4"], c["ub"])
            PE.wait(s.get(("idxc", e_ - 1)))
            for k in range(32):
                f = (lambda e, k=k: e.matmul(UB[:, 0:8], OH[:, k, :], V4[:, k * 16 + e_, :, :].rearrange("p q v -> p (q v)"),
                                             start=(k == 0), stop=(k == 31)))
                if k < 31:
                    PE.quiet(f)
                else:
                    m = s["idx", e_] = PE.do(f)
            DVE.wait(m, s.get(("gx", e_ - 3)), s.get(("scat", e_ - 3)))
            uv = UB[:, 0:8].rearrange("p (q v) -> p q v", v=2)
            m = DVE.do(lambda e: e.tensor_copy(sm2[:], UB[:, 0:8]))
            DVE.wait(m)
            sv = sm2[:].rearrange("p (q v) -> p q v", v=2)
            m = s["idxc", e_] = DVE.do(lambda e: e.scalar_tensor_tensor(out=IDX[e_ % 3][:], in0=sv[:, :, 1], scalar=128.0,
                                                                       in1=sv[:, :, 0], op0=ALU.mult, op1=ALU.add))
            PL.wait(m, c["stored"], s.get(("eo", e_ - 2)))
            for q in range(4):
                s["gx", e_] = PL.dma(c_xg[e_ % 2], lambda e, q=q: e.indirect_dma_start(
                    out=XG[e_ % 2][:, q, :], out_offset=None, in_=tab,
                    in_offset=bass.IndirectOffsetOnAxis(ap=IDX[e_ % 3][:, q:q + 1], axis=0)))

        def turn(e_, ck):
            PE.wait(s["gx", e_], s.get("xb"))
            for q in range(4):
                m = PE.do(lambda e, q=q: e.transpose(XB[:, q * 128:(q + 1) * 128], XG[e_ % 2][:, q, ck * 128:(ck + 1) * 128], ident))
            AC.wait(m, s.get(("glu", e_ - 2)))
            m1 = AC.do(lambda e: e.activation(XT[e_ % 2][:, 0, ck, :], XB[:], ACT.Copy))
            DVE.wait(m, m1)
            s["xt", e_] = s["xb"] = DVE.do(lambda e: e.tensor_tensor(XT[e_ % 2][:, 1, ck, :], XB[:],
                                                                     XT[e_ % 2][:, 0, ck, :].bitcast(F32), ALU.subtract))

        def kn(src):
            return src.rearrange("(k p) n -> p k n", p=128)

        for dst, src, k, n in (([w[:, :, 0:SH] for w in WG[1]], sg, 2, SH), ([w[:, :, 0:SH] for w in WU[1]], su, 2, SH),
                               ([w[:, 0:4, :] for w in WD], sd, 4, D)):
            for f in piece(dst, kn(src), k, n):
                mw = f()
        s["wd"] = s["w"] = mw

        def load_h(b):
            SP.wait(s.get(("glub", b - 2)), s["hd", b])
            s["xtb", b] = SP.dma(c_xt[b % 2], lambda e: e.dma_start(XT[b % 2][:].bitcast(F32), hD[b]))

        def load_xl(b):
            SP.wait(s.get(("xlf", b - 1)), s["xd", b])
            s["gbt", b] = SP.dma(c_gb, lambda e: e.dma_start(GBt[:], modD[b, 5:6, :].broadcast_to([128, D])))
            s["xl", b] = SP.dma(c_xl, lambda e: e.dma_start(XL[:], xD[b]))

        steps = []

        def step_v():
            if steps:
                steps[0][0]()

        def step_p():
            if steps:
                steps.pop(0)[1]()

        def mid():
            step_p()
            step_v()

        def shared_glu(b, m_):
            if m_ == 1 and b + 1 < NB:
                load_h(b + 1)
            step_v()
            PE.wait(mw)
            s["glub", b] = glu(m_, m_ % 2, [w[:, :, 0:SH] for w in WG[1]], [w[:, :, 0:SH] for w in WU[1]], XT[b % 2],
                               s["xtb", b], 0.0, 0.0, 4 * (b % 2) + m_, s.get(("downb", b - 2)), mid)
            step_p()

        def shared_down(b, half):
            if b == NB - 1 and half == 0:
                flush()
            for q in (2 * half, 2 * half + 1):
                step_v()
                ps, m = down(q, [4 * (b % 2) + j for j in range(4)])
                s["downb", b] = m
                step_p()
                DVE.wait(m, s["gbt", b], s.get(("tb", q % 2)))
                m = DVE.do(lambda e, ps=ps, q=q: e.tensor_tensor(tb[q % 2][:], ps, GBt[:], ALU.mult))
                dfree[q % 2] = m
                DVE.wait(m, s["xl", b], s.get(("outb", b - 1)))
                m = s["tb", q % 2] = DVE.do(lambda e, q=q: e.tensor_tensor(EO[:, q, :], tb[q % 2][:], XL[:, q, :], ALU.add))
            if half == 1:
                s["xlf", b] = m
                SP.wait(m)
                s["outb", b] = SP.dma(c_out, lambda e, b=b: e.dma_start(outv[b], EO[:]))
                if b + 1 < NB:
                    load_xl(b + 1)

        work = []
        for b in range(NB):
            for m_ in range(4):
                work.append(lambda b=b, m_=m_: shared_glu(b, m_))
                if b and m_ < 2:
                    work.append(lambda b=b, m_=m_: shared_down(b - 1, m_))
        work += [lambda h_=h_: shared_down(NB - 1, h_) for h_ in range(2)]
        load_h(0)
        load_xl(0)

        last = NB - 1
        tail = [
            (lambda: denominators(NU - 1),),
            (lambda: shift2(last - 1, 1),),
            (lambda: inverses(NU - 1), lambda: h2T(last - 1, 0, 1)),
            (lambda: gather_heads(NU - 1), lambda: h2T(last - 1, 1, 0)),
            (lambda: scores(last - 1, 1),),
            (lambda: normalise(NU - 1), lambda: split_heads(NU - 1)),
            (),
            (lambda: outproj(last, 0, 0),),
            (lambda: outproj(last, 1, 1), lambda: stats2(last, 0)),
            (lambda: stats2(last, 1), lambda: moments2(last)),
            (lambda: scale2(last, 0), lambda: scale2(last, 1), lambda: shift2(last, 0)),
            (lambda: shift2(last, 1),),
            (),
            (lambda: h2T(last, 0, 0), lambda: h2T(last, 1, 1)),
            (lambda: scores(last, 0),),
        ]
        for n_, fs in enumerate(tail):
            for f in fs:
                f()
            if 2 <= n_ < 14:
                work.pop(0)()
        low = [s["sc", last], s["lg"], s["h2", last]] + [(c_.sem, c_.n) for c_ in counts]
        steps += topk
        cuts0 = []
        while steps:
            if len(work) > 9:
                work.pop(0)()
            else:
                step_v()
                step_p()
        cuts0 += piece(WG[0], kn(gw[0]), 2, F)
        cuts0 += piece(WU[0], kn(uw[0]), 2, F)
        PL.wait(c["V4"], c["stored"])
        for p_ in range(4):
            onehot(0, p_)
        index(0)
        while len(work) > 4:
            work.pop(0)()
            if cuts0 and len(work) < 8:
                s["w"] = cuts0.pop(0)()
        s["glu", -2] = s["glub", NB - 2]
        while work:
            if len(work) in (4, 3):
                turn(0, 4 - len(work))
            work.pop(0)()
            if cuts0:
                s["w"] = cuts0.pop(0)()
        while cuts0:
            s["w"] = cuts0.pop(0)()

        s["glu", -1] = s["glub", NB - 1]
        PL.wait(s["outb", NB - 1])
        for p_ in range(4):
            onehot(1, p_)
        cutsd = piece(WD, kn(dw[0]), 8, D)
        s["downb", -1] = s["downb", NB - 1]
        dlast = s["downb", NB - 1]

        def load_db(e_):
            SP.wait(s.get(("eo", e_ - 2)))
            s["db", e_] = SP.dma(c_db[e_ % 2], lambda e: e.dma_start(DB[e_ % 2][:], db[e_:e_ + 1, :].broadcast_to([128, D])))

        load_db(0)
        scat = [s["outb", NB - 1]]
        for e_ in range(NE):
            nxt = e_ + 1 < NE
            if nxt:
                load_db(e_ + 1)
            wfree = s.get(("glu", e_ - 1))
            ready_w = s["w"]
            for m_ in range(8):
                PE.wait(ready_w)
                s["glu", e_] = glu(m_, m_ % 2, WG[e_ % 2], WU[e_ % 2], XT[e_ % 2], s["xt", e_],
                                   gbT[:, e_, m_:m_ + 1], ubT[:, e_, m_:m_ + 1], m_, dlast, lambda: None)
                if m_ < 4:
                    s["wd"] = cutsd[m_](dlast)
                if not nxt:
                    continue
                if m_ == 0:
                    cutsg = piece(WG[(e_ + 1) % 2], kn(gw[e_ + 1]), 2, F)
                if m_ == 1:
                    index(e_ + 1)
                if m_ == 3:
                    cutsu = piece(WU[(e_ + 1) % 2], kn(uw[e_ + 1]), 2, F)
                if 3 <= m_ < 7:
                    cutsg[m_ - 3](wfree)
                if m_ == 7:
                    cutsd = piece(WD, kn(dw[e_ + 1]), 8, D)
                    cutsu[0](wfree)
                if m_ >= 4 and e_ + 2 < NE:
                    onehot(e_ + 2, m_ - 4)
                if m_ >= 6:
                    turn(e_ + 1, m_ - 6)
            flush()
            PE.wait(s["wd"])
            PL.wait(scat[0])
            slots = list(range(8))
            for q in range(4):
                if q == 0:
                    down(0, slots, range(7))
                    down(1, slots, range(4))
                ps, m = down(q, slots, ((7,), (4, 5, 6, 7))[q] if q < 2 else None)
                dlast = m
                DVE.wait(m, s["db", e_], s.get(("tb", q % 2)))
                m = DVE.do(lambda e, ps=ps, q=q, e_=e_: e.tensor_tensor(tb[q % 2][:], ps, DB[e_ % 2][:], ALU.add))
                dfree[q % 2] = m
                DVE.wait(m, scat[0])
                xg = XG[e_ % 2]
                m = s["tb", q % 2] = DVE.do(lambda e, q=q, xg=xg, e_=e_: e.scalar_tensor_tensor(
                    out=EO[:, q, :], in0=tb[q % 2][:], scalar=xg[:, q, D + e_:D + e_ + 1], in1=xg[:, q, D + NE:ROW],
                    op0=ALU.mult, op1=ALU.mult))
                PL.wait(m)
                sc_ = PL.dma(c_sc, lambda e, q=q, e_=e_: e.indirect_dma_start(
                    out=out2, out_offset=bass.IndirectOffsetOnAxis(ap=IDX[e_ % 3][:, q:q + 1], axis=0),
                    in_=EO[:, q, :], in_offset=None, compute_op=ALU.add))
                if nxt and q < 3:
                    s["w"] = cutsu[q + 1](wfree)
            scat[0] = s["scat", e_] = sc_
            s["eo", e_] = m
        PL.wait(scat[0])

        block = ctx.enter_context(nc.Block())

        @block.sync
        def _(e):
            SP.emit(e)

        @block.scalar
        def _(e):
            AC.emit(e)

        @block.gpsimd
        def _(e):
            PL.emit(e)

        @block.vector
        def _(e):
            DVE.emit(e)

        @block.tensor
        def _(e):
            PE.emit(e)


def constants():
    import numpy as np

    p = np.arange(128)
    cst = np.zeros((128, 512), np.float32)
    cst[:, 0:128] = np.eye(128)
    cst[:, 128:256] = (p[:, None] % 16) == (p[None, :] % 16)
    cst[:, 256:384] = ((p[:, None] % 16) == (p[None, :] % 16)) & (p[:, None] // 16 < p[None, :] // 16)
    cst[:, 384:512] = p[None, :]
    cpos = np.zeros((128, 512 * 3), np.float32)
    cpos[:, 384:512] = np.where(p[None, :] > p[:, None], NEG, 0.0)
    cpos[:, 512:1024] = p[:, None]
    j = np.arange(512)
    cpos[:, 1024:1536] = ((j % 128) // 16 * 4 + j // 128)[None, :]
    return cst, cpos


def kernel(**inputs):
    import numpy as _np
    import concourse.bacc as _bacc
    from concourse import mybir as _mybir
    from concourse.bass_utils import run_bass_kernel_spmd as _run

    def c(a):
        return _np.ascontiguousarray(a)

    g = {n[3:]: _np.asarray(a) for n, a in inputs.items()}
    cst, cpos = constants()
    laid = {
        "x": c(g["attn_hidden_states"]),
        "wq": c(g["attn_Wq"].T),
        "wkd": c(g["attn_Wk_down"]),
        "wvd": c(g["attn_Wv_down"]),
        "q2l": c(g["attn_q_to_latent"].transpose(2, 0, 1).reshape(64, NH * DH)),
        "vup": c(g["attn_v_up"].transpose(1, 0, 2).reshape(64, NH * DH)),
        "wo": c(g["attn_Wout"].T),
        "gate": c(g["ffn_gate_w"].T),
        "uw": c(g["ffn_up_w"].transpose(0, 2, 1)),
        "ub": c(g["ffn_up_b"].reshape(NE, 8, 128).transpose(2, 0, 1).reshape(128, NE * 8)),
        "gw": c(g["ffn_gw"].transpose(0, 2, 1)),
        "gb": c(g["ffn_gb"].reshape(NE, 8, 128).transpose(2, 0, 1).reshape(128, NE * 8)),
        "dw": c(g["ffn_down_w"].transpose(0, 2, 1)),
        "db": c(g["ffn_down_b"]),
        "sg": c(g["ffn_sh_gate_w"].T),
        "su": c(g["ffn_sh_up_w"].T),
        "sd": c(g["ffn_sh_down_w"].T),
        "ct": c(g["c"].T),
        "wmod": c(g["wmod"]),
        "cst": cst,
        "cpos": cpos,
    }
    nc = _bacc.Bacc("TRN2", target_bir_lowering=False, num_devices=1)
    arrays, args = {}, {}
    for name, a in laid.items():
        arrays["in_" + name] = a
        args[name] = nc.dram_tensor("in_" + name, a.shape, _mybir.dt.from_np(a.dtype), kind="ExternalInput").ap()
    out = nc.dram_tensor("out_y", (NB, T, D), F32, kind="ExternalOutput").ap()
    block_program(nc, out=out, **args)
    r = _run(nc, [arrays], core_ids=[0])
    return r.results[0]["out_y"]
```

```python
from contextlib import ExitStack

import concourse.bass as bass
from concourse import mybir

ALU = mybir.AluOpType
ACT = mybir.ActivationFunctionType
F32 = mybir.dt.float32
F32R = mybir.dt.float32r
BF16 = mybir.dt.bfloat16
I32 = mybir.dt.int32
U32 = mybir.dt.uint32

NB = 8
T = 512
D = 256
NH = 16
DH = 16
NU = 16
NE = 16
F = 1024
SH = 512
CAP = 512
EPS = 1e-5
NEG = -1e30
ROW = D + NE + D

SPAN = {0: (0, 512), 1: (512, 384), 3: (896, 128), 2: (1024, 256)}
MSPAN = {3: (0, 512), 2: (512, 384), 0: (896, 128), 1: (1024, 256)}


class Lane:

    def __init__(self, sem):
        self.sem, self.n, self.ops, self.seen = sem, 0, [], {}

    def wait(self, *marks):
        for m in marks:
            if m is None:
                continue
            sem, v = m
            if self.seen.get(sem.name, 0) < v:
                self.seen[sem.name] = v
                self.ops.append((None, sem, v))

    def do(self, f):
        self.n += 1
        self.ops.append((f, self.sem, 1))
        return (self.sem, self.n)

    def quiet(self, f):
        self.ops.append((f, None, 0))

    def dma(self, c, f):
        c.n += 16
        self.ops.append((f, c.sem, 16))
        return (c.sem, c.n)

    def last(self):
        return (self.sem, self.n)

    def emit(self, eng):
        for f, sem, v in self.ops:
            if f is None:
                eng.wait_ge(sem, v)
            elif sem is None:
                f(eng)
            else:
                f(eng).then_inc(sem, v)


class Count:

    def __init__(self, sem):
        self.sem, self.n = sem, 0


def block_program(nc, x, wq, wkd, wvd, q2l, vup, wo, gate, uw, ub, gw, gb, dw, db, sg, su, sd, ct, wmod,
                  cst, cpos, out):
    ctx = ExitStack()
    with ctx:
        def sem(name):
            return ctx.enter_context(nc.semaphore(name))

        def sb_in(stack, name, shape, dt=F32):
            return stack.enter_context(nc.sbuf_tensor(name, shape, dt))

        def dram(name, shape, dt=F32):
            return nc.dram_tensor(name, shape, dt).ap()

        PE, DVE, AC, PL, SP = (Lane(sem(n)) for n in ("s_pe", "s_dve", "s_act", "s_pool", "s_sp"))

        def count(name):
            return Count(sem(name))

        LB = ctx.enter_context(nc.psum_tensor("LB", [128, 1536], F32))
        MB = ctx.enter_context(nc.psum_tensor("MB", [128, 1536], F32))
        UB = ctx.enter_context(nc.psum_tensor("UB", [128, 512], F32))
        XB = ctx.enter_context(nc.psum_tensor("XB", [128, 512], F32))

        modD = dram("modD", [NB, 6, D])
        sdD = dram("sdD", [NU, 2, 128, 2, 512])
        udD = dram("udD", [NU, 2, 128, 512])
        rdD = dram("rdD", [NU, 8, 512])
        hD = dram("hD", [NB, 128, 2, 2, 512])
        xD = dram("xD", [NB, 128, 4, D])
        tab = dram("tab", [NB * T, ROW])
        tabv = tab.rearrange("(b k p) r -> b p k r", k=4, p=128)
        outv = out.rearrange("b (k p) d -> b p k d", p=128)
        out2 = out.rearrange("b t d -> (b t) d")
        xv = x.rearrange("b (k p) d -> b p k d", p=128)

        C = sb_in(ctx, "C", [128, 512])
        ident, Gm, Lm, iotaf = C[:, 0:128], C[:, 128:256], C[:, 256:384], C[:, 384:512]
        LG = sb_in(ctx, "LG", [128, 512])
        ubT = sb_in(ctx, "ubT", [128, NE, 8])
        gbT = sb_in(ctx, "gbT", [128, NE, 8])

        A = ExitStack()

        def sa(name, shape, dt=F32):
            return sb_in(A, name, shape, dt)

        W = {"wo": (sa("woh", [128, 2, 256], F32R), sa("wol", [128, 2, 256], F32R))}
        GPh, GPl = sa("GPh", [128, 2, 240], F32R), sa("GPl", [128, 2, 240], F32R)
        X = sa("X", [128, 4, 4, D])
        HT = [sa(f"HT{i}", [128, 512]) for i in range(2)]
        DN = [sa(f"DN{i}", [128, 512]) for i in range(2)]
        D8 = [sa(f"D8{i}", [128, 32]) for i in range(2)]
        nf = sa("nf", [128, 512])
        HNh = sa("HNh", [128, 2, 512], F32R)
        HNl = sa("HNl", [128, 2, 512], F32R)
        BT = [sa(f"BT{i}", [128, 3, D]) for i in range(2)]
        pro = ExitStack()
        wor = sb_in(pro, "wor", [128, 512])
        grr = sb_in(pro, "grr", [128, 96])
        modS = sb_in(pro, "modS", [NB, 6 * D])
        modA = sb_in(pro, "modA", [NB, 2, D])
        modB = sb_in(pro, "modB", [NB, 2, D])
        pro.close()
        tf = sa("tf", [128, 2, D])
        th = sa("th", [128, 4, D])
        H2 = sa("H2", [128, 4, D])
        h2 = sa("h2", [128, 2, 2, 512], F32R)
        halfc = sa("halfc", [128, 4])
        st2 = sa("st2", [128, 4, 6])
        mv2 = sa("mv2", [128, 4, 2])
        rs2 = sa("rs2", [128, 4])
        nm2 = sa("nm2", [128, 4])

        for n in ("wq", "wk", "wv"):
            W[n] = (sa(n + "h", [128, 2, 256], F32R), sa(n + "l", [128, 2, 256], F32R))
        modT = sa("modT", [128, 2, 2, NB])
        xh = sa("xh", [128, 4, D])
        st = sa("st", [128, 4, 6])
        mv = sa("mv", [128, 4, 2])
        rs = sa("rs", [128, 4])
        nm1 = sa("nm1", [128, 4])
        hf = sa("hf", [128, 2, 512])
        hh = sa("hh", [128, 2, 512], F32R)
        hl = sa("hl", [128, 2, 512], F32R)
        ST = [sa(f"ST{i}", [128, 2, 512], F32R) for i in range(4)]
        V = [sa(f"V{i}", [128, 4, NH, 32]) for i in range(2)]
        QS = sa("QS", [128, 8, 512], F32R)
        KS = sa("KS", [128, 8, 512], F32R)
        MK = sa("MK", [128, 512])
        NM = sa("NM", [128, 2, 16])
        NMh = [sa(f"NMh{i}", [16, 128], F32R) for i in range(2)]
        NMl = [sa(f"NMl{i}", [16, 128], F32R) for i in range(2)]
        junk = sa("junk", [128, 1280], BF16)
        Us = [sa(f"Us{i}", [128, 512]) for i in range(2)]
        pro = ExitStack()
        wqr = sb_in(pro, "wqr", [128, 512])
        kdr = sb_in(pro, "kdr", [64, 4, 256])
        WM = sb_in(pro, "WM", [128, 2, 3 * 512])
        pro.close()
        NP = 6
        P = [sa(f"P{i}", [128, 1280]) for i in range(NP)]

        c_in, c_mod, c_mr = count("c_in"), count("c_mod"), count("c_mr")
        c_in0, c_in1, c_in2 = count("c_in0"), count("c_in1"), count("c_in2")
        c_x = [count(f"c_x{i}") for i in range(4)]
        c_w = [count(f"c_w{i}") for i in range(4)]
        c_q = [count(f"c_q{i}") for i in range(4)]
        c_nm = [count(f"c_nm{i}") for i in range(2)]
        c_u = [count(f"c_u{i}") for i in range(2)]
        c_ur = [count(f"c_ur{i}") for i in range(2)]
        c_bt = [count(f"c_bt{i}") for i in range(2)]
        c_gt = count("c_gt")
        c_d8 = [count(f"c_d8{i}") for i in range(2)]
        c_rd = [count(f"c_rd{i}") for i in range(2)]
        c_h2, c_hd, c_xd = count("c_h2"), count("c_hd"), count("c_xd")

        raw = {"wq": wqr[:], "wo": wor[:]}
        kd, vd, q2, vu = (kdr[:, i, :] for i in range(4))
        gr = grr[:, 0:32]
        cT = grr[:, 32:48]
        sT = grr[:, 64:80]

        m_xl, m_bt = {}, {}

        def load_x(b, free=None):
            SP.wait(free)
            m_xl[b] = SP.dma(c_x[b % 4], lambda e: e.dma_start(X[:, b % 4, :, :], xv[b]))

        def load_bt(b, free=None):
            SP.wait(free, m_modD)
            for i, r in enumerate((2, 4, 3)):
                m_bt[b] = SP.dma(c_bt[b % 2], lambda e, i=i, r=r: e.dma_start(
                    BT[b % 2][:, i, :], modD[b, r:r + 1, :].broadcast_to([128, D])))
            SP.dma(c_gt, lambda e: e.dma_start(tab[b * T:(b + 1) * T, D + NE:ROW], modD[b, 5:6, :].broadcast_to([T, D])))

        wmv = wmod.rearrange("(k p) n -> p k n", p=128)
        load_x(0)
        SP.dma(c_in0, lambda e: e.dma_start(cT.rearrange("p (k b) -> p k b", k=2), ct.rearrange("(k p) b -> p k b", p=128)))
        m_wm = SP.dma(c_in0, lambda e: e.dma_start(WM[:, :, 0:512], wmv[:, :, 0:512]))
        m_cst = SP.dma(c_in1, lambda e: e.dma_start(C[:], cst))
        for dst, src in ((kd, wkd), (vd, wvd), (q2, q2l), (vu, vup)):
            m_kv = SP.dma(c_in2, lambda e, dst=dst, src=src: e.dma_start(dst, src))
        for n, src in (("wq", wq), ("wo", wo)):
            SP.dma(c_in, lambda e, n=n, src=src: e.dma_start(raw[n].rearrange("p (k n) -> p k n", k=2), src.rearrange("(k p) n -> p k n", p=128)))
        SP.dma(c_in, lambda e: e.dma_start(gr.rearrange("p (k n) -> p k n", k=2), gate.rearrange("(k p) n -> p k n", p=128)))
        SP.dma(c_in, lambda e: e.dma_start(MK[:], cpos[:, 0:512]))
        SP.dma(c_in, lambda e: e.dma_start(ubT[:].rearrange("p e m -> p (e m)"), ub))
        m_in = SP.dma(c_in, lambda e: e.dma_start(gbT[:].rearrange("p e m -> p (e m)"), gb))
        load_x(1)
        m_wm2 = SP.dma(c_mod, lambda e: e.dma_start(WM[:, :, 512:], wmv[:, :, 512:]))
        for b in range(2, 4):
            load_x(b)

        m_half = PL.do(lambda e: e.memset(halfc[:], -0.5))

        def key_ones():
            PL.wait(PL.last())
            m = PL.do(lambda e: e.memset(KS[32:64, :, :].bitcast(F32), 1.0))
            PL.wait(m)
            m = PL.do(lambda e: e.memset(KS[96:128, :, :].bitcast(F32), 1.0))
            PL.wait(m)
            return m

        def other_fills():
            PL.wait(PL.last())
            for i in range(2):
                m1 = PL.do(lambda e, i=i: e.memset(V[i][:], 1.0))
            PL.do(lambda e: e.memset(GPh[:].bitcast(F32), 0.0))
            PL.do(lambda e: e.memset(GPl[:].bitcast(F32), 0.0))
            m2 = PL.do(lambda e: e.memset(LG[:], 0.0))
            PL.wait(m2)
            return m1, m2

        s = {}

        AC.wait(m_wm)
        m = AC.do(lambda e: e.activation(sT, cT, ACT.Exp, scale=-1.0))
        DVE.wait(m)
        m = DVE.do(lambda e: e.tensor_scalar(sT, sT, 1.0, None, ALU.add))
        DVE.wait(m)
        m = DVE.do(lambda e: e.reciprocal(sT, sT))
        DVE.wait(m)
        m_sT = DVE.do(lambda e: e.tensor_tensor(sT, sT, cT, ALU.mult))
        PE.wait(m_sT, m_wm)
        for c4 in range(4):
            for k in range(2):
                m = PE.do(lambda e, c4=c4, k=k: e.matmul(UB[:, c4 * 8:c4 * 8 + 8], WM[:, k, c4 * 128:(c4 + 1) * 128],
                                                        sT[:, 8 * k:8 * k + 8], start=(k == 0), stop=(k == 1)))
        m_modp = m

        PE.wait(m_kv)
        for dst, (a, r) in ((0, (kd, q2)), (1, (vd, vu))):
            for c in range(2):
                m_fold = PE.do(lambda e, dst=dst, a=a, r=r, c=c: e.matmul(
                    MB[:, dst * 512 + c * 256:dst * 512 + c * 256 + 256], a[:, c * 128:(c + 1) * 128], r, start=True, stop=True))
        srcs = {"wk": MB[:, 0:512], "wv": MB[:, 512:1024], "wq": raw["wq"], "wo": raw["wo"]}

        def split_weight(n):
            DVE.wait(m_fold, m_in)
            h_, l_ = (W[n][i][:].rearrange("p k n -> p (k n)") for i in range(2))
            m = DVE.do(lambda e: e.tensor_copy(h_, srcs[n]))
            DVE.wait(m)
            return DVE.do(lambda e: e.tensor_tensor(l_, srcs[n], h_.bitcast(F32), ALU.subtract))

        def column_mod():
            DVE.wait(m_modp)
            m = DVE.do(lambda e: e.tensor_copy(modT[:].rearrange("p a c b -> p (a c b)"), UB[:, 0:32]))
            DVE.wait(m)
            return m, DVE.do(lambda e: e.tensor_scalar(modT[:, 1, :, :], modT[:, 1, :, :], 1.0, None, ALU.add))

        def split_gate():
            grv = gr.rearrange("p (k n) -> p k n", k=2)
            DVE.wait(m_in, m_gp)
            m = DVE.do(lambda e: e.tensor_copy(GPh[:, :, 112:128], grv))
            DVE.wait(m)
            return DVE.do(lambda e: e.tensor_tensor(GPl[:, :, 112:128], grv, GPh[:, :, 112:128].bitcast(F32), ALU.subtract))

        def row_products():
            PE.wait(m_wm2)
            for g in range(3):
                for k in range(2):
                    m = PE.do(lambda e, g=g, k=k: e.matmul(LB[0:NB, g * 512:(g + 1) * 512], sT[:, 8 * k:8 * k + 8],
                                                          WM[:, k, g * 512:(g + 1) * 512], start=(k == 0), stop=(k == 1)))
            AC.wait(m)
            return AC.do(lambda e: e.activation(modS[:], LB[0:NB, :], ACT.Copy))

        def row_mod():
            DVE.wait(m_rows)
            gates = modS[:].rearrange("p (a r d) -> p a r d", a=2, r=3)[:, :, 2, :]
            m = DVE.do(lambda e: e.scalar_tensor_tensor(out=modA[:], in0=gates, scalar=-1.0, in1=gates, op0=ALU.mult, op1=ALU.max))
            DVE.do(lambda e: e.tensor_scalar(modB[:], gates, 0.0, 2.0, ALU.is_ge, ALU.mult))
            DVE.wait(m)
            DVE.do(lambda e: e.tensor_scalar(modA[:], modA[:], 0.25, None, ALU.max))
            DVE.wait(DVE.last())
            m = DVE.do(lambda e: e.tensor_scalar(modB[:], modB[:], -1.0, None, ALU.add))
            DVE.wait(m)
            DVE.do(lambda e: e.tensor_tensor(gates, modA[:], modB[:], ALU.mult))
            m = DVE.do(lambda e: e.tensor_scalar(modS[:, 4 * D:5 * D], modS[:, 4 * D:5 * D], 1.0, None, ALU.add))
            SP.wait(m)
            return SP.dma(c_mr, lambda e: e.dma_start(modD.rearrange("b r d -> b (r d)"), modS[:]))

        xfree = [None]
        ufree = [None]
        lfree = [None] * 3
        mfree = [None] * 3

        def terms3(ps, lh, ll, rh, rl, hook=None):
            seq = [(c, a, b) for c in range(2) for a, b in ((lh, rh), (lh, rl), (ll, rh))]
            for i, (c, a, b) in enumerate(seq):
                f = (lambda e, i=i, c=c, a=a, b=b: e.matmul(ps, a(c), b(c), start=(i == 0), stop=(i == 5)))
                if i < 5:
                    PE.quiet(f)
                else:
                    m = PE.do(f)
                if hook and i in (2, 5):
                    hook()
            return m

        def stats(b, blocks, stt):
            for k in blocks:
                m = DVE.do(lambda e, k=k: e.bn_stats(stt[:, k, :], X[:, b % 4, k, :]))
            return m

        def moments(stt, mvt, rst, nmt, after, free):
            DVE.wait(after, free)
            for k in range(4):
                m = DVE.do(lambda e, k=k: e.bn_aggr(mvt[:, k, :], stt[:, k, :]))
            DVE.wait(m)
            DVE.do(lambda e: e.tensor_scalar(rst[:], mvt[:, :, 1], EPS, None, ALU.add))
            m = DVE.do(lambda e: e.tensor_scalar(nmt[:], mvt[:, :, 0], -1.0, None, ALU.mult))
            PL.wait(m, m_half)
            m = PL.do(lambda e: e.tensor_tensor(rst[:], rst[:], halfc[:], ALU.pow))
            PL.wait(m)
            return PL.do(lambda e: e.tensor_tensor(nmt[:], nmt[:], rst[:], ALU.mult))

        def stats1(b):
            DVE.wait(m_xl[b], s.get("rs1"))
            s["s1", b] = stats(b, range(4), st)

        def moments1(b):
            s["m1", b] = s["rs1"] = moments(st, mv, rs, nm1, s["s1", b], s.get(("xh", b - 1)))

        def scale1(b, half):
            AC.wait(s["m1", b], s.get(("hTp", b - 1)), m_xl[b])
            for k in (2 * half, 2 * half + 1):
                m = AC.do(lambda e, k=k: e.activation(xh[:, k, :], X[:, b % 4, k, :], ACT.Identity, bias=nm1[:, k:k + 1],
                                                      scale=rs[:, k:k + 1]))
            s["xh", b] = m

        def hT(b, c, bk=0, q_=None):
            q_ = q_ or PL
            ps, free = ((XB, xfree), (UB, ufree))[bk]
            PE.wait(s["xh", b], free[0], m_cst)
            for k in range(4):
                m = PE.do(lambda e, k=k: e.transpose(ps[:, k * 128:(k + 1) * 128], xh[:, k, c * 128:(c + 1) * 128], ident))
            s["hTp", b] = m
            AC.wait(m, s.get(("hs", b - 1, c)), m_modT)
            m = free[0] = AC.do(lambda e: e.activation(hf[:, c, :], ps[:], ACT.Identity, bias=modT[:, 0, c, b:b + 1],
                                                        scale=modT[:, 1, c, b:b + 1]))
            DVE.wait(m, s.get(("proj", b - 1)))
            m = DVE.do(lambda e: e.tensor_copy(hh[:, c, :], hf[:, c, :]))
            q_.wait(m, s.get(("proj", b - 1)))
            s["hs", b, c] = q_.do(lambda e: e.tensor_tensor(hl[:, c, :], hf[:, c, :], hh[:, c, :].bitcast(F32), ALU.subtract))

        def qk(b, c, kind, bk=0):
            ps, free = ((XB, xfree), (UB, ufree))[bk]
            u = 2 * b + c
            sl = 2 * (u % 2) + kind
            wh, wl = W["wk" if kind else "wq"]
            PE.wait(s["hs", b, 0], s["hs", b, 1], free[0])
            m = terms3(ps[:], lambda k: wh[:, k, c * 128:(c + 1) * 128], lambda k: wl[:, k, c * 128:(c + 1) * 128],
                       lambda k: hh[:, k, :], lambda k: hl[:, k, :])
            sc = 1.0 if kind else 0.125
            AC.wait(m, s.get(("stw", u - 2, kind)))
            m1 = AC.do(lambda e: e.activation(ST[sl][:, 0, :], ps[:], ACT.Copy, scale=sc))
            DVE.wait(m1, m)
            m2 = free[0] = DVE.do(lambda e: e.scalar_tensor_tensor(out=ST[sl][:, 1, :], in0=ps[:], scalar=sc,
                                                                   in1=ST[sl][:, 0, :].bitcast(F32), op0=ALU.mult, op1=ALU.subtract))
            SP.wait(m1, m2)
            s["stw", u, kind] = SP.dma(c_w[sl], lambda e: e.dma_start(sdD[u, kind], ST[sl][:].bitcast(F32)))
            s["proj", b] = m

        def stack(u, half):
            base = 64 * (u % 2)
            SP.wait(s["stw", u, 0], s["stw", u, 1], s.get(("main", u - 2, 4 * half + 3)), m_ks)
            hs = slice(4 * half, 4 * half + 4)
            for kind, dst in ((0, QS), (1, KS)):
                src = sdD[u, kind].rearrange("(h d) k t -> k d h t", d=DH)
                for r, part in enumerate((0, 1, 0) if kind == 0 else (0, 0, 1)):
                    m = SP.dma(c_q[2 * (u % 2) + half], lambda e, r=r, part=part, dst=dst, src=src: e.dma_start(
                        dst[base + 16 * r:base + 16 * r + 16, hs, :].bitcast(F32), src[part, :, hs, :]))
            s["stack", u, half] = m

        def vproj(b, i, bk=0):
            ps, free = ((XB, xfree), (UB, ufree))[bk]
            PE.wait(s["hs", b, 0], s["hs", b, 1], free[0])
            wh, wl = W["wv"]
            for j in range(2):
                t0 = (2 * i + j) * 128
                m = terms3(ps[:, j * 256:(j + 1) * 256], lambda k, t0=t0: hh[:, k, t0:t0 + 128],
                           lambda k, t0=t0: hl[:, k, t0:t0 + 128], lambda k: wh[:, k, :], lambda k: wl[:, k, :])
            AC.wait(m, s.get(("pv", 2 * (b - 2) + 1, 1)), m_vs)
            for j in range(2):
                k2 = 2 * i + j
                mm = AC.do(lambda e, k2=k2, j=j: e.activation(V[b % 2][:, k2, :, 0:DH],
                                                             ps[:, j * 256:(j + 1) * 256].rearrange("p (h d) -> p h d", d=DH), ACT.Copy))
            free[0] = mm
            s["V", b, i] = mm
            s["proj", b] = m

        def maxima(u, k):
            base = 64 * (u % 2)
            PE.wait(s["stack", u, k // 4])
            for bank, blocks in ((0, (3,)), (1, (2, 0)), (2, (1,))):
                PE.wait(mfree[bank])
                for i in blocks:
                    o, w = MSPAN[i]
                    m = PE.do(lambda e, i=i, o=o, w=w: e.matmul(MB[:, o:o + w], QS[base:base + 48, k, i * 128:(i + 1) * 128],
                                                               KS[base:base + 48, k, 0:w], start=True, stop=True))
                DVE.wait(m, s.get(("nmT", u - 1, k // 4)))
                for i in blocks:
                    o, w = MSPAN[i]
                    DVE.wait(s.get(("junk", i)))
                    mfree[bank] = s["junk", i] = DVE.do(lambda e, i=i, o=o, w=w: e.tensor_tensor_reduce(
                        junk[:, o:o + w], MB[:, o:o + w], MK[:, 512 - w:512], 1.0, -3e38, ALU.add, ALU.max,
                        NM[:, k // 4, 4 * (k % 4) + i:4 * (k % 4) + i + 1]))
            s["nm", u, k] = mfree[2]
            if k % 4 == 3:
                s["nmall", u, k // 4] = list(mfree)

        def put_max(u, half):
            base = 64 * (u % 2)
            PE.wait(*s["nmall", u, half], mfree[2])
            m = s["nmT", u, half] = PE.do(lambda e: e.transpose(MB[0:16, 1280:1408], NM[:, half, :], ident))
            AC.wait(m, s.get(("nmd", u - 1, half)))
            m1 = AC.do(lambda e: e.activation(NMh[half][:], MB[0:16, 1280:1408], ACT.Copy, scale=-1.0))
            DVE.wait(m1, m)
            m2 = mfree[2] = DVE.do(lambda e: e.scalar_tensor_tensor(out=NMl[half][:], in0=MB[0:16, 1280:1408], scalar=-1.0,
                                                                   in1=NMh[half][:].bitcast(F32), op0=ALU.mult, op1=ALU.subtract))
            SP.wait(m1, m2, s.get(("main", u - 2, 4 * half + 3)))
            for r, src in ((48, NMh), (49, NMl)):
                m = SP.dma(c_nm[half], lambda e, r=r, src=src: e.dma_start(
                    QS[base + r:base + r + 1, 4 * half:4 * half + 4, :].rearrange("p h (i t) -> p (h i) t", t=128).bitcast(F32),
                    src[half][:].bitcast(F32)))
            s["nmd", u, half] = m

        def main(u, k):
            base = 64 * (u % 2)
            n = (8 * u + k)
            slot = n % NP
            PE.wait(s["stack", u, k // 4], s["nmd", u, k // 4])
            for bank, blocks in ((0, (0,)), (1, (1, 3)), (2, (2,))):
                PE.wait(lfree[bank])
                for j in blocks:
                    o, w = SPAN[j]
                    m = PE.do(lambda e, j=j, o=o, w=w: e.matmul(LB[:, o:o + w], KS[base:base + 50, k, j * 128:(j + 1) * 128],
                                                               QS[base:base + 50, k, 128 * j:512], start=True, stop=True))
                if bank == 0:
                    m0 = m
            s["main", u, k] = m
            AC.wait(m0, s.get(("pvn", n - NP)))
            lfree[0] = m1 = AC.do(lambda e: e.activation(P[slot][:, 0:512], LB[:, 0:512], ACT.Exp))
            AC.wait(m)
            m2 = AC.do(lambda e: e.activation(P[slot][:, 512:1280], LB[:, 512:1280], ACT.Exp))
            lfree[1] = lfree[2] = m2
            PL.wait(m2)
            d1 = P[slot][:, 0:1024].rearrange("p (a t) -> p a t", a=2)[:, :, 0:128]
            d2 = P[slot][:, 896:1152].rearrange("p (a t) -> p a t", a=2)
            for dd in (d1, d2):
                m = PL.do(lambda e, dd=dd: e.affine_select(out=dd, in_=dd, compare_op=ALU.is_ge, fill=0.0, base=0,
                                                          pattern=[[0, 2], [1, 128]], channel_multiplier=-1))
            s["P", n] = m

        def pv(u, g, part):
            b, c = u // 2, u % 2
            PE.wait(s["V", b, 0], s["V", b, 1], ufree[0])
            for h in range(4):
                PE.wait(s["P", 8 * u + 4 * g + h])
            for j in (2 * part, 2 * part + 1):
                o, w = SPAN[j]
                for h in range(4):
                    slot = (8 * u + 4 * g + h) % NP
                    hd = 8 * c + 4 * g + h
                    m = PE.do(lambda e, j=j, o=o, w=w, h=h, slot=slot, hd=hd: e.matmul(
                        UB[32 * h:32 * h + 32, 128 * j:512], V[b % 2][:, j, hd, :], P[slot][:, o:o + w],
                        start=(j == 0), stop=(j == 3), skip_group_check=True))
            if part == 0:
                return
            for h in range(4):
                s["pvn", 8 * u + 4 * g + h] = m
            s["pv", u, g] = m
            AC.wait(m, s.get(("uw", u - 1, g)))
            m = ufree[0] = AC.do(lambda e: e.activation(Us[g][:], UB[:], ACT.Copy))
            SP.wait(m)
            s["uw", u, g] = SP.dma(c_u[g], lambda e: e.dma_start(udD[u, g], Us[g][:]))

        def denominators(u):
            SP.wait(s["uw", u, 0], s["uw", u, 1], s.get(("rdw", u - 2)))
            for g in range(2):
                src = udD[u, g].rearrange("(h r) (c t) -> h r c t", r=32, t=32)[:, DH, :, :]
                m = SP.dma(c_d8[u % 2], lambda e, g=g, src=src: e.dma_start(D8[u % 2][64 * g:64 * g + 64, :], src))
            s["d8", u] = m

        def inverses(u):
            DVE.wait(s["d8", u])
            m = DVE.do(lambda e: e.reciprocal(D8[u % 2][:], D8[u % 2][:]))
            SP.wait(m)
            s["rdw", u] = SP.dma(c_rd[u % 2], lambda e: e.dma_start(rdD[u].rearrange("h (c t) -> (h c) t", t=32), D8[u % 2][:]))

        def gather_heads(u):
            SP.wait(s["rdw", u], s.get(("norm", u - 2)))
            for g in range(2):
                src = udD[u, g].rearrange("(h r) t -> h r t", r=32)
                SP.dma(c_ur[u % 2], lambda e, g=g, src=src: e.dma_start(HT[u % 2][64 * g:64 * g + 64, :], src[:, 0:DH, :]))
            s["ur", u] = SP.dma(c_ur[u % 2], lambda e: e.dma_start(
                DN[u % 2][:], rdD[u].unsqueeze(1).broadcast_to([8, DH, 512])))

        def normalise(u):
            b, c = u // 2, u % 2
            PL.wait(s["ur", u], s.get(("hn", u - 1)))
            s["norm", u] = PL.do(lambda e: e.tensor_tensor(nf[:], HT[u % 2][:], DN[u % 2][:], ALU.mult))

        def split_heads(u):
            b, c = u // 2, u % 2
            m = s["norm", u]
            AC.wait(m, s.get(("out", b - 1, 1)))
            mh = AC.do(lambda e: e.activation(HNh[:, c, :], nf[:], ACT.Copy))
            PL.wait(mh, s.get(("out", b - 1, 1)))
            s["hn", u] = PL.do(lambda e: e.tensor_tensor(HNl[:, c, :], nf[:], HNh[:, c, :].bitcast(F32), ALU.subtract))

        def outproj(b, i, bk=0):
            ps, free = ((XB, xfree), (UB, ufree))[bk]
            wh, wl = W["wo"]
            PE.wait(s["hn", 2 * b], s["hn", 2 * b + 1], free[0])
            for j in range(2):
                t0 = (2 * i + j) * 128
                m = terms3(ps[:, j * 256:(j + 1) * 256], lambda k, t0=t0: HNh[:, k, t0:t0 + 128],
                           lambda k, t0=t0: HNl[:, k, t0:t0 + 128], lambda k: wh[:, k, :], lambda k: wl[:, k, :])
            s["out", b, i] = m
            DVE.wait(m, m_bt[b], s.get("x2p"))
            m = free[0] = DVE.do(lambda e: e.tensor_tensor(tf[:], ps[:].rearrange("p (k d) -> p k d", k=2),
                                                            BT[b % 2][:, 0:1, :].broadcast_to([128, 2, D]), ALU.mult))
            PL.wait(m)
            xs = X[:, b % 4, 2 * i:2 * i + 2, :]
            m = s["x2p"] = s["x2", b, i] = PL.do(lambda e: e.tensor_tensor(xs, xs, tf[:], ALU.add))

        def stats2(b, i):
            DVE.wait(s["x2", b, i], s.get("rs2"))
            s["s2", b] = stats(b, (2 * i, 2 * i + 1), st2)
            if i == 1:
                SP.wait(s["x2", b, 0], s["x2", b, 1])
                s["xd", b] = SP.dma(c_xd, lambda e: e.dma_start(xD[b], X[:, b % 4, :, :]))

        def moments2(b):
            s["rs2"] = moments(st2, mv2, rs2, nm2, s["s2", b], s.get("th"))

        def scale2(b, half):
            AC.wait(s["rs2"], s.get(("h2", b - 1)))
            for k in (2 * half, 2 * half + 1):
                m = AC.do(lambda e, k=k: e.activation(th[:, k, :], X[:, b % 4, k, :], ACT.Identity, bias=nm2[:, k:k + 1],
                                                      scale=rs2[:, k:k + 1]))
            s["th"] = s["th", b, half] = m

        def shift2(b, half, q_=None):
            q_ = q_ or PL
            ks = slice(2 * half, 2 * half + 2)
            q_.wait(s["th", b, half], s.get(("h2T", b - 1, 1)), s.get(("tabw", b - 1)), m_bt[b])
            m = q_.do(lambda e: e.tensor_tensor(th[:, ks, :], th[:, ks, :], BT[b % 2][:, 1:2, :].broadcast_to([128, 2, D]), ALU.mult))
            q_.wait(m)
            m = q_.do(lambda e: e.tensor_tensor(H2[:, ks, :], th[:, ks, :], BT[b % 2][:, 2:3, :].broadcast_to([128, 2, D]), ALU.add))
            if half == 1:
                s["h2a", b] = s["h2", b]
            s["h2", b] = m
            if half == 1:
                SP.wait(m, s["h2a", b])
                s["tabw", b] = SP.dma(c_h2, lambda e: e.dma_start(tabv[b][:, :, 0:D], H2[:]))
                if b + 2 < NB:
                    load_bt(b + 2, m)

        def h2T(b, c, bk=0):
            ps, free = ((XB, xfree), (UB, ufree))[bk]
            PE.wait(s["h2a", b], s["h2", b], free[0])
            for k in range(4):
                m = PE.do(lambda e, k=k: e.transpose(ps[:, k * 128:(k + 1) * 128], H2[:, k, c * 128:(c + 1) * 128], ident))
            s["h2T", b, c] = m
            AC.wait(m, s.get(("sc", b - 1)), s.get(("hd", b - 1)))
            m1 = AC.do(lambda e: e.activation(h2[:, 0, c, :], ps[:], ACT.Copy))
            DVE.wait(m1, m)
            m = s["h2s", b, c] = free[0] = DVE.do(lambda e: e.tensor_tensor(h2[:, 1, c, :], ps[:], h2[:, 0, c, :].bitcast(F32), ALU.subtract))

        def scores(b, bk=0):
            ps, free = ((XB, xfree), (UB, ufree))[bk]
            PE.wait(s["h2s", b, 0], s["h2s", b, 1], free[0])
            o = 112 - 16 * b
            m = s["sc", b] = terms3(ps[:], lambda k: GPh[:, k, o:o + 128], lambda k: GPl[:, k, o:o + 128],
                                    lambda k: h2[:, 0, k, :], lambda k: h2[:, 1, k, :])
            DVE.wait(m, s.get("lg"))
            s["lg"] = free[0] = DVE.do(lambda e: e.tensor_tensor(LG[:], LG[:], ps[:], ALU.add))
            SP.wait(s["h2s", b, 1])
            s["hd", b] = SP.dma(c_hd, lambda e: e.dma_start(hD[b], h2[:].bitcast(F32)))

        counts = [c_in, c_in0, c_in1, c_in2, c_mod, c_mr, c_gt, c_h2, c_hd, c_xd] + c_x + c_w + c_q + c_nm + c_u + c_ur + c_bt + c_d8 + c_rd

        def so_far():
            return [q.last() for q in (PE, DVE, AC, PL)] + [(c_.sem, c_.n) for c_ in counts]

        A.close()

        def sb(name, shape, dt=F32):
            return sb_in(ctx, name, shape, dt)

        iotab = sb("iotab", [128, 128], BF16)
        B = ExitStack()
        S = sb_in(B, "S", [128, 512])
        jk = sb_in(B, "jk", [128, 512], BF16)
        GT = sb_in(B, "GT", [128, 512])
        EQ = sb_in(B, "EQ", [128, 512])
        SC = sb_in(B, "SC", [128, 512])
        PT = sb_in(B, "PT", [128, 512])
        sm = sb_in(B, "sm", [128, 16])
        si = sb_in(B, "si", [128, 4], I32)
        B.close()
        XG = [sb(f"XG{i}", [128, 4, ROW]) for i in range(2)]
        WG0 = [sb(f"WG0{p}", [128, 2, F], F32R) for p in "hl"]
        WU0 = [sb(f"WU0{p}", [128, 2, F], F32R) for p in "hl"]
        OH = sb("OH", [128, 32, 128], BF16)
        V4 = sb("V4", [128, 512, 4, 2], BF16)
        R = sb("R", [128, 512], BF16)
        IDX = [sb(f"IDX{i}", [128, 4], U32) for i in range(3)]
        sm2 = sb("sm2", [128, 8])
        pad = sb("pad", [128, 512])
        WG = [WG0, [sb(f"WG1{p}", [128, 2, F], F32R) for p in "hl"]]
        WU = [WU0, [sb(f"WU1{p}", [128, 2, F], F32R) for p in "hl"]]
        WR = [sb("WR0", [128, 2048])]
        XT = [sb("XT0", [128, 2, 2, 512], F32R)]
        WR.append(sb("WR1", [128, 2048]))
        XT.append(sb("XT1", [128, 2, 2, 512], F32R))
        WD = [sb(f"WD{p}", [128, 8, D], F32R) for p in "hl"]
        SIL = [sb(f"SIL{i}", [128, 512]) for i in range(2)]
        HF = [sb(f"HF{i}", [128, 512]) for i in range(2)]
        HTh, HTl = sb("HTh", [128, 8, 512], F32R), sb("HTl", [128, 8, 512], F32R)
        EO = sb("EO", [128, 4, D])
        tb = [sb(f"tb{i}", [128, D]) for i in range(2)]
        DB = [sb(f"DB{i}", [128, D]) for i in range(2)]
        XL = sb("XL", [128, 4, D])
        GBt = sb("GBt", [128, D])

        c_wr = [count(f"c_wr{i}") for i in range(2)]
        c_xt = [count(f"c_xt{i}") for i in range(2)]
        c_xl, c_st, c_out, c_cp = count("c_xl"), count("c_st"), count("c_out"), count("c_cp")
        c_gb = count("c_gb")
        c_db = [count(f"c_db{i}") for i in range(2)]
        c_xg = [count(f"c_xg{i}") for i in range(2)]
        c_sc = count("c_sc")

        setfree = [[None] * 2, [None] * 2]
        dfree = [None, None]
        wrfree = [None, None]
        npiece = [1]

        def piece(dst, src, k, n):
            i = npiece[0] % 2
            npiece[0] += 1
            SP.wait(wrfree[i])
            m = SP.dma(c_wr[i], lambda e: e.dma_start(WR[i][:, 0:k * n].rearrange("p (k n) -> p k n", k=k), src))
            rv = WR[i][:, 0:k * n].rearrange("p (k n) -> p k n", k=k)
            cuts = []
            if n >= 512:
                for kk in range(k):
                    for c in range(0, n, 512):
                        cuts.append((slice(kk, kk + 1), slice(c, c + 512)))
            else:
                for kk in range(0, k, 2):
                    cuts.append((slice(kk, kk + 2), slice(0, n)))

            def cut(j):
                ks, cs = cuts[j]

                def f(free=None):
                    AC.wait(m, free)
                    mh = AC.do(lambda e: e.activation(dst[0][:, ks, cs], rv[:, ks, cs], ACT.Copy))
                    DVE.wait(m, mh, free)
                    ml = DVE.do(lambda e: e.tensor_tensor(dst[1][:, ks, cs], rv[:, ks, cs], dst[0][:, ks, cs].bitcast(F32),
                                                          ALU.subtract))
                    wrfree[i] = ml
                    return ml
                return f
            return [cut(j) for j in range(len(cuts))]

        def shared_pieces():
            cuts = []
            for i, (dst, src) in enumerate(((WG[1], sg), (WU[1], su))):
                rv = WR[0][:, 1024 * i:1024 * i + 1024].rearrange("p (k n) -> p k n", k=2)
                m = SP.dma(c_wr[0], lambda e, rv=rv, src=src: e.dma_start(rv, kn(src)))
                for k in range(2):
                    def f(dst=dst, rv=rv, k=k):
                        AC.wait(mark[0])
                        mh = AC.do(lambda e: e.activation(dst[0][:, k, 0:SH], rv[:, k, :], ACT.Copy))
                        DVE.wait(mark[0], mh)
                        wrfree[0] = DVE.do(lambda e: e.tensor_tensor(dst[1][:, k, 0:SH], rv[:, k, :],
                                                                     dst[0][:, k, 0:SH].bitcast(F32), ALU.subtract))
                        return wrfree[0]
                    cuts.append(f)
            mark = [m]
            return cuts

        late = []

        def flush():
            while late:
                late.pop(0)()

        def glu(m, i, wg, wu, xt, ready, bg, bu, slot, hfree, hook=None):
            ps = (LB, MB)[i]
            PE.wait(ready, setfree[i][0])
            cs = slice(128 * m, 128 * m + 128)
            mg = terms3(ps[:, 0:512], lambda k: wg[0][:, k, cs], lambda k: wg[1][:, k, cs],
                        lambda k: xt[:, 0, k, :], lambda k: xt[:, 1, k, :], hook)
            PE.wait(setfree[i][1])
            mu = terms3(ps[:, 512:1024], lambda k: wu[0][:, k, cs], lambda k: wu[1][:, k, cs],
                        lambda k: xt[:, 0, k, :], lambda k: xt[:, 1, k, :], hook)
            AC.wait(mg, s.get(("hf", i)))
            ms = setfree[i][0] = AC.do(lambda e: e.activation(SIL[i][:], ps[:, 0:512], ACT.Silu, bias=bg))
            flush()
            DVE.wait(mu, ms, s.get(("ht", i)))
            mf = setfree[i][1] = s["hf", i] = DVE.do(lambda e: e.scalar_tensor_tensor(
                out=HF[i][:], in0=ps[:, 512:1024], scalar=bu, in1=SIL[i][:], op0=ALU.add, op1=ALU.mult))

            def split():
                AC.wait(mf, hfree)
                mh = AC.do(lambda e: e.activation(HTh[:, slot, :], HF[i][:], ACT.Copy))
                PL.wait(mf, mh, hfree)
                s["H", slot] = s["ht", i] = PL.do(lambda e: e.tensor_tensor(HTl[:, slot, :], HF[i][:],
                                                                          HTh[:, slot, :].bitcast(F32), ALU.subtract))
            late.append(split)
            return mu

        def down(q, slots, fs=None):
            n = len(slots)
            ps = (LB, MB)[q % 2][:, 1024:1280]
            PE.wait(dfree[q % 2])
            ts = slice(128 * q, 128 * q + 128)
            for f in fs or range(n):
                PE.wait(s["H", slots[f]])
                for t_, (a, b_) in enumerate(((HTh, WD[0]), (HTh, WD[1]), (HTl, WD[0]))):
                    g_ = (lambda e, f=f, a=a, b_=b_, t_=t_: e.matmul(ps, a[:, slots[f], ts], b_[:, f, :],
                                                                    start=(f == 0 and t_ == 0), stop=(f == n - 1 and t_ == 2),
                                                                    skip_group_check=True))
                    if t_ == 2:
                        m = PE.do(g_)
                    else:
                        PE.quiet(g_)
            return ps, m

        cnt, need, offe, offs, cc = (sm[:, i:i + 1] for i in range(5))
        cur, drop = (si[:, i:i + 1] for i in range(2))
        topk = []
        c = {}

        def score_v():
            AC.wait(*lowest)
            DVE.wait(*lowest)
            m = AC.do(lambda e: e.activation(S[:], LG[:], ACT.Exp, scale=-1.0))
            DVE.wait(m)
            m = DVE.do(lambda e: e.tensor_scalar(S[:], S[:], 1.0, None, ALU.add))
            DVE.wait(m)
            m = c["S"] = DVE.do(lambda e: e.reciprocal(S[:], S[:]))
            DVE.do(lambda e: e.tensor_copy(iotab[:], iotaf))
            c["cur"] = DVE.do(lambda e: e.memset(cur, 1 << 29))

        def score_p():
            PE.wait(c["S"])
            for k in range(4):
                m = PE.do(lambda e, k=k: e.transpose(UB[:, k * 128:(k + 1) * 128], S[:, k * 128:(k + 1) * 128], ident))
            c["ST"] = m

        def spread_v():
            DVE.wait(c["ST"])
            m = c["PT"] = DVE.do(lambda e: e.tensor_copy(PT[:], UB[:]))
            SP.wait(m)
            for k in range(4):
                dst = tab.rearrange("(b k p) r -> k p b r", k=4, p=128)[k, :, :, D:D + NE]
                c["stored"] = SP.dma(c_st, lambda e, k=k, dst=dst: e.dma_start(
                    dst, PT[:, k * 128:(k + 1) * 128].rearrange("p (b e) -> p b e", e=NE)))

        topk.append((score_v, score_p))
        topk.append((spread_v, lambda: None))

        def bit(n):
            def v():
                m = c["cur"]
                if n < 29:
                    DVE.wait(c["mm"])
                    m = DVE.do(lambda e: e.tensor_scalar(drop, XB[:, 0:1], float(CAP), float(1 << (n + 1)), ALU.is_lt, ALU.mult))
                    DVE.wait(m, c["cur"])
                    if n >= 0:
                        m = DVE.do(lambda e: e.scalar_tensor_tensor(out=cur, in0=drop, scalar=1 << n, in1=cur,
                                                                    op0=ALU.bitwise_or, op1=ALU.bitwise_xor))
                    else:
                        m = DVE.do(lambda e: e.tensor_tensor(cur, cur, drop, ALU.bitwise_xor))
                    c["cur"] = m
                DVE.wait(m, c.get("cnt"))
                if n >= 0:
                    c["cnt"] = DVE.do(lambda e: e.tensor_scalar(jk[:], S[:], cur.bitcast(F32), None, ALU.is_ge, ALU.add, accum_out=cnt))

            def p():
                if n < 0:
                    return
                PE.wait(c["cnt"])
                c["mm"] = PE.do(lambda e: e.matmul(XB[:, 0:1], Gm, cnt, start=True, stop=True))
            return v, p

        for n in range(29, -2, -1):
            topk.append(bit(n))
        thr = cur.bitcast(F32)

        def sel_v():
            DVE.do(lambda e: e.memset(SC[:], 0.0))
            DVE.wait(c["cnt"])
            c["c1"] = DVE.do(lambda e: e.tensor_scalar(GT[:], S[:], thr, None, ALU.is_gt, ALU.add, accum_out=cc))
            m = DVE.do(lambda e: e.tensor_scalar(EQ[:], S[:], thr, None, ALU.is_equal))
            DVE.wait(m, c["stored"])
            c["sE"] = DVE.do(lambda e: e.tensor_tensor_scan(PT[:], EQ[:], SC[:], 0.0, ALU.add, ALU.add))

        def sel_p():
            PE.wait(c["c1"], c["sE"])
            PE.do(lambda e: e.matmul(XB[:, 1:2], Gm, cc, start=True, stop=True))
            c["mm"] = PE.do(lambda e: e.matmul(XB[:, 2:3], Lm, PT[:, 511:512], start=True, stop=True))

        def tie_v():
            DVE.wait(c["mm"])
            DVE.do(lambda e: e.tensor_scalar(need, XB[:, 1:2], -1.0, float(CAP), ALU.mult, ALU.add))
            m = DVE.do(lambda e: e.tensor_copy(offe, XB[:, 2:3]))
            DVE.wait(m, c["sE"])
            m = DVE.do(lambda e: e.tensor_scalar(PT[:], PT[:], offe, need, ALU.add, ALU.is_le))
            DVE.wait(m)
            m = DVE.do(lambda e: e.tensor_tensor(EQ[:], EQ[:], PT[:], ALU.mult))
            DVE.wait(m)
            m = DVE.do(lambda e: e.tensor_tensor(GT[:], GT[:], EQ[:], ALU.add))
            DVE.wait(m)
            c["sS"] = DVE.do(lambda e: e.tensor_tensor_scan(PT[:], GT[:], SC[:], 0.0, ALU.add, ALU.add))

        def tie_p():
            PE.wait(c["sS"])
            c["mm"] = PE.do(lambda e: e.matmul(XB[:, 3:4], Lm, PT[:, 511:512], start=True, stop=True))

        def pos_v():
            SP.wait(c["sS"])
            SP.dma(c_cp, lambda e: e.dma_start(S[:], cpos[:, 512:1024]))
            c["tk"] = SP.dma(c_cp, lambda e: e.dma_start(SC[:], cpos[:, 1024:1536]))
            DVE.wait(c["mm"])
            m = DVE.do(lambda e: e.tensor_copy(offs, XB[:, 3:4]))
            DVE.wait(m)
            c["pos"] = DVE.do(lambda e: e.scalar_tensor_tensor(out=EQ[:], in0=PT[:], scalar=offs, in1=GT[:],
                                                               op0=ALU.add, op1=ALU.mult))

        def pos_p():
            PE.wait(c["pos"], c["PT"])
            for k in range(4):
                m = PE.do(lambda e, k=k: e.transpose(UB[:, k * 128:(k + 1) * 128], EQ[:, k * 128:(k + 1) * 128], ident))
            c["mm"] = m

        def val_v():
            DVE.wait(c["mm"])
            m = c["ub"] = DVE.do(lambda e: e.tensor_scalar(PT[:], UB[:], -1.0, None, ALU.add))
            DVE.wait(m)
            m = DVE.do(lambda e: e.tensor_scalar(GT[:], PT[:], 128.0, None, ALU.is_ge))
            for v_ in (256.0, 384.0):
                DVE.wait(m)
                m = DVE.do(lambda e, v_=v_: e.scalar_tensor_tensor(out=GT[:], in0=PT[:], scalar=v_, in1=GT[:], op0=ALU.is_ge, op1=ALU.add))
            DVE.wait(m, c["tk"], *low)
            c["R"] = DVE.do(lambda e: e.scalar_tensor_tensor(out=R[:], in0=GT[:], scalar=-128.0, in1=PT[:], op0=ALU.mult, op1=ALU.add))

        def val2_v():
            DVE.wait(*low)
            for q in range(4):
                for v_, src in enumerate((S, SC)):
                    m = DVE.do(lambda e, q=q, v_=v_, src=src: e.scalar_tensor_tensor(
                        out=V4[:, :, q, v_], in0=GT[:], scalar=float(q), in1=src[:], op0=ALU.is_equal, op1=ALU.mult))
            c["V4"] = m

        topk += [(sel_v, sel_p), (tie_v, tie_p), (pos_v, pos_p), (val_v, lambda: None), (val2_v, lambda: None)]

        def onehot(e_, part):
            ks = slice(8 * part, 8 * part + 8)
            rv = R[:].rearrange("p (k e) -> p k e", e=NE)[:, ks, e_:e_ + 1].broadcast_to([128, 8, 128])
            DVE.wait(c["R"], s.get(("idx", e_ - 1)))
            s["oh", e_] = DVE.do(lambda e: e.tensor_tensor(OH[:, ks, :], rv, iotab[:].unsqueeze(1).broadcast_to([128, 8, 128]),
                                                           ALU.is_equal))

        def index(e_):
            PE.wait(s["oh", e_], c["V4"], c["ub"])
            PE.wait(s.get(("idxc", e_ - 1)))
            for k in range(32):
                f = (lambda e, k=k: e.matmul(UB[:, 0:8], OH[:, k, :], V4[:, k * 16 + e_, :, :].rearrange("p q v -> p (q v)"),
                                             start=(k == 0), stop=(k == 31)))
                if k < 31:
                    PE.quiet(f)
                else:
                    m = s["idx", e_] = PE.do(f)
            DVE.wait(m, s.get(("gx", e_ - 3)), s.get(("scat", e_ - 3)))
            m = DVE.do(lambda e: e.tensor_copy(sm2[:], UB[:, 0:8]))
            DVE.wait(m)
            sv = sm2[:].rearrange("p (q v) -> p q v", v=2)
            m = s["idxc", e_] = DVE.do(lambda e: e.scalar_tensor_tensor(out=IDX[e_ % 3][:], in0=sv[:, :, 1], scalar=128.0,
                                                                       in1=sv[:, :, 0], op0=ALU.mult, op1=ALU.add))
            PL.wait(m, c["stored"], s.get(("eo", e_ - 2)))
            for q in range(4):
                s["gx", e_] = PL.dma(c_xg[e_ % 2], lambda e, q=q: e.indirect_dma_start(
                    out=XG[e_ % 2][:, q, :], out_offset=None, in_=tab,
                    in_offset=bass.IndirectOffsetOnAxis(ap=IDX[e_ % 3][:, q:q + 1], axis=0)))

        def turn(e_, ck):
            PE.wait(s["gx", e_], s.get("xb"))
            for q in range(4):
                m = PE.do(lambda e, q=q: e.transpose(XB[:, q * 128:(q + 1) * 128], XG[e_ % 2][:, q, ck * 128:(ck + 1) * 128], ident))
            AC.wait(m, s.get(("glu", e_ - 2)))
            m1 = AC.do(lambda e: e.activation(XT[e_ % 2][:, 0, ck, :], XB[:], ACT.Copy))
            DVE.wait(m, m1)
            s["xt", e_] = s["xb"] = DVE.do(lambda e: e.tensor_tensor(XT[e_ % 2][:, 1, ck, :], XB[:],
                                                                     XT[e_ % 2][:, 0, ck, :].bitcast(F32), ALU.subtract))

        def kn(src):
            return src.rearrange("(k p) n -> p k n", p=128)

        def load_h(b):
            SP.wait(s.get(("glub", b - 2)), s["hd", b])
            s["xtb", b] = SP.dma(c_xt[b % 2], lambda e: e.dma_start(XT[b % 2][:].bitcast(F32), hD[b]))

        def load_xl(b):
            SP.wait(s.get(("xlf", b - 1)), s["xd", b])
            s["gbt", b] = SP.dma(c_gb, lambda e: e.dma_start(GBt[:], modD[b, 5:6, :].broadcast_to([128, D])))
            s["xl", b] = SP.dma(c_xl, lambda e: e.dma_start(XL[:], xD[b]))

        steps = []

        def step_v():
            if steps:
                steps[0][0]()

        def step_p():
            if steps:
                steps.pop(0)[1]()

        ticks = [0]

        def hook():
            ticks[0] += 1
            if steps and ticks[0] > 0 and ticks[0] % 3 == 0:
                step_p()
                step_v()

        def shared_glu(b, m_):
            if m_ == 1 and b + 1 < NB:
                load_h(b + 1)
            PE.wait(mw)
            s["glub", b] = glu(m_, m_ % 2, [w[:, :, 0:SH] for w in WG[1]], [w[:, :, 0:SH] for w in WU[1]], XT[b % 2],
                               s["xtb", b], 0.0, 0.0, 4 * (b % 2) + m_, s.get(("downb", b - 2)), hook)

        def shared_down(b, half):
            if b == NB - 1 and half == 0:
                flush()
            PE.wait(s["wd"])
            for q in (2 * half, 2 * half + 1):
                slots = [4 * (b % 2) + j for j in range(4)]
                down(q, slots, (0, 1))
                hook()
                ps, m = down(q, slots, (2, 3))
                s["downb", b] = m
                hook()
                DVE.wait(m, s["gbt", b], s.get(("tb", q % 2)))
                m = DVE.do(lambda e, ps=ps, q=q: e.tensor_tensor(tb[q % 2][:], ps, GBt[:], ALU.mult))
                dfree[q % 2] = m
                DVE.wait(m, s["xl", b], s.get(("outb", b - 1)))
                m = s["tb", q % 2] = DVE.do(lambda e, q=q: e.tensor_tensor(EO[:, q, :], tb[q % 2][:], XL[:, q, :], ALU.add))
            if half == 1:
                s["xlf", b] = m
                SP.wait(m)
                s["outb", b] = SP.dma(c_out, lambda e, b=b: e.dma_start(outv[b], EO[:]))
                if b + 1 < NB:
                    load_xl(b + 1)

        work = []
        for b in range(NB):
            for m_ in range(4):
                work.append(lambda b=b, m_=m_: shared_glu(b, m_))
                if b and m_ < 2:
                    work.append(lambda b=b, m_=m_: shared_down(b - 1, m_))
        work += [lambda h_=h_: shared_down(NB - 1, h_) for h_ in range(2)]
        stats1(0)
        moments1(0)
        m_ks = key_ones()
        m, m_modT = column_mod()
        ufree[0] = m
        scale1(0, 0)
        scale1(0, 1)
        split_weight("wq")
        m_qk = split_weight("wk")
        for c_ in range(2):
            hT(0, c_, c_, DVE)
        m_vs, m_gp = other_fills()
        PE.wait(m_qk)
        for c_ in range(2):
            qk(0, c_, 0, 0)
            qk(0, c_, 1, 1)
            stack(c_, 0)
            stack(c_, 1)
        m_rows = row_products()
        m_v = split_weight("wv")
        mfree[0] = mfree[1] = mfree[2] = m_v
        lfree[0] = lfree[1] = lfree[2] = m_rows
        stats1(1)
        moments1(1)
        scale1(1, 0)
        scale1(1, 1)
        PE.wait(m_v)
        for k in range(8):
            maxima(0, k)
            if k == 0:
                vproj(0, 0, 0)
            if k == 1:
                vproj(0, 1, 1)
            if k in (2, 3):
                hT(1, k - 2, k - 2)
            if k == 4:
                put_max(0, 0)

        plan = {
            "q0": 3, "k0": 3, "v0": 1, "q1": 6, "k1": 7, "h2a": 5, "h2b": 7, "stats1": 5,
            "moments1": 5, "scale1a": 7, "scale2b": 0, "shift2a": 0, "shift2b": 3, "v1": 1,
            "scale1b": 0, "hTa": 4, "hTb": 3, "outa": 2, "outb": 3, "stats2a": 5, "stats2b": 4,
            "moments2": 5, "scores": 7, "scale2a": 7, "den": 1, "inv": 4, "gat": 5, "norm": 7,
            "split": 7, "pm1": 1, "pm0": 5, "stk0e": 3, "stk0o": 3,
        }
        bank = [0]

        def spare(k):
            bank[0] = 1 - bank[0] if k % 4 >= 2 else 0
            return bank[0]

        def chores(u, k):
            b, odd = u // 2, u % 2
            new, new2, old, old2 = b + 1 < NB, b + 2 < NB, 1 <= b <= NB, 2 <= b <= NB + 1
            even_work = [
                ("v0", new, lambda: vproj(b + 1, 0, spare(k))),
                ("q0", new, lambda: qk(b + 1, 0, 0, spare(k))),
                ("k0", new, lambda: qk(b + 1, 0, 1, spare(k))),
                ("q1", new, lambda: qk(b + 1, 1, 0, spare(k))),
                ("k1", new, lambda: qk(b + 1, 1, 1, spare(k))),
                ("h2a", old2, lambda: h2T(b - 2, 0, spare(k))),
                ("h2b", old2, lambda: h2T(b - 2, 1, spare(k))),
                ("stats1", new2, lambda: stats1(b + 2)),
                ("moments1", new2, lambda: moments1(b + 2)),
                ("scale2b", old2, lambda: scale2(b - 2, 1)),
                ("scale2b", old2 and new2, lambda: (SP.wait(s["th", b - 2, 1]), load_x(b + 2, s["xd", b - 2]))),
                ("shift2a", old2, lambda: shift2(b - 2, 0)),
                ("shift2b", old2, lambda: shift2(b - 2, 1)),
            ]
            odd_work = [
                ("v1", new, lambda: vproj(b + 1, 1, spare(k))),
                ("hTa", new2, lambda: hT(b + 2, 0, spare(k))),
                ("hTb", new2, lambda: hT(b + 2, 1, spare(k))),
                ("outa", old, lambda: outproj(b - 1, 0, spare(k))),
                ("outb", old, lambda: outproj(b - 1, 1, spare(k))),
                ("stats2a", old, lambda: stats2(b - 1, 0)),
                ("stats2b", old, lambda: stats2(b - 1, 1)),
                ("scores", old2, lambda: scores(b - 2, spare(k))),
                ("moments2", old, lambda: moments2(b - 1)),
                ("scale2a", old, lambda: scale2(b - 1, 0)),
            ]
            for name, due, f in odd_work if odd else even_work:
                if due and plan[name] == k:
                    f()

        for u in range(NU):
            for k in range(8):
                if k == plan["pm1"]:
                    put_max(u, 1)
                if k == plan["pm0"] and u + 1 < NU:
                    put_max(u + 1, 0)
                chores(u, k)
                main(u, k)
                if u // 2 + 2 < NB and (u % 2, k) in ((0, plan["scale1a"]), (1, plan["scale1b"])):
                    scale1(u // 2 + 2, u % 2)
                if (u, k) == (0, 2):
                    m_modD = row_mod()
                if (u, k) == (0, 4):
                    m = split_weight("wo")
                    PE.wait(split_gate())
                if (u, k) == (1, 2):
                    load_bt(0)
                    load_bt(1)
                if u + 1 < NU:
                    maxima(u + 1, k)
                if k in (4, 5):
                    pv(u, 0, k - 4)
                if k in (0, 1) and u:
                    pv(u - 1, 1, k)
                for name, f in (("den", denominators), ("inv", inverses), ("gat", gather_heads), ("norm", normalise),
                                ("split", split_heads)):
                    if u and plan[name] == k:
                        f(u - 1)
                if k in (plan["stk0o" if u % 2 else "stk0e"], 7) and u + 2 < NU:
                    stack(u + 2, k // 7)

                if (u, k) == (NU - 2, 0):
                    early = so_far()
                if (u, k) == (NU - 2, 5):
                    SP.wait(*early)
                    cuts_sh = shared_pieces()
                if (u, k) == (NU - 2, 7):
                    load_h(0)
                if u == NU - 1:
                    if k == 0:
                        DVE.wait(*early)
                        AC.wait(*early)
                    if 2 <= k < 6:
                        mw = cuts_sh[k - 2]()
        chores(NU, 0)
        pv(NU - 1, 1, 0)
        pv(NU - 1, 1, 1)
        high = so_far()
        denominators(NU - 1)
        PE.wait(*high[:4])
        for lane in (DVE, AC, PL, SP):
            lane.wait(*high)

        inverses(NU - 1)
        cuts_sd = piece([w[:, 0:4, :] for w in WD], kn(sd), 4, D)
        gather_heads(NU - 1)
        load_xl(0)

        last = NB - 1
        tail = [
            (3, lambda: shift2(last - 1, 1)),
            (0, lambda: h2T(last - 1, 0, 1), lambda: h2T(last - 1, 1, 0), lambda: scores(last - 1, 1)),
            (1, lambda: s.update(wd=[f() for f in cuts_sd][-1]), lambda: normalise(NU - 1), lambda: split_heads(NU - 1)),
            (1, lambda: outproj(last, 0, 0), lambda: outproj(last, 1, 1), lambda: stats2(last, 0)),
            (1, lambda: stats2(last, 1), lambda: moments2(last)),
            (3, lambda: scale2(last, 0), lambda: scale2(last, 1), lambda: shift2(last, 0, DVE), lambda: shift2(last, 1)),
            (1, lambda: h2T(last, 0, 0), lambda: h2T(last, 1, 1)),
            (0, lambda: scores(last, 0)),
        ]
        for n_, *fs in tail:
            for f in fs:
                f()
            for _ in range(n_):
                work.pop(0)()
        lowest = [s["sc", last], s["lg"], s["xd", last], s["ur", NU - 1]]
        low = lowest + [s["h2", last]] + [(c_.sem, c_.n) for c_ in counts]
        steps += topk + [(lambda h_=h_: (onehot(0, 2 * h_), onehot(0, 2 * h_ + 1)), lambda: None) for h_ in range(2)]
        cuts0 = []
        ticks[0] = -5
        step_v()
        while steps:
            if len(work) > 6:
                work.pop(0)()
            else:
                step_p()
                step_v()
        AC.wait(*low)
        cuts0 += piece(WG[0], kn(gw[0]), 2, F)
        cuts0 += piece(WU[0], kn(uw[0]), 2, F)
        PL.wait(c["V4"], c["stored"], *low)
        index(0)
        while len(work) > 4:
            work.pop(0)()
            if cuts0 and len(work) < 8:
                s["w"] = cuts0.pop(0)()
        s["glu", -2] = s["glub", NB - 2]
        while work:
            if len(work) in (4, 3):
                turn(0, 4 - len(work))
            work.pop(0)()
            if cuts0:
                s["w"] = cuts0.pop(0)()
        while cuts0:
            s["w"] = cuts0.pop(0)()

        s["glu", -1] = s["glub", NB - 1]
        PL.wait(s["outb", NB - 1])
        for p_ in range(4):
            onehot(1, p_)
        cutsd = piece(WD, kn(dw[0]), 8, D)
        s["downb", -1] = s["downb", NB - 1]
        dlast = s["downb", NB - 1]

        def load_db(e_):
            SP.wait(s.get(("eo", e_ - 2)))
            s["db", e_] = SP.dma(c_db[e_ % 2], lambda e: e.dma_start(DB[e_ % 2][:], db[e_:e_ + 1, :].broadcast_to([128, D])))

        load_db(0)
        scat = [s["outb", NB - 1]]
        for e_ in range(NE):
            nxt = e_ + 1 < NE
            if nxt:
                load_db(e_ + 1)
            wfree = s.get(("glu", e_ - 1))
            ready_w = s["w"]
            for m_ in range(8):
                PE.wait(ready_w)
                s["glu", e_] = glu(m_, m_ % 2, WG[e_ % 2], WU[e_ % 2], XT[e_ % 2], s["xt", e_],
                                   gbT[:, e_, m_:m_ + 1], ubT[:, e_, m_:m_ + 1], m_, dlast)
                if m_ < 4:
                    s["wd"] = cutsd[m_](dlast)
                if not nxt:
                    continue
                if m_ == 0:
                    cutsg = piece(WG[(e_ + 1) % 2], kn(gw[e_ + 1]), 2, F)
                if m_ == 1:
                    index(e_ + 1)
                if m_ == 3:
                    cutsu = piece(WU[(e_ + 1) % 2], kn(uw[e_ + 1]), 2, F)
                if 3 <= m_ < 7:
                    cutsg[m_ - 3](wfree)
                if m_ == 7:
                    cutsd = piece(WD, kn(dw[e_ + 1]), 8, D)
                    cutsu[0](wfree)
                if m_ >= 4 and e_ + 2 < NE:
                    onehot(e_ + 2, m_ - 4)
                if m_ >= 6:
                    turn(e_ + 1, m_ - 6)
            flush()
            PE.wait(s["wd"])
            PL.wait(scat[0])
            slots = list(range(8))
            for q in range(4):
                if q == 0:
                    down(0, slots, range(7))
                    down(1, slots, range(4))
                ps, m = down(q, slots, ((7,), (4, 5, 6, 7))[q] if q < 2 else None)
                dlast = m
                DVE.wait(m, s["db", e_], s.get(("tb", q % 2)))
                m = DVE.do(lambda e, ps=ps, q=q, e_=e_: e.tensor_tensor(tb[q % 2][:], ps, DB[e_ % 2][:], ALU.add))
                dfree[q % 2] = m
                DVE.wait(m, scat[0])
                xg = XG[e_ % 2]
                m = s["tb", q % 2] = DVE.do(lambda e, q=q, xg=xg, e_=e_: e.scalar_tensor_tensor(
                    out=EO[:, q, :], in0=tb[q % 2][:], scalar=xg[:, q, D + e_:D + e_ + 1], in1=xg[:, q, D + NE:ROW],
                    op0=ALU.mult, op1=ALU.mult))
                PL.wait(m)
                sc_ = PL.dma(c_sc, lambda e, q=q, e_=e_: e.indirect_dma_start(
                    out=out2, out_offset=bass.IndirectOffsetOnAxis(ap=IDX[e_ % 3][:, q:q + 1], axis=0),
                    in_=EO[:, q, :], in_offset=None, compute_op=ALU.add))
                if nxt and q < 3:
                    s["w"] = cutsu[q + 1](wfree)
            scat[0] = s["scat", e_] = sc_
            s["eo", e_] = m
        PL.wait(scat[0])

        block = ctx.enter_context(nc.Block())

        @block.sync
        def _(e):
            SP.emit(e)

        @block.scalar
        def _(e):
            AC.emit(e)

        @block.gpsimd
        def _(e):
            PL.emit(e)

        @block.vector
        def _(e):
            DVE.emit(e)

        @block.tensor
        def _(e):
            PE.emit(e)


def constants():
    import numpy as np

    p = np.arange(128)
    cst = np.zeros((128, 512), np.float32)
    cst[:, 0:128] = np.eye(128)
    cst[:, 128:256] = (p[:, None] % 16) == (p[None, :] % 16)
    cst[:, 256:384] = ((p[:, None] % 16) == (p[None, :] % 16)) & (p[:, None] // 16 < p[None, :] // 16)
    cst[:, 384:512] = p[None, :]
    cpos = np.zeros((128, 512 * 3), np.float32)
    cpos[:, 384:512] = np.where(p[None, :] > p[:, None], NEG, 0.0)
    cpos[:, 512:1024] = p[:, None]
    j = np.arange(512)
    cpos[:, 1024:1536] = ((j % 128) // 16 * 4 + j // 128)[None, :]
    return cst, cpos


def kernel(**inputs):
    import numpy as _np
    import concourse.bacc as _bacc
    from concourse import mybir as _mybir
    from concourse.bass_utils import run_bass_kernel_spmd as _run

    def c(a):
        return _np.ascontiguousarray(a)

    g = {n[3:]: _np.asarray(a) for n, a in inputs.items()}
    cst, cpos = constants()
    laid = {
        "x": c(g["attn_hidden_states"]),
        "wq": c(g["attn_Wq"].T),
        "wkd": c(g["attn_Wk_down"]),
        "wvd": c(g["attn_Wv_down"]),
        "q2l": c(g["attn_q_to_latent"].transpose(2, 0, 1).reshape(64, NH * DH)),
        "vup": c(g["attn_v_up"].transpose(1, 0, 2).reshape(64, NH * DH)),
        "wo": c(g["attn_Wout"].T),
        "gate": c(g["ffn_gate_w"].T),
        "uw": c(g["ffn_up_w"].transpose(0, 2, 1)),
        "ub": c(g["ffn_up_b"].reshape(NE, 8, 128).transpose(2, 0, 1).reshape(128, NE * 8)),
        "gw": c(g["ffn_gw"].transpose(0, 2, 1)),
        "gb": c(g["ffn_gb"].reshape(NE, 8, 128).transpose(2, 0, 1).reshape(128, NE * 8)),
        "dw": c(g["ffn_down_w"].transpose(0, 2, 1)),
        "db": c(g["ffn_down_b"]),
        "sg": c(g["ffn_sh_gate_w"].T),
        "su": c(g["ffn_sh_up_w"].T),
        "sd": c(g["ffn_sh_down_w"].T),
        "ct": c(g["c"].T),
        "wmod": c(g["wmod"]),
        "cst": cst,
        "cpos": cpos,
    }
    nc = _bacc.Bacc("TRN2", target_bir_lowering=False, num_devices=1)
    arrays, args = {}, {}
    for name, a in laid.items():
        arrays["in_" + name] = a
        args[name] = nc.dram_tensor("in_" + name, a.shape, _mybir.dt.from_np(a.dtype), kind="ExternalInput").ap()
    out = nc.dram_tensor("out_y", (NB, T, D), F32, kind="ExternalOutput").ap()
    block_program(nc, out=out, **args)
    r = _run(nc, [arrays], core_ids=[0])
    return r.results[0]["out_y"]
```
